# Optimizing a Trainium2 kernel written in Bass

```python
import numpy as np
import jax
import jax.numpy as jnp

def _softmax(x, axis=-1):
    return jax.nn.softmax(x, axis=axis)

def _gelu(x):
    return jax.nn.gelu(x, approximate=True)

def _silu(x):
    return jax.nn.silu(x)

def _sigmoid(x):
    return jax.nn.sigmoid(x)

def _layernorm(x, axis=-1, eps=1e-05):
    m = jnp.mean(x, axis=axis, keepdims=True)
    v = jnp.var(x, axis=axis, keepdims=True)
    return (x - m) / jnp.sqrt(v + eps)

def _scatter_add(tgt, idx, src, axis=0):
    return tgt.at[idx].add(src)

def _segment_sum(src, seg, n):
    return jax.ops.segment_sum(src, seg, n)
kernel_name = 'mk_cond_seq_d4_seqx_r4_95fc21'

def setup_inputs(seed: int=0):
    np.random.seed(seed)
    _w = jnp.asarray

    def _rec_inputs():
        import jax
        import jax.numpy as jnp
        _rk = jax.random.key(seed)
        x = -0.0005207 + 1.001 * jax.random.normal(jax.random.fold_in(_rk, 1), (8, 512, 256), jnp.float32)
        _lenS = 512 - jax.random.randint(jax.random.fold_in(_rk, 7), (8,), 0, max(1, 512 // 4) + 1, jnp.int32)
        _lenS2 = 512 - jax.random.randint(jax.random.fold_in(_rk, 8), (8,), 0, max(1, 512 // 4) + 1, jnp.int32)
        itok_B_34_63 = jax.random.randint(jax.random.fold_in(_rk, 12), (8,), 34, 64, jnp.int32)
        fside_Bx16xSxS_0 = -1.47943e-05 + 1.00017 * jax.random.normal(jax.random.fold_in(_rk, 13), (8, 16, 512, 512), jnp.float32)
        itok_B_0_15 = jax.random.randint(jax.random.fold_in(_rk, 14), (8,), 0, 16, jnp.int32)
        condB_theta = jax.random.uniform(jax.random.fold_in(_rk, 15), (8,), jnp.float32, 0.0, 0.983423)
        condB_phi = jax.random.uniform(jax.random.fold_in(_rk, 16), (8,), jnp.float32, 0.0, 0.961312)
        _validS = jnp.arange(512)[None, :] < _lenS[:, None]
        _validS2 = jnp.arange(512)[None, :] < _lenS2[:, None]
        _causal = jnp.tril(jnp.ones((512, 512), dtype=bool))
        mask_Bx1xSxS_bk0 = jnp.logical_not(jnp.broadcast_to(_validS[:, None, None, :], (8, 1, 512, 512)))
        return (x, itok_B_34_63, fside_Bx16xSxS_0, itok_B_0_15, condB_theta, condB_phi, mask_Bx1xSxS_bk0)
    x, itok_B_34_63, fside_Bx16xSxS_0, itok_B_0_15, condB_theta, condB_phi, mask_Bx1xSxS_bk0 = _rec_inputs()

    def _L0_cond_setup():
        import jax, jax.numpy as jnp
        import numpy as np
        import math
        D_MODEL = 256
        N_HEAD = 16
        HEAD_DIM = D_MODEL // N_HEAD
        D_FF = 1024
        NUM_STEPS = 100.0
        RESCALE = 4000.0
        EPS = 1e-05

        def _sin_emb(t):
            half = D_MODEL // 2
            x = t.astype(jnp.float32) / NUM_STEPS * RESCALE
            freqs = jnp.exp(jnp.arange(half, dtype=jnp.float32) * (-math.log(10000.0) / (half - 1)))
            e = x[:, None] * freqs[None, :]
            return jnp.concatenate([jnp.sin(e), jnp.cos(e)], axis=-1)

        def _ln(x):
            m = jnp.mean(x, axis=-1, keepdims=True)
            v = jnp.var(x, axis=-1, keepdims=True)
            return (x - m) / jnp.sqrt(v + EPS)

        def _gelu2(x):
            return x * jax.nn.sigmoid(1.702 * x)
        key = jax.random.key(seed)
        ks = jax.random.split(key, 24)
        B, S, D, F = (4, 128, D_MODEL, D_FF)
        std = 0.02
        inp = {'src': jax.random.normal(ks[0], (B, S, D), dtype=jnp.float32), 'src_mask': jax.random.randint(ks[1], (B, 1, S, S), 0, 2).astype(bool), 'timestep': jax.random.randint(ks[2], (B,), 0, 100, dtype=jnp.int32), 'attention_bias': jax.random.normal(ks[3], (B, N_HEAD, S, S), dtype=jnp.float32), 'W_ada': jax.random.normal(ks[4], (D, 2 * D), dtype=jnp.float32) * std, 'b_ada': jnp.zeros((2 * D,), dtype=jnp.float32), 'Wq': jax.random.normal(ks[5], (D, D), dtype=jnp.float32) * std, 'bq': jnp.zeros((D,), dtype=jnp.float32), 'Wk': jax.random.normal(ks[6], (D, D), dtype=jnp.float32) * std, 'bk': jnp.zeros((D,), dtype=jnp.float32), 'Wv': jax.random.normal(ks[7], (D, D), dtype=jnp.float32) * std, 'bv': jnp.zeros((D,), dtype=jnp.float32), 'Wo': jax.random.normal(ks[8], (D, D), dtype=jnp.float32) * std, 'bo': jnp.zeros((D,), dtype=jnp.float32), 'W1': jax.random.normal(ks[9], (D, F), dtype=jnp.float32) * std, 'b1': jnp.zeros((F,), dtype=jnp.float32), 'W2': jax.random.normal(ks[10], (F, D), dtype=jnp.float32) * std, 'b2': jnp.zeros((D,), dtype=jnp.float32), 'g2': jnp.ones((D,), dtype=jnp.float32), 'beta2': jnp.zeros((D,), dtype=jnp.float32)}
        return inp
    _L0_cond_all = _L0_cond_setup()
    _L0_cond_in = {k: v for k, v in _L0_cond_all.items() if k in ('W_ada', 'b_ada', 'Wq', 'bq', 'Wk', 'bk', 'Wv', 'bv', 'Wo', 'bo', 'W1', 'b1', 'W2', 'b2', 'g2', 'beta2')}
    del _L0_cond_all

    def _L1_cond_setup():
        import jax, jax.numpy as jnp
        import numpy as np
        B, S, D = (32, 256, 256)
        A = 64
        E = 16
        LN_EPS = 1e-05
        key = jax.random.key(seed)
        ks = jax.random.split(key, 10)
        s = lambda fan_in: 1.0 / np.sqrt(fan_in)
        return {'hidden_states': jax.random.normal(ks[0], (B, S, D), dtype=jnp.float32), 'domain_id': jax.random.randint(ks[1], (B,), 0, E, dtype=jnp.int64), 'down_W': jax.random.uniform(ks[2], (A, D), jnp.float32, -s(D), s(D)), 'down_b': jax.random.uniform(ks[3], (A,), jnp.float32, -s(D), s(D)), 'up_W': jax.random.uniform(ks[4], (D, A), jnp.float32, -s(A), s(A)), 'up_b': jax.random.uniform(ks[5], (D,), jnp.float32, -s(A), s(A)), 'expert_W': jax.random.uniform(ks[6], (E, A, A), jnp.float32, -s(A), s(A)), 'expert_b': jax.random.uniform(ks[7], (E, A), jnp.float32, -s(A), s(A)), 'domain_emb': jax.random.normal(ks[8], (E, A), dtype=jnp.float32), 'ln_gamma': jnp.ones((D,), jnp.float32), 'ln_beta': jnp.zeros((D,), jnp.float32)}
    _L1_cond_all = _L1_cond_setup()
    _L1_cond_in = {k: v for k, v in _L1_cond_all.items() if k in ('down_W', 'down_b', 'up_W', 'up_b', 'expert_W', 'expert_b', 'domain_emb', 'ln_gamma', 'ln_beta')}
    del _L1_cond_all

    def _L2_cond_setup():
        import jax, jax.numpy as jnp
        import numpy as np
        key = jax.random.key(seed)
        k1, k2, k3 = jax.random.split(key, 3)
        B, N, D = (16, 1024, 256)
        embeddings = jax.random.normal(k1, (B, N, D), dtype=jnp.float32)
        theta = jax.random.uniform(k2, (B,), dtype=jnp.float32)
        phi = jax.random.uniform(k3, (B,), dtype=jnp.float32)
        return {'embeddings': embeddings, 'theta': theta, 'phi': phi}
    _L2_cond_all = _L2_cond_setup()
    _L2_cond_in = {k: v for k, v in _L2_cond_all.items() if k in ()}
    del _L2_cond_all

    def _L3_cond_setup():
        import jax, jax.numpy as jnp
        import numpy as np
        B, S, D = (32, 256, 256)
        A = 64
        E = 16
        LN_EPS = 1e-05
        key = jax.random.key(seed)
        ks = jax.random.split(key, 10)
        s = lambda fan_in: 1.0 / np.sqrt(fan_in)
        return {'hidden_states': jax.random.normal(ks[0], (B, S, D), dtype=jnp.float32), 'domain_id': jax.random.randint(ks[1], (B,), 0, E, dtype=jnp.int64), 'down_W': jax.random.uniform(ks[2], (A, D), jnp.float32, -s(D), s(D)), 'down_b': jax.random.uniform(ks[3], (A,), jnp.float32, -s(D), s(D)), 'up_W': jax.random.uniform(ks[4], (D, A), jnp.float32, -s(A), s(A)), 'up_b': jax.random.uniform(ks[5], (D,), jnp.float32, -s(A), s(A)), 'expert_W': jax.random.uniform(ks[6], (E, A, A), jnp.float32, -s(A), s(A)), 'expert_b': jax.random.uniform(ks[7], (E, A), jnp.float32, -s(A), s(A)), 'domain_emb': jax.random.normal(ks[8], (E, A), dtype=jnp.float32), 'ln_gamma': jnp.ones((D,), jnp.float32), 'ln_beta': jnp.zeros((D,), jnp.float32)}
    _L3_cond_all = _L3_cond_setup()
    _L3_cond_in = {k: v for k, v in _L3_cond_all.items() if k in ('down_W', 'down_b', 'up_W', 'up_b', 'expert_W', 'expert_b', 'domain_emb', 'ln_gamma', 'ln_beta')}
    del _L3_cond_all
    return {'x': x, 'itok_B_34_63': itok_B_34_63, 'fside_Bx16xSxS_0': fside_Bx16xSxS_0, 'itok_B_0_15': itok_B_0_15, 'condB_theta': condB_theta, 'condB_phi': condB_phi, 'mask_Bx1xSxS_bk0': mask_Bx1xSxS_bk0, 'L0_cond_W_ada': _L0_cond_in['W_ada'], 'L0_cond_b_ada': _L0_cond_in['b_ada'], 'L0_cond_Wq': _L0_cond_in['Wq'], 'L0_cond_bq': _L0_cond_in['bq'], 'L0_cond_Wk': _L0_cond_in['Wk'], 'L0_cond_bk': _L0_cond_in['bk'], 'L0_cond_Wv': _L0_cond_in['Wv'], 'L0_cond_bv': _L0_cond_in['bv'], 'L0_cond_Wo': _L0_cond_in['Wo'], 'L0_cond_bo': _L0_cond_in['bo'], 'L0_cond_W1': _L0_cond_in['W1'], 'L0_cond_b1': _L0_cond_in['b1'], 'L0_cond_W2': _L0_cond_in['W2'], 'L0_cond_b2': _L0_cond_in['b2'], 'L0_cond_g2': _L0_cond_in['g2'], 'L0_cond_beta2': _L0_cond_in['beta2'], 'L1_cond_down_W': _L1_cond_in['down_W'], 'L1_cond_down_b': _L1_cond_in['down_b'], 'L1_cond_up_W': _L1_cond_in['up_W'], 'L1_cond_up_b': _L1_cond_in['up_b'], 'L1_cond_expert_W': _L1_cond_in['expert_W'], 'L1_cond_expert_b': _L1_cond_in['expert_b'], 'L1_cond_domain_emb': _L1_cond_in['domain_emb'], 'L1_cond_ln_gamma': _L1_cond_in['ln_gamma'], 'L1_cond_ln_beta': _L1_cond_in['ln_beta'], 'L3_cond_down_W': _L3_cond_in['down_W'], 'L3_cond_down_b': _L3_cond_in['down_b'], 'L3_cond_up_W': _L3_cond_in['up_W'], 'L3_cond_up_b': _L3_cond_in['up_b'], 'L3_cond_expert_W': _L3_cond_in['expert_W'], 'L3_cond_expert_b': _L3_cond_in['expert_b'], 'L3_cond_domain_emb': _L3_cond_in['domain_emb'], 'L3_cond_ln_gamma': _L3_cond_in['ln_gamma'], 'L3_cond_ln_beta': _L3_cond_in['ln_beta']}

def reference(x, itok_B_34_63, fside_Bx16xSxS_0, itok_B_0_15, condB_theta, condB_phi, mask_Bx1xSxS_bk0, L0_cond_W_ada, L0_cond_b_ada, L0_cond_Wq, L0_cond_bq, L0_cond_Wk, L0_cond_bk, L0_cond_Wv, L0_cond_bv, L0_cond_Wo, L0_cond_bo, L0_cond_W1, L0_cond_b1, L0_cond_W2, L0_cond_b2, L0_cond_g2, L0_cond_beta2, L1_cond_down_W, L1_cond_down_b, L1_cond_up_W, L1_cond_up_b, L1_cond_expert_W, L1_cond_expert_b, L1_cond_domain_emb, L1_cond_ln_gamma, L1_cond_ln_beta, L3_cond_down_W, L3_cond_down_b, L3_cond_up_W, L3_cond_up_b, L3_cond_expert_W, L3_cond_expert_b, L3_cond_domain_emb, L3_cond_ln_gamma, L3_cond_ln_beta):
    import jax
    import jax.numpy as jnp

    def _L0_cond_ref(src, src_mask, timestep, attention_bias, W_ada, b_ada, Wq, bq, Wk, bk, Wv, bv, Wo, bo, W1, b1, W2, b2, g2, beta2):
        import jax, jax.numpy as jnp
        import numpy as np
        import math
        D_MODEL = 256
        N_HEAD = 16
        HEAD_DIM = D_MODEL // N_HEAD
        D_FF = 1024
        NUM_STEPS = 100.0
        RESCALE = 4000.0
        EPS = 1e-05

        def _sin_emb(t):
            half = D_MODEL // 2
            x = t.astype(jnp.float32) / NUM_STEPS * RESCALE
            freqs = jnp.exp(jnp.arange(half, dtype=jnp.float32) * (-math.log(10000.0) / (half - 1)))
            e = x[:, None] * freqs[None, :]
            return jnp.concatenate([jnp.sin(e), jnp.cos(e)], axis=-1)

        def _ln(x):
            m = jnp.mean(x, axis=-1, keepdims=True)
            v = jnp.var(x, axis=-1, keepdims=True)
            return (x - m) / jnp.sqrt(v + EPS)

        def _gelu2(x):
            return x * jax.nn.sigmoid(1.702 * x)
        B, S, D = src.shape
        emb = jax.nn.silu(_sin_emb(timestep)) @ W_ada + b_ada
        scale, shift = jnp.split(emb[:, None, :], 2, axis=-1)
        x = _ln(src) * (1.0 + scale) + shift
        q = (x @ Wq + bq).reshape(B, S, N_HEAD, HEAD_DIM).transpose(0, 2, 1, 3)
        k = (x @ Wk + bk).reshape(B, S, N_HEAD, HEAD_DIM).transpose(0, 2, 1, 3)
        v = (x @ Wv + bv).reshape(B, S, N_HEAD, HEAD_DIM).transpose(0, 2, 1, 3)
        scores = jnp.einsum('bhqd,bhkd->bhqk', q / math.sqrt(HEAD_DIM), k)
        scores = scores + attention_bias
        scores = jnp.where(src_mask, -jnp.inf, scores.astype(jnp.float32))
        probs = jax.nn.softmax(scores, axis=-1).astype(v.dtype)
        ctx = jnp.einsum('bhqk,bhkd->bhqd', probs, v)
        ctx = ctx.transpose(0, 2, 1, 3).reshape(B, S, D)
        x = x + (ctx @ Wo + bo)
        h = _ln(x) * g2 + beta2
        ff = _gelu2(h @ W1 + b1) @ W2 + b2
        return x + ff

    def _L1_cond_ref(hidden_states, domain_id, down_W, down_b, up_W, up_b, expert_W, expert_b, domain_emb, ln_gamma, ln_beta):
        import jax, jax.numpy as jnp
        import numpy as np
        B, S, D = (32, 256, 256)
        A = 64
        E = 16
        LN_EPS = 1e-05
        residual = hidden_states
        hidden = jnp.einsum('bsd,ad->bsa', hidden_states, down_W) + down_b
        hidden = jax.nn.gelu(hidden, approximate=False)
        valid = (domain_id >= 0) & (domain_id < E)
        idx = jnp.clip(domain_id, 0, E - 1)
        Wsel = expert_W[idx]
        bsel = expert_b[idx]
        expert_out = jnp.einsum('bsa,boa->bso', hidden, Wsel) + bsel[:, None, :]
        domain_output = jnp.where(valid[:, None, None], expert_out, hidden)
        hidden = domain_output + domain_emb[idx][:, None, :]
        hidden = jnp.einsum('bsa,da->bsd', hidden, up_W) + up_b
        x = hidden + residual
        mu = jnp.mean(x, axis=-1, keepdims=True)
        var = jnp.mean(jnp.square(x - mu), axis=-1, keepdims=True)
        return (x - mu) * jax.lax.rsqrt(var + LN_EPS) * ln_gamma + ln_beta

    def _L2_cond_ref(embeddings, theta, phi):
        import jax, jax.numpy as jnp
        import numpy as np
        B, N, D = embeddings.shape
        e = embeddings.reshape(B, N, D // 4, 4)
        ct = jnp.cos(theta)[:, None, None]
        st = jnp.sin(theta)[:, None, None]
        cp = jnp.cos(phi)[:, None, None]
        sp = jnp.sin(phi)[:, None, None]
        x0, x1, x2, x3 = (e[..., 0], e[..., 1], e[..., 2], e[..., 3])
        out = jnp.stack([x0 * ct + x1 * st, -x0 * st + x1 * ct, x2 * cp + x3 * sp, -x2 * sp + x3 * cp], axis=-1)
        return out.reshape(B, N, D)

    def _L3_cond_ref(hidden_states, domain_id, down_W, down_b, up_W, up_b, expert_W, expert_b, domain_emb, ln_gamma, ln_beta):
        import jax, jax.numpy as jnp
        import numpy as np
        B, S, D = (32, 256, 256)
        A = 64
        E = 16
        LN_EPS = 1e-05
        residual = hidden_states
        hidden = jnp.einsum('bsd,ad->bsa', hidden_states, down_W) + down_b
        hidden = jax.nn.gelu(hidden, approximate=False)
        valid = (domain_id >= 0) & (domain_id < E)
        idx = jnp.clip(domain_id, 0, E - 1)
        Wsel = expert_W[idx]
        bsel = expert_b[idx]
        expert_out = jnp.einsum('bsa,boa->bso', hidden, Wsel) + bsel[:, None, :]
        domain_output = jnp.where(valid[:, None, None], expert_out, hidden)
        hidden = domain_output + domain_emb[idx][:, None, :]
        hidden = jnp.einsum('bsa,da->bsd', hidden, up_W) + up_b
        x = hidden + residual
        mu = jnp.mean(x, axis=-1, keepdims=True)
        var = jnp.mean(jnp.square(x - mu), axis=-1, keepdims=True)
        return (x - mu) * jax.lax.rsqrt(var + LN_EPS) * ln_gamma + ln_beta
    x = _L0_cond_ref(x, mask_Bx1xSxS_bk0, itok_B_34_63, fside_Bx16xSxS_0, L0_cond_W_ada, L0_cond_b_ada, L0_cond_Wq, L0_cond_bq, L0_cond_Wk, L0_cond_bk, L0_cond_Wv, L0_cond_bv, L0_cond_Wo, L0_cond_bo, L0_cond_W1, L0_cond_b1, L0_cond_W2, L0_cond_b2, L0_cond_g2, L0_cond_beta2)
    x = _L1_cond_ref(x, itok_B_0_15, L1_cond_down_W, L1_cond_down_b, L1_cond_up_W, L1_cond_up_b, L1_cond_expert_W, L1_cond_expert_b, L1_cond_domain_emb, L1_cond_ln_gamma, L1_cond_ln_beta)
    x = _L2_cond_ref(x, condB_theta, condB_phi)
    x = _L3_cond_ref(x, itok_B_0_15, L3_cond_down_W, L3_cond_down_b, L3_cond_up_W, L3_cond_up_b, L3_cond_expert_W, L3_cond_expert_b, L3_cond_domain_emb, L3_cond_ln_gamma, L3_cond_ln_beta)
    return x

_drawn_inputs = setup_inputs


def setup_inputs(seed=0):
    import zlib

    import numpy as np

    out = dict(_drawn_inputs(seed))
    spreads = {'L0_cond_b_ada': (0.0, 0.1),
     'L0_cond_bq': (0.0, 0.8),
     'L0_cond_bk': (0.0, 0.8),
     'L0_cond_bv': (0.0, 0.408),
     'L0_cond_bo': (0.0, 0.1),
     'L0_cond_b1': (0.0, 0.337),
     'L0_cond_b2': (0.0, 0.1),
     'L0_cond_g2': (1.0, 0.6),
     'L0_cond_beta2': (0.0, 0.8),
     'L1_cond_ln_gamma': (1.0, 0.2),
     'L1_cond_ln_beta': (0.0, 0.1),
     'L3_cond_ln_gamma': (1.0, 0.2),
     'L3_cond_ln_beta': (0.0, 0.1)}
    factors = {'fside_Bx16xSxS_0': 8.0,
     'L0_cond_Wq': 8.0,
     'L0_cond_Wk': 8.0,
     'L0_cond_Wv': 4.729,
     'L1_cond_down_b': 8.0,
     'L3_cond_down_b': 8.0}
    for name, (base, spread) in spreads.items():
        noise = np.random.default_rng([zlib.crc32(name.encode()), seed]).standard_normal(out[name].shape)
        drawn = base * np.exp(spread * noise) if base else spread * noise
        out[name] = jnp.asarray(drawn.astype(out[name].dtype))
    for name, factor in factors.items():
        out[name] = (out[name] * factor).astype(out[name].dtype)
    return out
```

```python
from contextlib import ExitStack

import numpy as np

import concourse.bass as bass
from concourse import mybir

F32 = mybir.dt.float32
BF16 = mybir.dt.bfloat16
I32 = mybir.dt.int32
U8 = mybir.dt.uint8
ALU = mybir.AluOpType
ACT = mybir.ActivationFunctionType

P = 128
B, S, D, H, HD, F = 8, 512, 256, 16, 16, 1024
A, E = 64, 16
QT = S // P
DC = D // P
FC = F // P
HC = H // DC
G = 4
NG = H // G
VW = 32
STEPS = H * QT
EPS = 1e-5
MASKED = -1e30
QPIECE = [0, 0, 1, 0, 2, 1, 1, 2]
KPIECE = [0, 1, 0, 2, 0, 1, 2, 1]
NP8 = len(QPIECE)

INPUTS = [
    "x", "itok_B_34_63", "fside_Bx16xSxS_0", "itok_B_0_15", "condB_theta", "condB_phi", "mask_Bx1xSxS_bk0",
    "L0_cond_W_ada", "L0_cond_b_ada", "L0_cond_Wq", "L0_cond_bq", "L0_cond_Wk", "L0_cond_bk", "L0_cond_Wv",
    "L0_cond_bv", "L0_cond_Wo", "L0_cond_bo", "L0_cond_W1", "L0_cond_b1", "L0_cond_W2", "L0_cond_b2",
    "L0_cond_g2", "L0_cond_beta2",
] + [f"L{n}_cond_{w}" for n in (1, 3) for w in (
    "down_W", "down_b", "up_W", "up_b", "expert_W", "expert_b", "domain_emb", "ln_gamma", "ln_beta")]

BY_FEATURE = ("b_ada", "bq", "bk", "bo", "b1", "b2", "g2", "beta2")


def apart(eng, sem):
    eng.sem_inc(sem, 1)


class Count:

    def __init__(self, sem, per, ahead):
        self.sem, self.per, self.ahead = sem, per, ahead

    def at(self, b, k):
        return b * self.per + (self.ahead + k)


def load_layouts(d):
    v = dict(
        x=d["x"].rearrange("b (t p) d -> p b t d", p=P),
        bias=d["fside_Bx16xSxS_0"].rearrange("b h (t p) k -> p (b h) t k", p=P),
        mask=d["mask_Bx1xSxS_bk0"].rearrange("b o (t p) k -> p (b o) t k", p=P),
        out=d["out"].rearrange("b (t p) d -> p b t d", p=P),
    )
    for w in ("W_ada", "Wq", "Wk", "Wv", "Wo", "W1", "W2"):
        v[w] = d["L0_cond_" + w].rearrange("(c p) n -> p c n", p=P)
    for w in BY_FEATURE:
        v[w] = d["L0_cond_" + w]
    return v


def setup_block(nc, d, v, k):
    with ExitStack() as ctx:
        def sb(name, shape, dt=F32):
            return ctx.enter_context(nc.sbuf_tensor(name, shape, dt))

        def sem(name):
            return ctx.enter_context(nc.semaphore(name))

        w_ada = sb("w_ada", [P, DC, 2 * D])
        b_ada = sb("b_ada", [P, 4])
        freq = sb("freq", [P, 1])
        tok = sb("tok", [P, B], I32)
        tokf = sb("tokf", [P, 4, B])
        arg = sb("arg", [P, 6, B])
        turns = sb("turns", [P, 6, B])
        quarter = sb("quarter", [P, 6, B])
        emb = sb("emb", [P, DC, B])
        dom = sb("dom", [P, B], I32)
        domf = sb("domf", [P, 4, B])
        domi = sb("domi", [P, B], I32)
        wsel = sb("wsel", [A, 2, B, A])
        bsel = sb("bsel", [A, 2, B])
        dsel = sb("dsel", [A, 2, B])
        ada_ps = ctx.enter_context(nc.psum_tensor("ada_ps", [P, 4, B], F32))
        loaded = sem("loaded")
        cond_in = sem("cond_in")
        clipped = sem("clipped")
        chosen = sem("chosen")
        dve_step = sem("dve_step")
        sines = sem("sines")
        embedded = sem("embedded")
        ada_done = sem("ada_done")
        block = ctx.enter_context(nc.Block())
        loads = [
            (k["ident"][:], d["ident"]), (k["wq"][:], v["Wq"]), (k["wk"][:], v["Wk"]),
            (k["wv"][:], v["Wv"]), (k["wo"][:], v["Wo"]), (k["bq"][:], v["bq"]), (k["bk"][:], v["bk"]),
            (k["bo"][:], v["bo"]), (k["b1"][:], v["b1"]), (k["b2"][:], v["b2"]), (k["g2"][:], v["g2"]),
            (k["beta2"][:], v["beta2"]), (k["bv"][:], d["L0_cond_bv"].partition_broadcast(P)),
        ]
        for l, n in enumerate((1, 3)):
            loads += [
                (k["down_w"][:, l], d[f"L{n}_cond_down_W"].rearrange("(c p) a -> p c a", p=P)),
                (k["down_b"][:, l:l + 1], d[f"L{n}_cond_down_b"].rearrange("(a o) -> a o", o=1)),
                (k["up_w"][:, l], d[f"L{n}_cond_up_W"]),
                (k["up_b"][:, l], d[f"L{n}_cond_up_b"]),
                (k["gamma"][:, l], d[f"L{n}_cond_ln_gamma"].partition_broadcast(P)),
                (k["beta"][:, l], d[f"L{n}_cond_ln_beta"].partition_broadcast(P)),
            ]
        conds = [
            (tok[:], d["itok_B_34_63"].partition_broadcast(P)), (dom[:], d["itok_B_0_15"].partition_broadcast(P)),
            (arg[:, 2], d["condB_theta"].partition_broadcast(P)), (arg[:, 3], d["condB_theta"].partition_broadcast(P)),
            (arg[:, 4], d["condB_phi"].partition_broadcast(P)), (arg[:, 5], d["condB_phi"].partition_broadcast(P)),
            (freq[:], d["freq"]), (w_ada[:], v["W_ada"]), (b_ada[:], v["b_ada"]),
        ]

        @block.sync
        def _(sp):
            for dst, src in conds:
                sp.dma_start(dst, src).then_inc(cond_in, 16)
            for dst, src in loads:
                sp.dma_start(dst, src).then_inc(loaded, 16)
            sp.wait_ge(clipped, 1)
            for b in range(B):
                e = sp.value_load(domi[0:1, b:b + 1], min_val=0, max_val=E - 1)
                for l, n in enumerate((1, 3)):
                    for dst, name in ((wsel[:, l, b, :], "expert_W"), (bsel[:, l, b:b + 1], "expert_b"),
                                      (dsel[:, l, b:b + 1], "domain_emb")):
                        src = d[f"L{n}_cond_{name}"]
                        if name == "expert_W":
                            src = src[bass.ds(e, 1)].rearrange("e i o -> (e i) o")
                        else:
                            src = src[bass.ds(e, 1)].rearrange("e a -> a e")
                        sp.dma_start(dst, src).then_inc(chosen, 16)
            sp.wait_ge(loaded, 16 * len(loads))
            sp.wait_ge(chosen, 16 * 6 * B)

        @block.vector
        def _(dve):
            n = [0]

            def link(ins):
                n[0] += 1
                ins.then_inc(dve_step, 1)
                dve.wait_ge(dve_step, n[0])

            dve.memset(quarter[:], 0.0).then_inc(dve_step, 1)
            n[0] += 1
            dve.wait_ge(dve_step, n[0])
            for i in (1, 3, 5):
                link(dve.memset(quarter[:, i], 0.25))
            dve.wait_ge(cond_in, 16 * len(conds))
            link(dve.tensor_copy(domf[:, 0], dom[:]))
            link(dve.tensor_scalar(domf[:, 1], domf[:, 0], 0.0, E - 1.0, ALU.max, ALU.min))
            dve.tensor_copy(domi[:], domf[:, 1]).then_inc(clipped, 1)
            link(dve.tensor_tensor(domf[:, 2], domf[:, 0], domf[:, 1], ALU.is_equal))
            link(dve.tensor_scalar(domf[:, 3], domf[:, 2], -1.0, 1.0, ALU.mult, ALU.add))
            link(dve.tensor_copy(tokf[:, 0], tok[:]))
            link(dve.tensor_scalar(tokf[:, 1], tokf[:, 0], 0.01, None, ALU.mult))
            link(dve.tensor_copy(tokf[:, 2], tokf[:, 0]))
            for part in (64.0, 32.0, 4.0):
                link(dve.scalar_tensor_tensor(tokf[:, 3], tokf[:, 1], -part, tokf[:, 2], ALU.mult, ALU.add))
                link(dve.tensor_copy(tokf[:, 2], tokf[:, 3]))
            link(dve.scalar_tensor_tensor(tokf[:, 3], tokf[:, 2], 0.01, tokf[:, 1], ALU.mult, ALU.add))
            link(dve.tensor_scalar(tokf[:, 1], tokf[:, 3], 4000.0, None, ALU.mult))
            link(dve.tensor_scalar(arg[:, 0], tokf[:, 1], freq[:, 0:1], None, ALU.mult))
            link(dve.tensor_scalar(arg[:, 1], tokf[:, 1], freq[:, 0:1], None, ALU.mult))
            link(dve.scalar_tensor_tensor(turns[:], arg[:], 1.0 / (2.0 * np.pi), quarter[:], ALU.mult, ALU.add))
            link(dve.tensor_scalar(turns[:], turns[:], 12582912.0, None, ALU.add))
            link(dve.tensor_scalar(turns[:], turns[:], -12582912.0, None, ALU.add))
            for part in TWO_PI_PARTS:
                link(dve.scalar_tensor_tensor(arg[:], turns[:], -part, arg[:], ALU.mult, ALU.add))
            link(dve.scalar_tensor_tensor(arg[:], quarter[:], 2.0 * np.pi, arg[:], ALU.mult, ALU.add))
            dve.tensor_scalar(arg[:], arg[:], 3.1415925, -3.1415925, ALU.min, ALU.max).then_inc(sines, 1)
            dve.wait_ge(sines, 2)
            for i, (src, sign) in enumerate(((3, 1.0), (2, 1.0), (2, -1.0), (5, 1.0), (4, 1.0), (4, -1.0))):
                link(dve.tensor_scalar(k["rot"][:, i], k["trig"][:, src], sign, None, ALU.mult))
            dve.wait_ge(ada_done, 1)
            for c in range(4):
                link(dve.tensor_scalar(k["ada"][:, c], ada_ps[:, c], b_ada[:, c:c + 1], 1.0 if c < DC else 0.0,
                                       ALU.add, ALU.add))
            dve.wait_ge(chosen, 16 * 6 * B)
            dve.wait_ge(loaded, 16 * len(loads))
            for l in range(2):
                for b in range(B):
                    link(dve.tensor_scalar(wsel[:, l, b], wsel[:, l, b], domf[0:A, 2, b:b + 1], None, ALU.mult))
                    link(dve.scalar_tensor_tensor(k["expert_w"][:, l, b], k["ident"][0:A, 0:A],
                                                  domf[0:A, 3, b:b + 1], wsel[:, l, b], ALU.mult, ALU.add))
                link(dve.tensor_tensor(bsel[:, l], bsel[:, l], domf[0:A, 2], ALU.mult))
                link(dve.tensor_tensor(k["expert_b"][:, l], bsel[:, l], dsel[:, l], ALU.add))
            link(dve.tensor_copy(k["ident_bf"][:], k["ident"][:]))

        @block.scalar
        def _(act):
            act.wait_ge(sines, 1)
            act.activation(k["trig"][:], arg[:], ACT.Sin).then_inc(sines, 1)
            act.wait_ge(sines, 2)
            act.activation(emb[:], k["trig"][:, 0:2], ACT.Silu).then_inc(embedded, 1)

        @block.tensor
        def _(pe):
            pe.wait_ge(embedded, 1)
            pe.wait_ge(cond_in, 16 * len(conds))
            for c in range(4):
                for i in range(DC):
                    last = pe.matmul(ada_ps[:, c], w_ada[:, i, c * P:(c + 1) * P], emb[:, i],
                                     start=(i == 0), stop=(i == DC - 1))
            last.then_inc(ada_done, 1)


_c1 = 6.28125
_c2 = float(np.float32(np.round((2 * np.pi - _c1) * 2.0 ** 19) / 2.0 ** 19))
TWO_PI_PARTS = (_c1, _c2, 2 * np.pi - _c1 - _c2)

AHEAD = [("XT", 0, 9), ("XT", 1, 11), ("Q", 0, 13), ("Q", 1, 15), ("K", 0, 17), ("K", 1, 20)]
SPARE = AHEAD + [("O", 0, 23), ("V", 0, 26), ("V", 1, 29), ("O", 1, 38), ("O", 2, 54),
                 ("O", 3, STEPS), ("C", 0, STEPS), ("C", 1, STEPS), ("W", 0, STEPS), ("W", 1, STEPS)]
PROLOGUE = AHEAD + [("V", 0, 26), ("V", 1, 29)]


class SpareBanks:

    def __init__(self, kind):
        uses = dict(first=PROLOGUE, middle=SPARE, last=[u for u in SPARE if u[0] in "OCW"])[kind]
        self.kind = kind
        self.where = {u[:2]: (i % 2, i // 2) for i, u in enumerate(uses)}
        self.uses = uses

    def __contains__(self, use):
        return use in self.where

    def bank(self, use):
        return self.where[use][0]

    def before(self, use, b):
        k = self.where[use][1]
        return k if self.kind == "first" else b * (len(SPARE) // 2) + (len(PROLOGUE) // 2 + k)

    def after(self, use, b):
        return self.before(use, b) + 1


def attention_block(nc, d, v, k, x1_dram, pieces_dram):
    with ExitStack() as ctx:
        def sb(name, shape, dt=F32):
            return ctx.enter_context(nc.sbuf_tensor(name, shape, dt))

        def ps(name):
            return ctx.enter_context(nc.psum_tensor(name, [P, 512], F32))

        def sem(name):
            return ctx.enter_context(nc.semaphore(name))

        NB = 4
        xin = sb("xin", [P, QT, D])
        xhat = sb("xhat", [P, QT, D])
        stats = sb("stats", [P, QT, 6])
        mv = sb("mv", [P, QT, 2])
        std = sb("std", [P, QT])
        rstd = sb("rstd", [P, QT])
        eps = sb("eps", [P, 1])
        xt = sb("xt", [P, DC, S])
        xres = sb("xres", [P, DC, S])
        proj = sb("proj", [P, 2, S])
        rest = sb("rest", [P, S])
        pieces = sb("pieces", [P, 2, 3, DC, S], BF16)
        stack_q = sb("stack_q", [P, H, S], BF16)
        stack_k = sb("stack_k", [P, H, S], BF16)
        vst = sb("vst", [P, QT, D])
        val = sb("val", [P, QT, H, VW])
        mraw = sb("mraw", [P, QT, S], U8)
        mterm = sb("mterm", [P, QT, S], BF16)
        bias = sb("bias", [P, NB, QT, S])
        prob = sb("prob", [P, 2, QT, S])
        nmax = sb("nmax", [P, 2, QT])
        pt = sb("pt", [P, G, QT, S])
        osb = sb("osb", [P, S])
        rsum = sb("rsum", [P, QT, G, 1])
        con = sb("con", [P, QT, D])
        cont = sb("cont", [P, DC, S])
        x1 = sb("x1", [P, DC, S])

        s_bank = [ps(f"s_bank{i}") for i in range(3)]
        t_bank = [ps(f"t_bank{i}") for i in range(2)]
        o_bank = ps("o_bank")
        spare = [ps(f"spare{i}") for i in range(2)]

        x_in = Count(sem("x_in"), 16, 16)
        mask_in = Count(sem("mask_in"), 16, 16)
        stat_done = Count(sem("stat_done"), 1, 1)
        std_done = Count(sem("std_done"), 1, 1)
        xhat_done = Count(sem("xhat_done"), 1, 1)
        xt_done = Count(sem("xt_done"), DC, DC)
        proj_done = Count(sem("proj_done"), 4, 4)
        cut_done = Count(sem("cut_done"), 4, 4)
        pieces_out = Count(sem("pieces_out"), 64, 64)
        stack_in = [Count(sem(f"stack_in{c}"), 16 * 2 * NP8, 16 * 2 * NP8) for c in range(DC)]
        vst_done = Count(sem("vst_done"), 2, 2)
        val_done = Count(sem("val_done"), NG, NG)
        mask_done = Count(sem("mask_done"), QT, QT)
        res_done = Count(sem("res_done"), 1, 1)
        scored = Count(sem("scored"), STEPS, STEPS)
        biased = Count(sem("biased"), STEPS, STEPS)
        exped = Count(sem("exped"), STEPS, STEPS)
        turned = Count(sem("turned"), STEPS, STEPS)
        evac = [Count(sem("evac_act"), STEPS // 2, STEPS // 2), Count(sem("evac_dve"), STEPS // 2, STEPS // 2)]
        weighed = Count(sem("weighed"), NG, NG)
        o_out = Count(sem("o_out"), NG, NG)
        normed = Count(sem("normed"), NG, NG)
        cont_done = Count(sem("cont_done"), DC, DC)
        x1_done = Count(sem("x1_done"), DC, DC)
        x1_out = Count(sem("x1_out"), 16, 16)
        credited = [scored, biased, exped, turned, *evac, weighed, o_out, normed, cont_done,
                    x1_done, x1_out]
        bias_in = [sem(f"bias_in{i}") for i in range(NB)]
        spare_full = [sem(f"spare_full{i}") for i in range(2)]
        dve_link = sem("dve_link")
        pool_link = sem("pool_link")
        dve_apart = sem("dve_apart")
        pool_apart = sem("pool_apart")
        sp_apart = sem("sp_apart")
        consts = sem("consts")
        block = ctx.enter_context(nc.Block())

        def read_of(use, b):
            what, i = use
            count = dict(XT=xt_done, Q=proj_done, K=proj_done, V=vst_done, O=normed, C=cont_done, W=x1_done)[what]
            return count.sem, count.at(b, i + 1 + (DC if what == "K" else 0))

        @block.sync
        def _(sp):
            for c in credited:
                sp.sem_inc(c.sem, c.ahead)
            bias_flat = v["bias"]

            def load_bias(b, h):
                sp.dma_start(bias[:, h % NB], bias_flat[:, bass.ds(b * H + h, 1)].rearrange("p o t k -> p (o t) k")
                             ).then_inc(bias_in[h % NB], 16)

            def load_x(b):
                sp.wait_ge(xhat_done.sem, xhat_done.at(b - 1, 1))
                apart(sp, sp_apart)
                sp.dma_start(xin[:], v["x"][:, bass.ds(b + 1, 1)].rearrange("p o t k -> p (o t) k")
                             ).then_inc(x_in.sem, 16)
                sp.wait_ge(mask_done.sem, mask_done.at(b - 1, QT))
                apart(sp, sp_apart)
                sp.dma_start(mraw[:], v["mask"][:, bass.ds(b + 1, 1)].rearrange("p o t k -> p (o t) k")
                             ).then_inc(mask_in.sem, 16)

            def store_pieces(b, first=False):
                if not first:
                    for c in range(DC):
                        sp.wait_ge(stack_in[c].sem, stack_in[c].at(b - 1, stack_in[c].per))
                for qk in range(2):
                    for c in range(DC):
                        sp.wait_ge(cut_done.sem, cut_done.at(b, 2 * qk + c + 1))
                        sp.dma_start(pieces_dram[:, qk, c], pieces[:, qk, :, c, :]).then_inc(pieces_out.sem, 16)

            def load_stack(b, c, first=False):
                sp.wait_ge(pieces_out.sem, pieces_out.at(b, 64))
                if not first:
                    sp.wait_ge(scored.sem, scored.at(b, STEPS // 2 * (c + 1)))
                for qk, (stack, piece) in enumerate(((stack_q, QPIECE), (stack_k, KPIECE))):
                    for i in range(NP8):
                        src = pieces_dram[:, qk, c, piece[i]].rearrange("(h e) t -> e h t", e=HD)
                        sp.dma_start(stack[i * HD:(i + 1) * HD, c * HC:(c + 1) * HC], src
                                     ).then_inc(stack_in[c].sem, 16)

            def store_x1(b):
                sp.wait_ge(x1_done.sem, x1_done.at(b, DC))
                apart(sp, sp_apart)
                sp.dma_start(x1_dram[bass.ds(b, 1)].rearrange("o p c t -> (o p) c t"), x1[:]
                             ).then_inc(x1_out.sem, 16)

            def iteration(b, last=False):
                if not last:
                    load_x(b)
                for h in range(H):
                    if not (last and h + NB >= H):
                        sp.wait_ge(biased.sem, biased.at(b, QT * (h + 1)))
                        apart(sp, sp_apart)
                        load_bias(b, h + NB)
                    if h == 6 and not last:
                        store_pieces(b)
                    if h == 8 and not last:
                        load_stack(b, 0)
                if not last:
                    load_stack(b, 1)
                store_x1(b)

            sp.dma_start(xin[:], v["x"][:, 0]).then_inc(x_in.sem, 16)
            sp.dma_start(mraw[:], v["mask"][:, 0]).then_inc(mask_in.sem, 16)
            for h in range(NB):
                load_bias(0, h)
            store_pieces(-1, first=True)
            load_stack(-1, 0, first=True)
            load_stack(-1, 1, first=True)
            with sp.Fori(0, B - 1) as b:
                iteration(b)
            iteration(B - 1, last=True)
            sp.wait_ge(x1_out.sem, x1_out.at(B - 1, 16))

        @block.tensor
        def _(pe):
            ident = k["ident"]

            def spare_take(banks, use, b):
                at = banks.uses.index(next(u for u in banks.uses if u[:2] == use))
                if at >= 2:
                    pe.wait_ge(*read_of(banks.uses[at - 2][:2], b))
                elif banks.kind != "first":
                    pe.wait_ge(*read_of(("W", at), b - 1))
                    pe.wait_ge(*read_of(("V", at), b - 1))
                return spare[banks.bank(use)]

            def spare_give(banks, use, ins):
                ins.then_inc(spare_full[banks.bank(use)], 1)

            def scores(b, n):
                h, t = n // QT, n % QT
                if n % (STEPS // 2) == 0:
                    c = n // (STEPS // 2)
                    pe.wait_ge(stack_in[c].sem, stack_in[c].at(b - 1, stack_in[c].per))
                if n < QT:
                    pe.wait_ge(mask_done.sem, mask_done.at(b - 1, n + 1))
                before = n - 3 if n >= 3 else (63, 61, 62)[n] - STEPS
                pe.wait_ge(biased.sem, biased.at(b, before + 1))
                bank = s_bank[n % 3][:, :]
                pe.matmul(bank, stack_q[:, h, t * P:(t + 1) * P], stack_k[:, h, :], start=True, stop=False)
                pe.matmul(bank, k["ident_bf"][:], mterm[:, t, :], start=False, stop=True).then_inc(scored.sem, 1)

            def turn(b, n):
                h, t = n // QT, n % QT
                pe.wait_ge(exped.sem, exped.at(b, n + 1))
                pe.wait_ge(evac[n % 2].sem, evac[n % 2].at(b, n // 2))
                for c in range(QT):
                    last = pe.transpose(t_bank[n % 2][:, c * P:(c + 1) * P], prob[:, h % 2, t, c * P:(c + 1) * P],
                                        ident[:])
                last.then_inc(turned.sem, 1)

            def weigh(b, g):
                for e in evac:
                    pe.wait_ge(e.sem, e.at(b, 8 * (g + 1)))
                pe.wait_ge(val_done.sem, val_done.at(b - 1, g + 1))
                pe.wait_ge(o_out.sem, o_out.at(b, g))
                for c in range(QT):
                    for j in range(G):
                        last = pe.matmul(o_bank[VW * j:VW * (j + 1), :], val[:, c, G * g + j, :], pt[:, j, c, :],
                                         start=(c == 0), stop=(c == QT - 1), tile_position=(0, VW * j))
                last.then_inc(weighed.sem, 1)

            def spare_use(banks, use, b):
                what, i = use
                if what == "XT":
                    if i == 0:
                        pe.wait_ge(xhat_done.sem, xhat_done.at(b, 1))
                    bank = spare_take(banks, use, b)
                    for t in range(QT):
                        last = pe.transpose(bank[:, t * P:(t + 1) * P], xhat[:, t, i * P:(i + 1) * P], ident[:])
                elif what in "QK":
                    pe.wait_ge(xt_done.sem, xt_done.at(b, DC))
                    bank = spare_take(banks, use, b)
                    w = k["wq"] if what == "Q" else k["wk"]
                    for c in range(DC):
                        last = pe.matmul(bank[:, :], w[:, c, i * P:(i + 1) * P], xt[:, c, :],
                                         start=(c == 0), stop=(c == DC - 1))
                elif what == "V":
                    bank = spare_take(banks, use, b)
                    for t in range(2):
                        tok = (2 * i + t) * P
                        for c in range(DC):
                            last = pe.matmul(bank[:, t * D:(t + 1) * D], xt[:, c, tok:tok + P], k["wv"][:, c, :],
                                             start=(c == 0), stop=(c == DC - 1))
                elif what == "O":
                    pe.wait_ge(o_out.sem, o_out.at(b, i + 1))
                    bank = spare_take(banks, use, b)
                    for t in range(QT):
                        last = pe.transpose(bank[:, t * P:(t + 1) * P], osb[:, t * P:(t + 1) * P], ident[:])
                elif what == "C":
                    if i == 0:
                        pe.wait_ge(normed.sem, normed.at(b, NG))
                    bank = spare_take(banks, use, b)
                    for t in range(QT):
                        last = pe.transpose(bank[:, t * P:(t + 1) * P], con[:, t, i * P:(i + 1) * P], ident[:])
                elif what == "W":
                    if i == 0:
                        pe.wait_ge(cont_done.sem, cont_done.at(b, DC))
                    bank = spare_take(banks, use, b)
                    for c in range(DC):
                        last = pe.matmul(bank[:, :], k["wo"][:, c, i * P:(i + 1) * P], cont[:, c, :],
                                         start=(c == 0), stop=(c == DC - 1))
                spare_give(banks, use, last)

            def iteration(b, last=False):
                banks = SpareBanks("last" if last else "middle")
                for n in range(3):
                    scores(b, n)
                for n in range(STEPS):
                    if n + 3 < STEPS:
                        scores(b, n + 3)
                    if n % 16 == 1 and n > 16:
                        weigh(b, n // 16 - 1)
                    turn(b, n)
                    for use in banks.uses:
                        if use[2] == n:
                            spare_use(banks, use[:2], b)
                weigh(b, NG - 1)
                for use in banks.uses:
                    if use[2] == STEPS:
                        spare_use(banks, use[:2], b)

            banks = SpareBanks("first")
            for use in banks.uses:
                spare_use(banks, use[:2], -1)
            with pe.Fori(0, B - 1) as b:
                iteration(b)
            iteration(B - 1, last=True)

        @block.vector
        def _(dve):
            links = [0]
            per_link = [None]

            def link(b, ins):
                links[0] += 1
                ins.then_inc(dve_link, 1)
                dve.wait_ge(dve_link, links[0] if per_link[0] is None else b * per_link[0] + links[0])

            def add_bias(b, n):
                h, t = n // QT, n % QT
                if t == 0:
                    dve.wait_ge(bias_in[h % NB], b * (16 * H // NB) + 16 * (h // NB + 1))
                dve.wait_ge(scored.sem, scored.at(b, n + 1))
                dve.wait_ge(turned.sem, turned.at(b, n + 1 - 2 * QT))
                apart(dve, dve_apart)
                dve.tensor_tensor_reduce(out=prob[:, h % 2, t, :], in0=s_bank[n % 3][:, :],
                                         in1=bias[:, h % NB, t, :], scale=-1.0, scalar=3e38,
                                         op0=ALU.add, op1=ALU.min, accum_out=nmax[:, h % 2, t:t + 1]
                                         ).then_inc(biased.sem, 1)

            def take_turned(b, n):
                h, t = n // QT, n % QT
                dve.wait_ge(turned.sem, turned.at(b, n + 1))
                dve.wait_ge(weighed.sem, weighed.at(b, h // G))
                dve.tensor_copy(pt[:, h % G, :, t * P:(t + 1) * P],
                                t_bank[n % 2][:, :].rearrange("p (c q) -> p c q", c=QT)).then_inc(evac[1].sem, 1)

            def statistics(b):
                dve.wait_ge(x_in.sem, x_in.at(b, 16))
                for t in range(QT):
                    last = dve.bn_stats(stats[:, t], xin[:, t])
                link(b, last)
                apart(dve, dve_apart)
                for t in range(QT):
                    last = dve.bn_aggr(mv[:, t], stats[:, t])
                last.then_inc(stat_done.sem, 1)

            def normalise(b):
                dve.wait_ge(std_done.sem, std_done.at(b, 1))
                link(b, dve.reciprocal(rstd[:], std[:]))
                for t in range(QT):
                    last = dve.tensor_scalar(xhat[:, t], xin[:, t], mv[:, t, 0:1], rstd[:, t:t + 1],
                                             ALU.subtract, ALU.mult)
                last.then_inc(xhat_done.sem, 1)

            def spare_use(banks, use, b, first=False):
                what, i = use
                s = spare[banks.bank(use)]
                dve.wait_ge(spare_full[banks.bank(use)], banks.after(use, b))
                if what == "XT":
                    if i == 0 and not first:
                        dve.wait_ge(res_done.sem, res_done.at(b - 1, 1))
                    dve.tensor_scalar(xt[:, i], s[:, :], k["ada"][:, i, bass.ds(b + 1, 1)],
                                      k["ada"][:, DC + i, bass.ds(b + 1, 1)], ALU.mult, ALU.add
                                      ).then_inc(xt_done.sem, 1)
                elif what in "QK":
                    u = 2 * "QK".index(what) + i
                    if not (first and u < 2):
                        dve.wait_ge(cut_done.sem, cut_done.at(b, u - 1))
                    dve.tensor_scalar(proj[:, u % 2], s[:, :], k["bq" if what == "Q" else "bk"][:, i:i + 1],
                                      HD ** -0.5 if what == "Q" else 1.0, ALU.add, ALU.mult
                                      ).then_inc(proj_done.sem, 1)
                elif what == "V":
                    if i == 0 and not first:
                        dve.wait_ge(val_done.sem, val_done.at(b - 1, NG))
                    for t in range(2):
                        last = dve.tensor_tensor(vst[:, 2 * i + t], s[:, t * D:(t + 1) * D], k["bv"][:], ALU.add)
                    last.then_inc(vst_done.sem, 1)
                elif what == "O":
                    o = s[:, :].rearrange("p (t j e) -> p t j e", t=QT, j=G)
                    link(b, dve.reciprocal(rsum[:], o[:, :, :, HD:HD + 1]))
                    dve.tensor_tensor(con[:, :, i * G * HD:(i + 1) * G * HD].rearrange("p t (j e) -> p t j e", j=G),
                                      o[:, :, :, 0:HD], rsum[:].to_broadcast([P, QT, G, HD]), ALU.mult
                                      ).then_inc(normed.sem, 1)
                elif what == "C":
                    dve.tensor_copy(cont[:, i], s[:, :]).then_inc(cont_done.sem, 1)
                elif what == "W":
                    dve.wait_ge(res_done.sem, res_done.at(b - 1, 1))
                    dve.wait_ge(x1_out.sem, x1_out.at(b, 0))
                    dve.scalar_tensor_tensor(x1[:, i], s[:, :], k["bo"][:, i:i + 1], xres[:, i],
                                             ALU.add, ALU.add).then_inc(x1_done.sem, 1)

            def iteration(b, last=False):
                banks = SpareBanks("last" if last else "middle")
                for n in range(2):
                    add_bias(b, n)
                for n in range(STEPS + 1):
                    if n + 2 < STEPS:
                        add_bias(b, n + 2)
                    if n % 2 == 0 and n > 0:
                        take_turned(b, n - 1)
                    if not last and n == 4:
                        statistics(b)
                    if not last and n == 7:
                        normalise(b)
                    for use in banks.uses:
                        if use[2] + 1 == n and n <= STEPS - 1:
                            spare_use(banks, use[:2], b)
                for use in banks.uses:
                    if use[2] == STEPS:
                        spare_use(banks, use[:2], b)

            dve.memset(val[:], 0.0).then_inc(consts, 1)
            dve.wait_ge(consts, 1)
            dve.memset(val[:, :, :, HD:HD + 1], 1.0).then_inc(consts, 1)
            dve.memset(eps[:], EPS).then_inc(consts, 1)
            statistics(-1)
            normalise(-1)
            banks = SpareBanks("first")
            for use in banks.uses:
                spare_use(banks, use[:2], -1, first=True)
            before = links[0]
            links_a, links_o = 2, NG
            per_link[0] = links_a + links_o
            with dve.Fori(0, B - 1) as b:
                iteration(b)
            assert links[0] - before == per_link[0]
            links[0] = before
            iteration(B - 1, last=True)

        @block.scalar
        def _(act):
            def exponent(b, n):
                h, t = n // QT, n % QT
                act.wait_ge(biased.sem, biased.at(b, n + 1))
                tile = prob[:, h % 2, t, :]
                act.activation(tile, tile, ACT.Exp, bias=nmax[:, h % 2, t:t + 1], scale=-1.0
                               ).then_inc(exped.sem, 1)

            def take_turned(b, n):
                h, t = n // QT, n % QT
                act.wait_ge(turned.sem, turned.at(b, n + 1))
                act.wait_ge(weighed.sem, weighed.at(b, h // G))
                act.copy(pt[:, h % G, :, t * P:(t + 1) * P],
                         t_bank[n % 2][:, :].rearrange("p (c q) -> p c q", c=QT)).then_inc(evac[0].sem, 1)

            def deviation(b):
                act.wait_ge(stat_done.sem, stat_done.at(b, 1))
                act.activation(std[:], mv[:, :, 1], ACT.Sqrt, bias=eps[:, 0:1]).then_inc(std_done.sem, 1)

            def take_context(b, g):
                act.wait_ge(weighed.sem, weighed.at(b, g + 1))
                act.wait_ge(normed.sem, normed.at(b, g))
                act.copy(osb[:], o_bank[:, :]).then_inc(o_out.sem, 1)

            def iteration(b, last=False):
                exponent(b, 0)
                for n in range(STEPS):
                    if n + 1 < STEPS:
                        exponent(b, n + 1)
                    if n % 2 == 1:
                        take_turned(b, n - 1)
                    if not last and n == 5:
                        deviation(b)
                    if n % 16 == 2 and n > 16:
                        take_context(b, n // 16 - 1)
                take_context(b, NG - 1)

            act.wait_ge(consts, 3)
            deviation(-1)
            with act.Fori(0, B - 1) as b:
                iteration(b)
            iteration(B - 1, last=True)

        @block.gpsimd
        def _(pool):
            links = [0]
            per_link = [None]

            def link(b, ins):
                links[0] += 1
                ins.then_inc(pool_link, 1)
                pool.wait_ge(pool_link, links[0] if per_link[0] is None else b * per_link[0] + links[0])

            def cut(b, u, first=False):
                qk, c = u // 2, u % 2
                pool.wait_ge(proj_done.sem, proj_done.at(b, u + 1))
                if u == 0 and not first:
                    pool.wait_ge(pieces_out.sem, pieces_out.at(b - 1, 64))
                high, mid, low = (pieces[:, qk, i, c, :] for i in range(3))
                apart(pool, pool_apart)
                link(b, pool.tensor_copy(high, proj[:, u % 2]))
                link(b, pool.tensor_tensor(rest[:], proj[:, u % 2], high, ALU.subtract))
                apart(pool, pool_apart)
                link(b, pool.tensor_copy(mid, rest[:]))
                pool.tensor_tensor(low, rest[:], mid, ALU.subtract).then_inc(cut_done.sem, 1)
                pool.wait_ge(cut_done.sem, cut_done.at(b, u + 1))

            def copy_values(b, g, first=False):
                if g == 0:
                    pool.wait_ge(vst_done.sem, vst_done.at(b, 2))
                if not first:
                    pool.wait_ge(weighed.sem, weighed.at(b, g + 1))
                apart(pool, pool_apart)
                for t in range(QT):
                    last = pool.tensor_copy(val[:, t, G * g:G * (g + 1), 0:HD],
                                            vst[:, t, G * HD * g:G * HD * (g + 1)].rearrange("p (j e) -> p j e", j=G))
                last.then_inc(val_done.sem, 1)

            def mask_term(b, t, first=False):
                if t == 0:
                    pool.wait_ge(mask_in.sem, mask_in.at(b, 16))
                if not first:
                    pool.wait_ge(scored.sem, scored.at(b, STEPS - QT + t + 1))
                apart(pool, pool_apart)
                pool.tensor_scalar(mterm[:, t, :], mraw[:, t, :], MASKED, None, ALU.mult).then_inc(mask_done.sem, 1)

            def keep_residual(b, first=False):
                pool.wait_ge(xt_done.sem, xt_done.at(b, DC))
                if not first:
                    pool.wait_ge(x1_done.sem, x1_done.at(b, DC))
                apart(pool, pool_apart)
                pool.tensor_copy(xres[:], xt[:]).then_inc(res_done.sem, 1)

            def iteration(b):
                for u in range(4):
                    cut(b, u)
                for g in range(NG - 1):
                    copy_values(b, g)
                for t in range(QT):
                    mask_term(b, t)
                copy_values(b, NG - 1)
                keep_residual(b)

            for t in range(QT):
                mask_term(-1, t, first=True)
            for u in range(4):
                cut(-1, u, first=True)
            pool.wait_ge(consts, 2)
            for g in range(NG):
                copy_values(-1, g, first=True)
            keep_residual(-1, first=True)
            before = links[0]
            per_link[0] = 3 * 4
            with pool.Fori(0, B - 1) as b:
                iteration(b)
            assert links[0] - before == per_link[0]


def network_block(nc, d, v, k, x1_dram):
    U = 2
    with ExitStack() as ctx:
        def sb(name, shape, dt=F32):
            return ctx.enter_context(nc.sbuf_tensor(name, shape, dt))

        def sem(name):
            return ctx.enter_context(nc.semaphore(name))

        w1 = sb("w1", [P, DC, F])
        w2 = sb("w2", [P, FC, D])
        x1s = sb("x1s", [P, U, DC, S])
        xh = sb("xh", [P, U, QT, D])
        ht = sb("ht", [P, U, DC, S])
        gt = sb("gt", [P, U, FC, S])
        x2 = sb("x2", [P, U, DC, S])
        hid = sb("hid", [A, U, S])
        exp_out = sb("exp_out", [A, U, S])
        x3 = sb("x3", [P, U, DC, S])
        y = sb("y", [P, U, QT, D])
        y2 = sb("y2", [P, U, QT, D])
        z = sb("z", [P, U, QT, D])
        x4 = sb("x4", [P, U, DC, S])
        res = sb("res", [P, U, QT, D])
        stats = sb("stats3", [P, U, QT, 6])
        mv = sb("mv3", [P, U, QT, 2])
        std = sb("std3", [P, U, QT])
        rstd = sb("rstd3", [P, U, QT])
        eps = sb("eps3", [P, 1])
        ew = sb("ew", [A, U, 2, A])
        bank = [[ctx.enter_context(nc.psum_tensor(f"bank{u}{i}", [P, 512], F32)) for i in range(4)]
                for u in range(U)]

        N3 = 3
        x1_in = [Count(sem(f"x1_in{u}"), 16, 0) for u in range(U)]
        ew_done = Count(sem("ew_done"), U, 0)
        to_t = [Count(sem(f"to_t{i}"), U, 0) for i in range(N3)]
        stat_done = [Count(sem(f"stat_done{i}"), U, 0) for i in range(N3)]
        std_done = [Count(sem(f"std_done{i}"), U, 0) for i in range(N3)]
        norm_done = [Count(sem(f"norm_done{i}"), U, U if i == 2 else 0) for i in range(N3)]
        to_f = [Count(sem(f"to_f{i}"), U, 0) for i in range(2)]
        ht_done = Count(sem("ht_done"), U, 0)
        w1_done = Count(sem("w1_done"), U * FC, 0)
        gt_done = Count(sem("gt_done"), U * FC, 0)
        w2_done = Count(sem("w2_done"), U, 0)
        x2_done = Count(sem("x2_done"), U, U)
        down_done = [Count(sem(f"down_done{i}"), U, 0) for i in range(2)]
        hid_done = [Count(sem(f"hid_done{i}"), U, 0) for i in range(2)]
        expert_done = [Count(sem(f"expert_done{i}"), U, U if i == 1 else 0) for i in range(2)]
        exp_done = [Count(sem(f"exp_done{i}"), U, 0) for i in range(2)]
        up_done = [Count(sem(f"up_done{i}"), U, 0) for i in range(2)]
        x3_done = [Count(sem(f"x3_done{i}"), U, 0) for i in range(2)]
        z_done = Count(sem("z_done"), U, 0)
        x4_done = Count(sem("x4_done"), U, 0)
        res_done = Count(sem("out_made"), U, 0)
        stored = [Count(sem(f"stored{u}"), 16, 16) for u in range(U)]
        scaled = Count(sem("scaled"), U, U)
        credited = [norm_done[2], x2_done, expert_done[1], *stored, scaled]
        eps_set = sem("eps_set")
        weights_in = sem("weights_in")
        dve_link = sem("dve_link3")
        dve_apart = sem("dve_apart3")
        pool_apart = sem("pool_apart3")
        sp_apart = sem("sp_apart3")
        pe_apart = sem("pe_apart3")
        block = ctx.enter_context(nc.Block())
        PAIRS = B // U

        @block.sync
        def _(sp):
            for c in credited:
                sp.sem_inc(c.sem, c.ahead)
            sp.dma_start(w1[:], v["W1"]).then_inc(weights_in, 16)
            sp.dma_start(w2[:], v["W2"]).then_inc(weights_in, 16)
            with sp.Fori(0, PAIRS) as j:
                for u in range(U):
                    sp.wait_ge(x2_done.sem, x2_done.at(j - 1, u + 1))
                    apart(sp, sp_apart)
                    sp.dma_start(x1s[:, u], x1_dram[bass.ds(j * U + u, 1)].rearrange("o p c t -> (o p) c t")
                                 ).then_inc(x1_in[u].sem, 16)
                for u in range(U):
                    sp.wait_ge(res_done.sem, res_done.at(j, u + 1))
                    apart(sp, sp_apart)
                    sp.dma_start(v["out"][:, bass.ds(j * U + u, 1)].rearrange("p o t k -> p (o t) k"), res[:, u]
                                 ).then_inc(stored[u].sem, 16)
            for u in range(U):
                sp.wait_ge(stored[u].sem, stored[u].at(PAIRS - 1, 16))

        @block.tensor
        def _(pe):
            ident = k["ident"]

            def to_tokens(j, u, i, src):
                for t in range(QT):
                    for c in range(DC):
                        at = (t % 2) * D + c * P
                        last = pe.transpose(bank[u][t // 2][:, at:at + P], src[:, u, c, t * P:(t + 1) * P], ident[:])
                last.then_inc(to_t[i].sem, 1)

            def to_features(j, u, i, src):
                for c in range(DC):
                    for t in range(QT):
                        last = pe.transpose(bank[u][2 + c][:, t * P:(t + 1) * P], src[:, u, t, c * P:(c + 1) * P],
                                            ident[:])
                last.then_inc(to_f[i].sem, 1)

            def down(j, u, l, src):
                for c in range(DC):
                    last = pe.matmul(bank[u][0][0:A, :], k["down_w"][:, l, c, :], src[:, u, c, :],
                                     start=(c == 0), stop=(c == DC - 1))
                last.then_inc(down_done[l].sem, 1)

            def expert(j, u, l):
                pe.wait_ge(hid_done[l].sem, hid_done[l].at(j, u + 1))
                pe.wait_ge(ew_done.sem, ew_done.at(j, u + 1))
                apart(pe, pe_apart)
                pe.matmul(bank[u][1][0:A, :], ew[:, u, l, :], hid[:, u, :], start=True, stop=True
                          ).then_inc(expert_done[l].sem, 1)

            def up(j, u, l):
                pe.wait_ge(exp_done[l].sem, exp_done[l].at(j, u + 1))
                for c in range(DC):
                    last = pe.matmul(bank[u][2 + c][:, :], k["up_w"][:, l, c * P:(c + 1) * P], exp_out[:, u, :],
                                     start=True, stop=True)
                last.then_inc(up_done[l].sem, 1)

            def adapter(j, l, src, ready):
                for u in range(U):
                    pe.wait_ge(ready.sem, ready.at(j, u + 1))
                    down(j, u, l, src)
                for u in range(U):
                    expert(j, u, l)
                for u in range(U):
                    up(j, u, l)

            with pe.Fori(0, PAIRS) as j:
                for u in range(U):
                    pe.wait_ge(x1_in[u].sem, x1_in[u].at(j, 16))
                    pe.wait_ge(norm_done[2].sem, norm_done[2].at(j - 1, u + 1))
                    to_tokens(j, u, 0, x1s)
                pe.wait_ge(weights_in, 32)
                for u in range(U):
                    pe.wait_ge(norm_done[0].sem, norm_done[0].at(j, u + 1))
                    to_features(j, u, 0, xh)
                for u in range(U):
                    pe.wait_ge(ht_done.sem, ht_done.at(j, u + 1))
                    for f in range(FC):
                        if f >= 2:
                            pe.wait_ge(gt_done.sem, gt_done.at(j, u * FC + f - 1))
                        for c in range(DC):
                            last = pe.matmul(bank[u][f % 2][:, :], w1[:, c, f * P:(f + 1) * P], ht[:, u, c, :],
                                             start=(c == 0), stop=(c == DC - 1))
                        last.then_inc(w1_done.sem, 1)
                for u in range(U):
                    for c in range(DC):
                        for f in range(FC):
                            if c == 0:
                                pe.wait_ge(gt_done.sem, gt_done.at(j, u * FC + f + 1))
                            last = pe.matmul(bank[u][2 + c][:, :], w2[:, f, c * P:(c + 1) * P], gt[:, u, f, :],
                                             start=(f == 0), stop=(f == FC - 1))
                    last.then_inc(w2_done.sem, 1)
                adapter(j, 0, x2, x2_done)
                for u in range(U):
                    pe.wait_ge(x3_done[0].sem, x3_done[0].at(j, u + 1))
                    to_tokens(j, u, 1, x3)
                for u in range(U):
                    pe.wait_ge(z_done.sem, z_done.at(j, u + 1))
                    to_features(j, u, 1, z)
                adapter(j, 1, x4, x4_done)
                for u in range(U):
                    pe.wait_ge(x3_done[1].sem, x3_done[1].at(j, u + 1))
                    to_tokens(j, u, 2, x3)

        @block.vector
        def _(dve):
            links = [0]
            PER_LINK = U * (2 * N3 + 3)

            def link(j, ins):
                links[0] += 1
                ins.then_inc(dve_link, 1)
                dve.wait_ge(dve_link, j * PER_LINK + links[0])

            def tile(u, t):
                return bank[u][t // 2][:, (t % 2) * D:(t % 2 + 1) * D]

            def statistics(j, u, i):
                dve.wait_ge(to_t[i].sem, to_t[i].at(j, u + 1))
                for t in range(QT):
                    last = dve.bn_stats(stats[:, u, t], tile(u, t))
                link(j, last)
                apart(dve, dve_apart)
                for t in range(QT):
                    last = dve.bn_aggr(mv[:, u, t], stats[:, u, t])
                last.then_inc(stat_done[i].sem, 1)

            def normalise(j, u, i, dst):
                dve.wait_ge(std_done[i].sem, std_done[i].at(j, u + 1))
                link(j, dve.reciprocal(rstd[:, u], std[:, u]))
                for t in range(QT):
                    last = dve.tensor_scalar(dst[:, u, t], tile(u, t), mv[:, u, t, 0:1], rstd[:, u, t:t + 1],
                                             ALU.subtract, ALU.mult)
                last.then_inc(norm_done[i].sem, 1)

            def add(j, u, ready, bias, res, dst, done):
                dve.wait_ge(ready.sem, ready.at(j, u + 1))
                for c in range(DC):
                    last = dve.scalar_tensor_tensor(dst[:, u, c], bank[u][2 + c][:, :], bias[:, c:c + 1], res[:, u, c],
                                                    ALU.add, ALU.add)
                last.then_inc(done.sem, 1)

            def take_expert(j, u, l):
                dve.wait_ge(expert_done[l].sem, expert_done[l].at(j, u + 1))
                dve.tensor_scalar(exp_out[:, u], bank[u][1][0:A, :], k["expert_b"][:, l, bass.ds(j * U + u, 1)], None,
                                  ALU.add).then_inc(exp_done[l].sem, 1)

            def rotate(j, u):
                dve.wait_ge(norm_done[1].sem, norm_done[1].at(j, u + 1))
                gamma = k["gamma"][:, 0:1].to_broadcast([P, QT, D])
                beta = k["beta"][:, 0:1].to_broadcast([P, QT, D])
                link(j, dve.tensor_tensor(y2[:, u], y[:, u], gamma, ALU.mult))
                link(j, dve.tensor_tensor(y[:, u], y2[:, u], beta, ALU.add))
                src, tmp, dst = (w[:, u].rearrange("p t (i e) -> p (t i) e", e=4) for w in (y, y2, z))

                def coef(i):
                    return k["rot"][:, i, bass.ds(j * U + u, 1)]

                dve.tensor_scalar(tmp[:, :, 0:2], src[:, :, 0:2], coef(0), None, ALU.mult)
                link(j, dve.tensor_scalar(tmp[:, :, 2:4], src[:, :, 2:4], coef(3), None, ALU.mult))
                for e, other, c in ((0, 1, 1), (1, 0, 2), (2, 3, 4), (3, 2, 5)):
                    last = dve.scalar_tensor_tensor(dst[:, :, e], src[:, :, other], coef(c), tmp[:, :, e],
                                                    ALU.mult, ALU.add)
                last.then_inc(z_done.sem, 1)

            def adapter(j, l, res):
                for u in range(U):
                    take_expert(j, u, l)
                for u in range(U):
                    add(j, u, up_done[l], k["up_b"][:, l], res, x3, x3_done[l])
                for u in range(U):
                    statistics(j, u, l + 1)

            dve.memset(eps[:], EPS).then_inc(eps_set, 1)
            with dve.Fori(0, PAIRS) as j:
                for u in range(U):
                    statistics(j, u, 0)
                for u in range(U):
                    dve.wait_ge(scaled.sem, scaled.at(j - 1, u + 1))
                    normalise(j, u, 0, xh)
                for u in range(U):
                    add(j, u, w2_done, k["b2"], x1s, x2, x2_done)
                adapter(j, 0, x2)
                for u in range(U):
                    normalise(j, u, 1, y)
                    rotate(j, u)
                adapter(j, 1, x4)
                for u in range(U):
                    normalise(j, u, 2, xh)
            assert links[0] == PER_LINK

        @block.scalar
        def _(act):
            def deviation(j, i):
                for u in range(U):
                    act.wait_ge(stat_done[i].sem, stat_done[i].at(j, u + 1))
                    act.activation(std[:, u], mv[:, u, :, 1], ACT.Sqrt, bias=eps[:, 0:1]).then_inc(std_done[i].sem, 1)

            def adapter(j, l):
                for u in range(U):
                    act.wait_ge(down_done[l].sem, down_done[l].at(j, u + 1))
                    act.activation(hid[:, u], bank[u][0][0:A, :], ACT.Gelu, bias=k["down_b"][:, l:l + 1]
                                   ).then_inc(hid_done[l].sem, 1)

            act.wait_ge(eps_set, 1)
            with act.Fori(0, PAIRS) as j:
                deviation(j, 0)
                for u in range(U):
                    act.wait_ge(to_f[0].sem, to_f[0].at(j, u + 1))
                    for c in range(DC):
                        last = act.activation(ht[:, u, c], bank[u][2 + c][:, :], ACT.Identity,
                                              bias=k["beta2"][:, c:c + 1], scale=k["g2"][:, c:c + 1])
                    last.then_inc(ht_done.sem, 1)
                for u in range(U):
                    for f in range(FC):
                        act.wait_ge(w1_done.sem, w1_done.at(j, u * FC + f + 1))
                        act.activation(gt[:, u, f], bank[u][f % 2][:, :], ACT.Gelu_apprx_sigmoid,
                                       bias=k["b1"][:, f:f + 1]).then_inc(gt_done.sem, 1)
                adapter(j, 0)
                deviation(j, 1)
                for u in range(U):
                    act.wait_ge(to_f[1].sem, to_f[1].at(j, u + 1))
                    for c in range(DC):
                        last = act.copy(x4[:, u, c], bank[u][2 + c][:, :])
                    last.then_inc(x4_done.sem, 1)
                adapter(j, 1)
                deviation(j, 2)

        @block.gpsimd
        def _(pool):
            with pool.Fori(0, PAIRS) as j:
                for u in range(U):
                    pool.wait_ge(expert_done[1].sem, expert_done[1].at(j - 1, u + 1))
                    apart(pool, pool_apart)
                    pool.tensor_copy(ew[:, u], k["expert_w"][:, :, bass.ds(j * U + u, 1)].rearrange(
                        "p l o a -> p l (o a)")).then_inc(ew_done.sem, 1)
                for u in range(U):
                    pool.wait_ge(norm_done[2].sem, norm_done[2].at(j, u + 1))
                    pool.wait_ge(stored[u].sem, stored[u].at(j - 1, 16))
                    pool.tensor_tensor(res[:, u], xh[:, u], k["gamma"][:, 1:2].to_broadcast([P, QT, D]), ALU.mult
                                       ).then_inc(scaled.sem, 1)
                    pool.wait_ge(scaled.sem, scaled.at(j, u + 1))
                    pool.tensor_tensor(res[:, u], res[:, u], k["beta"][:, 1:2].to_broadcast([P, QT, D]), ALU.add
                                       ).then_inc(res_done.sem, 1)


def build(nc, d):
    v = load_layouts(d)
    x1_dram = nc.dram_tensor("x1_dram", [B, P, DC, S], F32, kind="Internal").ap()
    pieces_dram = nc.dram_tensor("pieces_dram", [2, DC, 3, P, S], BF16, kind="Internal").ap()
    pieces_dram = pieces_dram.rearrange("q c i p t -> p q c i t")
    with ExitStack() as ctx:
        def sb(name, shape, dt=F32):
            return ctx.enter_context(nc.sbuf_tensor(name, shape, dt))

        k = dict(
            ident=sb("ident", [P, P]), ident_bf=sb("ident_bf", [P, P], BF16),
            wq=sb("wq", [P, DC, D]), wk=sb("wk", [P, DC, D]), wv=sb("wv", [P, DC, D]), wo=sb("wo", [P, DC, D]),
            bq=sb("bq", [P, DC]), bk=sb("bk", [P, DC]), bv=sb("bv", [P, D]), bo=sb("bo", [P, DC]),
            b1=sb("b1", [P, FC]), b2=sb("b2", [P, DC]), g2=sb("g2", [P, DC]), beta2=sb("beta2", [P, DC]),
            down_w=sb("down_w", [P, 2, DC, A]), down_b=sb("down_b", [A, 2]),
            up_w=sb("up_w", [A, 2, D]), up_b=sb("up_b", [P, 2, DC]),
            gamma=sb("gamma", [P, 2, D]), beta=sb("beta", [P, 2, D]),
            expert_w=sb("expert_w", [A, 2, B, A]), expert_b=sb("expert_b", [A, 2, B]),
            ada=sb("ada", [P, 4, B]), trig=sb("trig", [P, 6, B]), rot=sb("rot", [P, 6, B]),
        )
        setup_block(nc, d, v, k)
        attention_block(nc, d, v, k, x1_dram, pieces_dram)
        network_block(nc, d, v, k, x1_dram)


def kernel(**inputs):
    import concourse.bacc as bacc
    from concourse.bass_utils import run_bass_kernel_spmd

    nc = bacc.Bacc("TRN2", target_bir_lowering=False, num_devices=1)
    arrays = {}
    for name in INPUTS:
        a = np.asarray(inputs[name])
        if name.endswith("down_W") or name.endswith("up_W"):
            a = a.T
        elif name.endswith("expert_W"):
            a = a.transpose(0, 2, 1)
        elif name.endswith("up_b") or name in ["L0_cond_" + w for w in BY_FEATURE]:
            a = a.reshape(-1, P).T
        arrays[name] = np.ascontiguousarray(a)
    arrays["ident"] = np.eye(P, dtype=np.float32)
    half = D // 2
    freq = np.exp(np.arange(half, dtype=np.float32) * np.float32(-np.log(10000.0) / (half - 1)))
    arrays["freq"] = freq.astype(np.float32).reshape(P, 1)
    d = {name: nc.dram_tensor("in_" + name, a.shape, mybir.dt.from_np(a.dtype), kind="ExternalInput").ap()
         for name, a in arrays.items()}
    d["out"] = nc.dram_tensor("out", (B, S, D), F32, kind="ExternalOutput").ap()
    build(nc, d)
    r = run_bass_kernel_spmd(nc, [{"in_" + n: a for n, a in arrays.items()}], core_ids=[0])
    return r.results[0]["out"]
```

```python
from contextlib import ExitStack

import numpy as np

import concourse.bass as bass
from concourse import mybir

F32 = mybir.dt.float32
BF16 = mybir.dt.bfloat16
F32R = mybir.dt.float32r
I32 = mybir.dt.int32
U8 = mybir.dt.uint8
ALU = mybir.AluOpType
ACT = mybir.ActivationFunctionType

P = 128
B, S, D, H, HD, F = 8, 512, 256, 16, 16, 1024
A, E = 64, 16
QT = S // P
DC = D // P
FC = F // P
HC = H // DC
G = 4
NG = H // G
VW = 32
STEPS = H * QT
EPS = 1e-5
MASKED = -1e30
QPIECE = [0, 0, 1, 0, 2, 1, 1, 2]
KPIECE = [0, 1, 0, 2, 0, 1, 2, 1]
NP8 = len(QPIECE)

INPUTS = [
    "x", "itok_B_34_63", "fside_Bx16xSxS_0", "itok_B_0_15", "condB_theta", "condB_phi", "mask_Bx1xSxS_bk0",
    "L0_cond_W_ada", "L0_cond_b_ada", "L0_cond_Wq", "L0_cond_bq", "L0_cond_Wk", "L0_cond_bk", "L0_cond_Wv",
    "L0_cond_bv", "L0_cond_Wo", "L0_cond_bo", "L0_cond_W1", "L0_cond_b1", "L0_cond_W2", "L0_cond_b2",
    "L0_cond_g2", "L0_cond_beta2",
] + [f"L{n}_cond_{w}" for n in (1, 3) for w in (
    "down_W", "down_b", "up_W", "up_b", "expert_W", "expert_b", "domain_emb", "ln_gamma", "ln_beta")]

BY_FEATURE = ("b_ada", "bq", "bk", "bo", "b1", "b2", "g2", "beta2")


LATE_LOADS = 21
HALVES = (slice(0, A), slice(A, P))


def apart(eng, sem):
    eng.sem_inc(sem, 1)


class Count:

    def __init__(self, sem, per, ahead):
        self.sem, self.per, self.ahead = sem, per, ahead

    def at(self, b, k):
        if isinstance(b, int):
            b = min(b, B - 1)
        return b * self.per + (self.ahead + k)


def load_layouts(d):
    v = dict(
        x=d["x"].rearrange("b (t p) d -> p b t d", p=P),
        bias=d["fside_Bx16xSxS_0"].rearrange("b h (t p) k -> p (b h) t k", p=P),
        mask=d["mask_Bx1xSxS_bk0"].rearrange("b o (t p) k -> p (b o) t k", p=P),
        out=d["out"].rearrange("b (t p) d -> p b t d", p=P),
    )
    for w in ("W_ada", "Wq", "Wk", "Wv", "Wo", "W1", "W2"):
        v[w] = d["L0_cond_" + w].rearrange("(c p) n -> p c n", p=P)
    for w in BY_FEATURE:
        v[w] = d["L0_cond_" + w]
    return v


def setup_block(nc, d, v, k, first_loads, bank):
    with ExitStack() as ctx:
        def sb(name, shape, dt=F32):
            return ctx.enter_context(nc.sbuf_tensor(name, shape, dt))

        def sem(name):
            return ctx.enter_context(nc.semaphore(name))

        w_ada = sb("w_ada", [P, DC, 2 * D])
        b_ada = sb("b_ada", [P, 4])
        freq = sb("freq", [P, 1])
        tok = sb("tok", [P, B], I32)
        tokf = sb("tokf", [P, 4, B])
        arg = sb("arg", [P, 6, B])
        turns = sb("turns", [P, 6, B])
        quarter = sb("quarter", [P, 6, B])
        emb = sb("emb", [P, DC, B])
        dom = sb("dom", [P, B], I32)
        pairs = sb("pairs", [P, 2])
        rotp = sb("rotp", [P, 2, B])
        ada_ps = bank[:, 0:4 * B].rearrange("p (c b) -> p c b", b=B)
        cond_in = sem("cond_in")
        dve_step = sem("dve_step")
        sines = sem("sines")
        embedded = sem("embedded")
        ada_done = sem("ada_done")
        block = ctx.enter_context(nc.Block())
        conds = [
            (tok[:], d["itok_B_34_63"].partition_broadcast(P)), (dom[:], d["itok_B_0_15"].partition_broadcast(P)),
            (arg[:, 2], d["condB_theta"].partition_broadcast(P)), (arg[:, 3], d["condB_theta"].partition_broadcast(P)),
            (arg[:, 4], d["condB_phi"].partition_broadcast(P)), (arg[:, 5], d["condB_phi"].partition_broadcast(P)),
            (freq[:], d["freq"]), (pairs[:], d["pairs"]), (w_ada[:], v["W_ada"]), (b_ada[:], v["b_ada"]),
        ]

        @block.sync
        def _(sp):
            for dst, src in conds:
                sp.dma_start(dst, src).then_inc(cond_in, 16)
            for dst, src, arrived in first_loads:
                sp.dma_start(dst, src).then_inc(arrived, 16)
        @block.vector
        def _(dve):
            n = [0]

            def link(ins):
                n[0] += 1
                ins.then_inc(dve_step, 1)
                dve.wait_ge(dve_step, n[0])

            dve.memset(quarter[:], 0.0).then_inc(dve_step, 1)
            n[0] += 1
            dve.wait_ge(dve_step, n[0])
            for i in (1, 3, 5):
                link(dve.memset(quarter[:, i], 0.25))
            dve.wait_ge(cond_in, 16 * len(conds))
            link(dve.tensor_copy(k["domf"][:, 0], dom[:]))
            link(dve.tensor_scalar(k["domf"][:, 1], k["domf"][:, 0], 0.0, E - 1.0, ALU.max, ALU.min))
            link(dve.tensor_copy(k["domi"][:], k["domf"][:, 1]))
            link(dve.tensor_tensor(k["domf"][:, 2], k["domf"][:, 0], k["domf"][:, 1], ALU.is_equal))
            link(dve.tensor_scalar(k["domf"][:, 3], k["domf"][:, 2], -1.0, 1.0, ALU.mult, ALU.add))
            link(dve.tensor_copy(tokf[:, 0], tok[:]))
            link(dve.tensor_scalar(tokf[:, 1], tokf[:, 0], 0.01, None, ALU.mult))
            link(dve.tensor_copy(tokf[:, 2], tokf[:, 0]))
            for part in (64.0, 32.0, 4.0):
                link(dve.scalar_tensor_tensor(tokf[:, 3], tokf[:, 1], -part, tokf[:, 2], ALU.mult, ALU.add))
                link(dve.tensor_copy(tokf[:, 2], tokf[:, 3]))
            link(dve.scalar_tensor_tensor(tokf[:, 3], tokf[:, 2], 0.01, tokf[:, 1], ALU.mult, ALU.add))
            link(dve.tensor_scalar(tokf[:, 1], tokf[:, 3], 4000.0, None, ALU.mult))
            link(dve.tensor_scalar(arg[:, 0], tokf[:, 1], freq[:, 0:1], None, ALU.mult))
            link(dve.tensor_scalar(arg[:, 1], tokf[:, 1], freq[:, 0:1], None, ALU.mult))
            link(dve.scalar_tensor_tensor(turns[:], arg[:], 1.0 / (2.0 * np.pi), quarter[:], ALU.mult, ALU.add))
            link(dve.tensor_scalar(turns[:], turns[:], 12582912.0, None, ALU.add))
            link(dve.tensor_scalar(turns[:], turns[:], -12582912.0, None, ALU.add))
            for part in TWO_PI_PARTS:
                link(dve.scalar_tensor_tensor(arg[:], turns[:], -part, arg[:], ALU.mult, ALU.add))
            link(dve.scalar_tensor_tensor(arg[:], quarter[:], 2.0 * np.pi, arg[:], ALU.mult, ALU.add))
            dve.tensor_scalar(arg[:], arg[:], 3.1415925, -3.1415925, ALU.min, ALU.max).then_inc(sines, 1)
            dve.wait_ge(sines, 2)
            for i in range(2):
                link(dve.tensor_scalar(rotp[:, i], k["trig"][:, 5 - i], pairs[:, 1:2], None, ALU.mult))
                link(dve.scalar_tensor_tensor(k["rot"][:, i], k["trig"][:, 3 - i], pairs[:, 0:1], rotp[:, i],
                                              ALU.mult, ALU.add))
            dve.wait_ge(ada_done, 1)
            for c in range(4):
                link(dve.tensor_scalar(k["ada"][:, c], ada_ps[:, c], b_ada[:, c:c + 1], 1.0 if c < DC else 0.0,
                                       ALU.add, ALU.add))
        @block.scalar
        def _(act):
            act.wait_ge(sines, 1)
            act.activation(k["trig"][:], arg[:], ACT.Sin).then_inc(sines, 1)
            act.wait_ge(sines, 2)
            act.activation(emb[:], k["trig"][:, 0:2], ACT.Silu).then_inc(embedded, 1)

        @block.tensor
        def _(pe):
            pe.wait_ge(embedded, 1)
            pe.wait_ge(cond_in, 16 * len(conds))
            for c in range(4):
                for i in range(DC):
                    last = pe.matmul(ada_ps[:, c], w_ada[:, i, c * P:(c + 1) * P], emb[:, i],
                                     start=(i == 0), stop=(i == DC - 1))
            last.then_inc(ada_done, 1)


_c1 = 6.28125
_c2 = float(np.float32(np.round((2 * np.pi - _c1) * 2.0 ** 19) / 2.0 ** 19))
TWO_PI_PARTS = (_c1, _c2, 2 * np.pi - _c1 - _c2)

TAIL = [("O", 3, 3, 1), ("C", 0, 5, 1), ("C", 1, 6, 1), ("W", 0, 8, 1), ("W", 1, 9, 1)]
AHEAD = [("XT", 0, 12, 0), ("XT", 1, 14, 0), ("Q", 0, 16, 0), ("K", 0, 18, 0), ("Q", 1, 20, 0), ("K", 1, 22, 0)]
VALUES = [("V", 0, 27, 0), ("V", 1, 30, 0)]
GROUPS = [("O", 0, 24, 0), ("O", 1, 38, 0), ("O", 2, 54, 0)]
SPARE = TAIL + AHEAD + GROUPS[:1] + VALUES + GROUPS[1:]
PROLOGUE = AHEAD + VALUES
LAST = TAIL + GROUPS
FINAL = [(what, i, STEPS, 0) for what, i, _, _ in TAIL]


class SpareBanks:

    def __init__(self, kind):
        self.uses = dict(first=PROLOGUE, middle=SPARE, last=LAST + FINAL)[kind]
        self.kind = kind

    def full(self, n, b):
        k = n // 2 + 1
        return k if self.kind == "first" else b * (len(SPARE) // 2) + (len(PROLOGUE) // 2 + k)


def attention_block(nc, d, v, k, x1_dram, pieces_dram):
    with ExitStack() as ctx:
        def sb(name, shape, dt=F32):
            return ctx.enter_context(nc.sbuf_tensor(name, shape, dt))

        def ps(name):
            return ctx.enter_context(nc.psum_tensor(name, [P, 512], F32))

        def sem(name):
            return ctx.enter_context(nc.semaphore(name))

        NB = 4
        ident_bf = sb("ident_bf", [P, P], BF16)
        xin = sb("xin", [P, QT, D])
        xhat = sb("xhat", [P, QT, D])
        stats = sb("stats", [P, QT, 6])
        mv = sb("mv", [P, QT, 2])
        std = sb("std", [P, QT])
        rstd = sb("rstd", [P, QT])
        eps = sb("eps", [P, 1])
        xt = sb("xt", [P, DC, S])
        xres = sb("xres", [P, DC, S])
        proj = sb("proj", [P, 2, S])
        rest = sb("rest", [P, S])
        pieces = sb("pieces", [P, 2, 3, DC, S], BF16)
        stack_q = sb("stack_q", [P, H, S], BF16)
        stack_k = sb("stack_k", [P, H, S], BF16)
        vst = sb("vst", [P, QT, D])
        val = sb("val", [P, QT, H, VW])
        mraw = sb("mraw", [P, QT, S], U8)
        mterm = sb("mterm", [P, QT, S], BF16)
        bias = sb("bias", [P, NB, QT, S])
        prob = sb("prob", [P, 2, QT, S])
        nmax = sb("nmax", [P, 2, QT])
        pt = sb("pt", [P, G, QT, S])
        osb = sb("osb", [P, S])
        rsum = sb("rsum", [P, QT, G, 1])
        con = sb("con", [P, QT, D])
        cont = sb("cont", [P, DC, S])
        x1 = sb("x1", [P, DC, S])

        s_bank = [ps(f"s_bank{i}") for i in range(3)]
        t_bank = [ps(f"t_bank{i}") for i in range(2)]
        o_bank = ps("o_bank")
        spare = [ps(f"spare{i}") for i in range(2)]

        x_in = Count(sem("x_in"), 16, 16)
        mask_in = Count(sem("mask_in"), 16, 16)
        stat_done = Count(sem("stat_done"), 1, 1)
        std_done = Count(sem("std_done"), 1, 1)
        xhat_done = Count(sem("xhat_done"), 1, 1)
        xt_done = Count(sem("xt_done"), DC, DC)
        proj_done = Count(sem("proj_done"), 4, 4)
        cut_done = Count(sem("cut_done"), 4, 4)
        pieces_out = [Count(sem(f"pieces_out{c}"), 32, 32) for c in range(DC)]
        stack_in = [Count(sem(f"stack_in{c}"), 16 * 2 * NP8, 16 * 2 * NP8) for c in range(DC)]
        vst_done = Count(sem("vst_done"), 2, 2)
        val_done = Count(sem("val_done"), NG, NG)
        mask_done = Count(sem("mask_done"), QT, QT)
        res_done = Count(sem("res_done"), 1, 1)
        scored = Count(sem("scored"), STEPS, STEPS)
        biased = Count(sem("biased"), STEPS, STEPS)
        exped = Count(sem("exped"), STEPS, STEPS)
        turned = Count(sem("turned"), STEPS, STEPS)
        evac = [Count(sem("evac_act"), STEPS // 2, STEPS // 2), Count(sem("evac_dve"), STEPS // 2, STEPS // 2)]
        weighed = Count(sem("weighed"), NG, NG)
        o_out = Count(sem("o_out"), NG, NG)
        normed = Count(sem("normed"), NG, NG)
        cont_done = Count(sem("cont_done"), DC, DC)
        x1_done = Count(sem("x1_done"), DC, DC)
        x1_out = Count(sem("x1_out"), 16, 16)
        credited = [scored, biased, exped, turned, *evac, weighed, o_out, normed, cont_done,
                    x1_done, x1_out]
        bias_in = [sem(f"bias_in{i}") for i in range(NB)]
        spare_full = [sem(f"spare_full{i}") for i in range(2)]
        dve_link = sem("dve_link")
        pool_link = sem("pool_link")
        dve_apart = sem("dve_apart")
        pool_apart = sem("pool_apart")
        sp_apart = sem("sp_apart")
        consts = sem("consts")
        ident_bf_made = sem("ident_bf_made")
        early_in, weights_in = sem("early_in"), sem("weights_in2")
        w = {n: sb(n, [P, DC, D]) for n in ("wq", "wk", "wv", "wo")}
        vec = {n: sb(n, [P, DC]) for n in ("bq", "bk", "bo")}
        bv = sb("bv", [P, D])
        early = [(k["ident"], d["ident"]), (w["wq"], v["Wq"]), (w["wk"], v["Wk"]), (vec["bq"], v["bq"]),
                 (vec["bk"], v["bk"])]
        later = [(w["wv"], v["Wv"]), (bv, d["L0_cond_bv"].partition_broadcast(P)), (w["wo"], v["Wo"]),
                 (vec["bo"], v["bo"])]
        late_loads = [(k["b1"][:], v["b1"]), (k["b2"][:], v["b2"]), (k["g2"][:], v["g2"]),
                      (k["beta2"][:], v["beta2"])]
        for l, n in enumerate((1, 3)):
            late_loads += [
                (k["down_w"][:, l], d[f"L{n}_cond_down_W"].rearrange("(c p) a -> p c a", p=P)),
                (k["up_b"][:, l], d[f"L{n}_cond_up_b"]),
            ]
            for rows in HALVES:
                late_loads += [
                    (k["down_b"][rows, l:l + 1], d[f"L{n}_cond_down_b"].rearrange("(a o) -> a o", o=1)),
                    (k["up_w"][rows, l], d[f"L{n}_cond_up_W"]),
                ]
        late_loads += [
            (k["gamma_f"][:], d["L1_cond_ln_gamma"]), (k["beta_f"][:], d["L1_cond_ln_beta"]),
            (k["gamma"][:], d["L3_cond_ln_gamma"].partition_broadcast(P)),
            (k["beta"][:], d["L3_cond_ln_beta"].partition_broadcast(P)),
            (k["beside"][:], d["beside"]),
        ]
        assert len(late_loads) == LATE_LOADS
        first_loads = [(xin[:], v["x"][:, 0], x_in.sem)] + [(dst[:], src, early_in) for dst, src in early]
        first_loads += [(mraw[:], v["mask"][:, 0], mask_in.sem)] + [(dst[:], src, weights_in) for dst, src in later]
        first_loads += [(bias[:, h], v["bias"][:, h], bias_in[h]) for h in range(NB)]
        setup_block(nc, d, v, k, first_loads, s_bank[0])
        block = ctx.enter_context(nc.Block())

        def read_of(use, b):
            what, i, _, back = use
            count = dict(XT=xt_done, Q=proj_done, K=proj_done, V=vst_done, O=normed, C=cont_done, W=x1_done)[what]
            if what in "QK":
                i = 2 * i + "QK".index(what)
            return count.sem, count.at(b - back, i + 1)

        @block.sync
        def _(sp):
            for c in credited:
                sp.sem_inc(c.sem, c.ahead)
            bias_flat = v["bias"]

            def load_bias(b, h):
                sp.dma_start(bias[:, h % NB], bias_flat[:, bass.ds(b * H + h, 1)].rearrange("p o t k -> p (o t) k")
                             ).then_inc(bias_in[h % NB], 16)

            def load_x(b):
                sp.wait_ge(xhat_done.sem, xhat_done.at(b - 1, 1))
                apart(sp, sp_apart)
                sp.dma_start(xin[:], v["x"][:, bass.ds(b + 1, 1)].rearrange("p o t k -> p (o t) k")
                             ).then_inc(x_in.sem, 16)
                sp.wait_ge(mask_done.sem, mask_done.at(b - 1, QT))
                apart(sp, sp_apart)
                sp.dma_start(mraw[:], v["mask"][:, bass.ds(b + 1, 1)].rearrange("p o t k -> p (o t) k")
                             ).then_inc(mask_in.sem, 16)

            def store_pieces(b, c, first=False):
                if not first:
                    sp.wait_ge(stack_in[c].sem, stack_in[c].at(b - 1, stack_in[c].per))
                    apart(sp, sp_apart)
                for qk in range(2):
                    sp.wait_ge(cut_done.sem, cut_done.at(b, 2 * c + qk + 1))
                    apart(sp, sp_apart)
                    sp.dma_start(pieces_dram[:, qk, c], pieces[:, qk, :, c, :]).then_inc(pieces_out[c].sem, 16)

            def load_stack(b, c, first=False):
                sp.wait_ge(pieces_out[c].sem, pieces_out[c].at(b, 32))
                apart(sp, sp_apart)
                if not first:
                    sp.wait_ge(scored.sem, scored.at(b, STEPS // 2 * (c + 1)))
                for qk, (stack, piece) in enumerate(((stack_q, QPIECE), (stack_k, KPIECE))):
                    for i in range(NP8):
                        src = pieces_dram[:, qk, c, piece[i]].rearrange("(h e) t -> e h t", e=HD)
                        sp.dma_start(stack[i * HD:(i + 1) * HD, c * HC:(c + 1) * HC], src
                                     ).then_inc(stack_in[c].sem, 16)

            def store_x1(b):
                sp.wait_ge(x1_done.sem, x1_done.at(b, DC))
                apart(sp, sp_apart)
                sp.dma_start(x1_dram[bass.ds(b, 1)].rearrange("o p c t -> (o p) c t"), x1[:]
                             ).then_inc(x1_out.sem, 16)

            def iteration(b, first=False, last=False):
                if not last:
                    load_x(b)
                for h in range(H):
                    if not (last and h + NB >= H):
                        sp.wait_ge(biased.sem, biased.at(b, QT * (h + 1)))
                        apart(sp, sp_apart)
                        load_bias(b, h + NB)
                    if h == 2 and not first:
                        store_x1(b - 1)
                    if h == 7 and not last:
                        for c in range(DC):
                            store_pieces(b, c)
                    if h == 9 and not last:
                        load_stack(b, 0)
                if not last:
                    load_stack(b, 1)

            for c in range(DC):
                store_pieces(-1, c, first=True)
                load_stack(-1, c, first=True)
            iteration(0, first=True)
            with sp.Fori(1, B - 1) as b:
                iteration(b)
            for dst, src in late_loads:
                sp.dma_start(dst, src).then_inc(k["late_in"], 16)
            iteration(B - 1, last=True)
            store_x1(B - 1)
            sp.wait_ge(x1_out.sem, x1_out.at(B - 1, 16))

        @block.tensor
        def _(pe):
            ident = k["ident"]

            def spare_take(banks, n, b):
                if n >= 2:
                    pe.wait_ge(*read_of(banks.uses[n - 2], b))
                elif banks.kind != "first":
                    pe.wait_ge(*read_of(SPARE[n - 2], b - 1))
                return spare[n % 2]

            def scores(b, n):
                h, t = n // QT, n % QT
                if n % (STEPS // 2) == 0:
                    c = n // (STEPS // 2)
                    pe.wait_ge(stack_in[c].sem, stack_in[c].at(b - 1, stack_in[c].per))
                if n < QT:
                    pe.wait_ge(mask_done.sem, mask_done.at(b - 1, n + 1))
                before = n - 3 if n >= 3 else (63, 61, 62)[n] - STEPS
                pe.wait_ge(biased.sem, biased.at(b, before + 1))
                bank = s_bank[n % 3][:, :]
                pe.matmul(bank, stack_q[:, h, t * P:(t + 1) * P], stack_k[:, h, :], start=True, stop=False)
                pe.matmul(bank, ident_bf[:], mterm[:, t, :], start=False, stop=True).then_inc(scored.sem, 1)

            def turn(b, n):
                h, t = n // QT, n % QT
                pe.wait_ge(exped.sem, exped.at(b, n + 1))
                pe.wait_ge(evac[n % 2].sem, evac[n % 2].at(b, n // 2))
                for c in range(QT):
                    last = pe.transpose(t_bank[n % 2][:, c * P:(c + 1) * P], prob[:, h % 2, t, c * P:(c + 1) * P],
                                        ident[:])
                last.then_inc(turned.sem, 1)

            def weigh(b, g):
                for e in evac:
                    pe.wait_ge(e.sem, e.at(b, 8 * (g + 1)))
                pe.wait_ge(val_done.sem, val_done.at(b - 1, g + 1))
                pe.wait_ge(o_out.sem, o_out.at(b, g))
                for c in range(QT):
                    for j in range(G):
                        last = pe.matmul(o_bank[VW * j:VW * (j + 1), :], val[:, c, G * g + j, :], pt[:, j, c, :],
                                         start=(c == 0), stop=(c == QT - 1), tile_position=(0, VW * j))
                last.then_inc(weighed.sem, 1)

            def spare_use(banks, n, b):
                what, i, _, back = banks.uses[n]
                if what == "XT":
                    if i == 0:
                        pe.wait_ge(xhat_done.sem, xhat_done.at(b, 1))
                    bank = spare_take(banks, n, b)
                    for t in range(QT):
                        last = pe.transpose(bank[:, t * P:(t + 1) * P], xhat[:, t, i * P:(i + 1) * P], ident[:])
                elif what in "QK":
                    pe.wait_ge(xt_done.sem, xt_done.at(b, DC))
                    bank = spare_take(banks, n, b)
                    for c in range(DC):
                        last = pe.matmul(bank[:, :], w["wq" if what == "Q" else "wk"][:, c, i * P:(i + 1) * P],
                                         xt[:, c, :], start=(c == 0), stop=(c == DC - 1))
                elif what == "V":
                    bank = spare_take(banks, n, b)
                    for t in range(2):
                        tok = (2 * i + t) * P
                        for c in range(DC):
                            last = pe.matmul(bank[:, t * D:(t + 1) * D], xt[:, c, tok:tok + P], w["wv"][:, c, :],
                                             start=(c == 0), stop=(c == DC - 1))
                elif what == "O":
                    pe.wait_ge(o_out.sem, o_out.at(b - back, i + 1))
                    bank = spare_take(banks, n, b)
                    for t in range(QT):
                        last = pe.transpose(bank[:, t * P:(t + 1) * P], osb[:, t * P:(t + 1) * P], ident[:])
                elif what == "C":
                    if i == 0:
                        pe.wait_ge(normed.sem, normed.at(b - back, NG))
                    bank = spare_take(banks, n, b)
                    for t in range(QT):
                        last = pe.transpose(bank[:, t * P:(t + 1) * P], con[:, t, i * P:(i + 1) * P], ident[:])
                elif what == "W":
                    if i == 0:
                        pe.wait_ge(cont_done.sem, cont_done.at(b - back, DC))
                    bank = spare_take(banks, n, b)
                    for c in range(DC):
                        last = pe.matmul(bank[:, :], w["wo"][:, c, i * P:(i + 1) * P], cont[:, c, :],
                                         start=(c == 0), stop=(c == DC - 1))
                last.then_inc(spare_full[n % 2], 1)

            def iteration(b, first=False, last=False):
                banks = SpareBanks("last" if last else "middle")
                for n in range(STEPS):
                    if n + 3 < STEPS:
                        scores(b, n + 3)
                    elif not last:
                        scores(b + 1, n + 3 - STEPS)
                    if n == 1 and not first:
                        weigh(b - 1, NG - 1)
                    if n % 16 == 1 and n > 16:
                        weigh(b, n // 16 - 1)
                    turn(b, n)
                    for m, use in enumerate(banks.uses):
                        if use[2] == n and not (first and use in TAIL):
                            spare_use(banks, m, b)
                if last:
                    weigh(b, NG - 1)
                    for m in range(len(LAST), len(banks.uses)):
                        spare_use(banks, m, b)

            banks = SpareBanks("first")
            pe.wait_ge(early_in, 16 * len(early))
            for m, use in enumerate(banks.uses):
                if use in VALUES:
                    pe.wait_ge(weights_in, 16 * len(later))
                spare_use(banks, m, -1)
            pe.wait_ge(ident_bf_made, 1)
            pe.wait_ge(vst_done.sem, vst_done.at(-1, 2))
            for m in range(len(TAIL)):
                pe.sem_inc(spare_full[m % 2], 1)
            for n in range(3):
                scores(0, n)
            iteration(0, first=True)
            with pe.Fori(1, B - 1) as b:
                iteration(b)
            iteration(B - 1, last=True)

        @block.vector
        def _(dve):
            links = [0]
            per_link = 2 + NG

            def link(b, ins):
                links[0] += 1
                ins.then_inc(dve_link, 1)
                dve.wait_ge(dve_link, links[0] if isinstance(b, int) else (b - 1) * per_link + links[0])

            def add_bias(b, n):
                h, t = n // QT, n % QT
                if t == 0:
                    dve.wait_ge(bias_in[h % NB], b * (16 * H // NB) + 16 * (h // NB + 1))
                dve.wait_ge(scored.sem, scored.at(b, n + 1))
                dve.wait_ge(turned.sem, turned.at(b, n + 1 - 2 * QT))
                apart(dve, dve_apart)
                dve.tensor_tensor_reduce(out=prob[:, h % 2, t, :], in0=s_bank[n % 3][:, :],
                                         in1=bias[:, h % NB, t, :], scale=-1.0, scalar=3e38,
                                         op0=ALU.add, op1=ALU.min, accum_out=nmax[:, h % 2, t:t + 1]
                                         ).then_inc(biased.sem, 1)

            def take_turned(b, n):
                h, t = n // QT, n % QT
                dve.wait_ge(turned.sem, turned.at(b, n + 1))
                dve.wait_ge(weighed.sem, weighed.at(b, h // G))
                dve.tensor_copy(pt[:, h % G, :, t * P:(t + 1) * P],
                                t_bank[n % 2][:, :].rearrange("p (c q) -> p c q", c=QT)).then_inc(evac[1].sem, 1)

            def statistics(b):
                dve.wait_ge(x_in.sem, x_in.at(b, 16))
                for t in range(QT):
                    last = dve.bn_stats(stats[:, t], xin[:, t])
                link(b, last)
                apart(dve, dve_apart)
                for t in range(QT):
                    last = dve.bn_aggr(mv[:, t], stats[:, t])
                last.then_inc(stat_done.sem, 1)

            def normalise(b):
                dve.wait_ge(std_done.sem, std_done.at(b, 1))
                link(b, dve.reciprocal(rstd[:], std[:]))
                for t in range(QT):
                    last = dve.tensor_scalar(xhat[:, t], xin[:, t], mv[:, t, 0:1], rstd[:, t:t + 1],
                                             ALU.subtract, ALU.mult)
                last.then_inc(xhat_done.sem, 1)

            def spare_use(banks, m, b, first=False):
                what, i, _, back = banks.uses[m]
                s = spare[m % 2]
                dve.wait_ge(spare_full[m % 2], banks.full(m, b))
                if what == "XT":
                    if i == 0 and not first:
                        dve.wait_ge(res_done.sem, res_done.at(b - 1, 1))
                    dve.tensor_scalar(xt[:, i], s[:, :], k["ada"][:, i, bass.ds(b + 1, 1)],
                                      k["ada"][:, DC + i, bass.ds(b + 1, 1)], ALU.mult, ALU.add
                                      ).then_inc(xt_done.sem, 1)
                elif what in "QK":
                    u = 2 * i + "QK".index(what)
                    if not (first and u < 2):
                        dve.wait_ge(cut_done.sem, cut_done.at(b, u - 1))
                    dve.tensor_scalar(proj[:, u % 2], s[:, :], vec["bq" if what == "Q" else "bk"][:, i:i + 1],
                                      HD ** -0.5 if what == "Q" else 1.0, ALU.add, ALU.mult
                                      ).then_inc(proj_done.sem, 1)
                elif what == "V":
                    if i == 0 and not first:
                        dve.wait_ge(val_done.sem, val_done.at(b - 1, NG))
                    for t in range(2):
                        last = dve.tensor_tensor(vst[:, 2 * i + t], s[:, t * D:(t + 1) * D], bv[:], ALU.add)
                    last.then_inc(vst_done.sem, 1)
                elif what == "O":
                    o = s[:, :].rearrange("p (t j e) -> p t j e", t=QT, j=G)
                    link(b, dve.reciprocal(rsum[:], o[:, :, :, HD:HD + 1]))
                    dve.tensor_tensor(con[:, :, i * G * HD:(i + 1) * G * HD].rearrange("p t (j e) -> p t j e", j=G),
                                      o[:, :, :, 0:HD], rsum[:].to_broadcast([P, QT, G, HD]), ALU.mult
                                      ).then_inc(normed.sem, 1)
                elif what == "C":
                    dve.tensor_copy(cont[:, i], s[:, :]).then_inc(cont_done.sem, 1)
                elif what == "W":
                    dve.wait_ge(res_done.sem, res_done.at(b - back - 1, 1))
                    dve.wait_ge(x1_out.sem, x1_out.at(b - back, 0))
                    dve.scalar_tensor_tensor(x1[:, i], s[:, :], vec["bo"][:, i:i + 1], xres[:, i],
                                             ALU.add, ALU.add).then_inc(x1_done.sem, 1)

            def iteration(b, first=False, last=False):
                banks = SpareBanks("last" if last else "middle")
                for n in range(STEPS + 1):
                    if n + 2 < STEPS:
                        add_bias(b, n + 2)
                    elif n < STEPS and not last:
                        add_bias(b + 1, n + 2 - STEPS)
                    if n % 2 == 0 and n > 0:
                        take_turned(b, n - 1)
                    if not last and n == 5:
                        statistics(b)
                    if not last and n == 8:
                        normalise(b)
                    for m, use in enumerate(banks.uses):
                        if use[2] + 1 == n and not (first and use in TAIL):
                            spare_use(banks, m, b)
                if last:
                    for m in range(len(LAST), len(banks.uses)):
                        spare_use(banks, m, b)

            def cut(u):
                dve.wait_ge(proj_done.sem, proj_done.at(-1, u + 1))
                high, mid, low = (pieces[:, u % 2, i, u // 2, :] for i in range(3))
                link(-1, dve.tensor_copy(high, proj[:, u % 2]))
                link(-1, dve.tensor_tensor(rest[:], proj[:, u % 2], high, ALU.subtract))
                link(-1, dve.tensor_copy(mid, rest[:]))
                dve.tensor_tensor(low, rest[:], mid, ALU.subtract).then_inc(cut_done.sem, 1)
                dve.wait_ge(cut_done.sem, cut_done.at(-1, u + 1))

            dve.memset(eps[:], EPS).then_inc(consts, 1)
            statistics(-1)
            normalise(-1)
            dve.memset(val[:], 0.0).then_inc(consts, 1)
            dve.wait_ge(consts, 2)
            dve.memset(val[:, :, :, HD:HD + 1], 1.0).then_inc(consts, 1)
            banks = SpareBanks("first")
            dve.wait_ge(early_in, 16 * len(early))
            dve.tensor_copy(ident_bf[:], k["ident"][:]).then_inc(ident_bf_made, 1)
            for m, use in enumerate(banks.uses):
                if use in VALUES:
                    dve.wait_ge(weights_in, 16 * len(later))
                spare_use(banks, m, -1, first=True)
                if use[0] in "QK":
                    cut(2 * use[1] + "QK".index(use[0]))
            for n in range(2):
                add_bias(0, n)
            iteration(0, first=True)
            before = links[0]
            with dve.Fori(1, B - 1) as b:
                iteration(b)
            assert links[0] - before == per_link
            links[0] = before + (B - 2) * per_link
            iteration(B - 1, last=True)

        @block.scalar
        def _(act):
            def exponent(b, n):
                h, t = n // QT, n % QT
                act.wait_ge(biased.sem, biased.at(b, n + 1))
                tile = prob[:, h % 2, t, :]
                act.activation(tile, tile, ACT.Exp, bias=nmax[:, h % 2, t:t + 1], scale=-1.0
                               ).then_inc(exped.sem, 1)

            def take_turned(b, n):
                h, t = n // QT, n % QT
                act.wait_ge(turned.sem, turned.at(b, n + 1))
                act.wait_ge(weighed.sem, weighed.at(b, h // G))
                act.copy(pt[:, h % G, :, t * P:(t + 1) * P],
                         t_bank[n % 2][:, :].rearrange("p (c q) -> p c q", c=QT)).then_inc(evac[0].sem, 1)

            def deviation(b):
                act.wait_ge(stat_done.sem, stat_done.at(b, 1))
                act.activation(std[:], mv[:, :, 1], ACT.Sqrt, bias=eps[:, 0:1]).then_inc(std_done.sem, 1)

            def take_context(b, g):
                act.wait_ge(weighed.sem, weighed.at(b, g + 1))
                act.wait_ge(normed.sem, normed.at(b, g))
                act.copy(osb[:], o_bank[:, :]).then_inc(o_out.sem, 1)

            def iteration(b, first=False, last=False):
                for n in range(STEPS):
                    if n + 1 < STEPS:
                        exponent(b, n + 1)
                    elif not last:
                        exponent(b + 1, 0)
                    if n % 2 == 1:
                        take_turned(b, n - 1)
                    if not last and n == 6:
                        deviation(b)
                    if n == 2 and not first:
                        take_context(b - 1, NG - 1)
                    if n % 16 == 2 and n > 16:
                        take_context(b, n // 16 - 1)
                if last:
                    take_context(b, NG - 1)

            act.wait_ge(consts, 1)
            deviation(-1)
            exponent(0, 0)
            iteration(0, first=True)
            with act.Fori(1, B - 1) as b:
                iteration(b)
            iteration(B - 1, last=True)

        @block.gpsimd
        def _(pool):
            links = [0]
            per_link = [None]

            def link(b, ins):
                links[0] += 1
                ins.then_inc(pool_link, 1)
                pool.wait_ge(pool_link, links[0] if per_link[0] is None else b * per_link[0] + links[0])

            def cut(b, u):
                c, qk = u // 2, u % 2
                pool.wait_ge(proj_done.sem, proj_done.at(b, u + 1))
                if qk == 0:
                    pool.wait_ge(pieces_out[c].sem, pieces_out[c].at(b - 1, 32))
                high, mid, low = (pieces[:, qk, i, c, :] for i in range(3))
                apart(pool, pool_apart)
                link(b, pool.tensor_scalar(high, proj[:, u % 2], 1.0, 0.0, ALU.mult, ALU.add))
                link(b, pool.tensor_tensor(rest[:], proj[:, u % 2], high, ALU.subtract))
                apart(pool, pool_apart)
                link(b, pool.tensor_scalar(mid, rest[:], 1.0, 0.0, ALU.mult, ALU.add))
                pool.tensor_tensor(low, rest[:], mid, ALU.subtract).then_inc(cut_done.sem, 1)
                pool.wait_ge(cut_done.sem, cut_done.at(b, u + 1))

            def copy_values(b, g, first=False):
                if g == 0:
                    pool.wait_ge(vst_done.sem, vst_done.at(b, 2))
                if not first:
                    pool.wait_ge(weighed.sem, weighed.at(b, g + 1))
                apart(pool, pool_apart)
                for t in range(QT):
                    last = pool.tensor_scalar(val[:, t, G * g:G * (g + 1), 0:HD],
                                              vst[:, t, G * HD * g:G * HD * (g + 1)].rearrange("p (j e) -> p j e", j=G),
                                              1.0, 0.0, ALU.mult, ALU.add)
                last.then_inc(val_done.sem, 1)

            def mask_term(b, t, first=False):
                if t == 0:
                    pool.wait_ge(mask_in.sem, mask_in.at(b, 16))
                if not first:
                    pool.wait_ge(scored.sem, scored.at(b, STEPS - QT + t + 1))
                apart(pool, pool_apart)
                pool.tensor_scalar(mterm[:, t, :], mraw[:, t, :], MASKED, 0.0, ALU.mult, ALU.add).then_inc(mask_done.sem, 1)

            def keep_residual(b, first=False):
                pool.wait_ge(xt_done.sem, xt_done.at(b, DC))
                if not first:
                    pool.wait_ge(x1_done.sem, x1_done.at(b, DC))
                apart(pool, pool_apart)
                pool.tensor_scalar(xres[:], xt[:], 1.0, 0.0, ALU.mult, ALU.add).then_inc(res_done.sem, 1)

            def iteration(b):
                for u in range(4):
                    cut(b, u)
                for g in range(NG - 2):
                    copy_values(b, g)
                load_expert(b)
                copy_values(b, NG - 2)
                for t in range(QT):
                    mask_term(b, t)
                copy_values(b, NG - 1)
                keep_residual(b)

            def load_expert(b):
                e = pool.value_load(k["domi"][0:1, bass.ds(b, 1)], min_val=0, max_val=E - 1)
                for l, n in enumerate((1, 3)):
                    for name, dst in (("expert_W", k["expert_w"][:, l, bass.ds(b, 1), :]),
                                      ("expert_b", k["expert_b"][:, l, bass.ds(b, 1)]),
                                      ("domain_emb", k["domain_emb"][:, l, bass.ds(b, 1)])):
                        src = d[f"L{n}_cond_{name}"][bass.ds(e, 1)]
                        src = src.rearrange("e i o -> (e i) o") if name == "expert_W" else src.rearrange("e a -> a e")
                        if name == "expert_W":
                            dst = dst.rearrange("p o a -> p (o a)")
                        for rows in HALVES:
                            pool.dma_start(dst[rows], src).then_inc(k["chosen"], 16)

            for t in range(QT):
                mask_term(-1, t, first=True)
            pool.wait_ge(consts, 3)
            for g in range(NG):
                copy_values(-1, g, first=True)
            keep_residual(-1, first=True)
            before = links[0]
            per_link[0] = 3 * 4
            with pool.Fori(0, B - 1) as b:
                iteration(b)
            assert links[0] - before == per_link[0]
            load_expert(B - 1)


def network_block(nc, d, v, k, x1_dram):
    with ExitStack() as ctx:
        def sb(name, shape, dt=F32):
            return ctx.enter_context(nc.sbuf_tensor(name, shape, dt))

        def sem(name):
            return ctx.enter_context(nc.semaphore(name))

        w1h, w1l = (sb(n, [P, DC, F], F32R) for n in ("w1h", "w1l"))
        w2h, w2l = (sb(n, [P, FC, D], F32R) for n in ("w2h", "w2l"))
        dwh, dwl = (sb(n, [P, 2, DC, 2, A], F32R) for n in ("dwh", "dwl"))
        uwh, uwl = (sb(n, [P, 2, D], F32R) for n in ("uwh", "uwl"))
        ew = sb("ew", [P, 2, 2, A])
        ewh, ewl = (sb(n, [P, 2, 2, A], F32R) for n in ("ewh", "ewl"))
        rotm = sb("rotm", [P, P])
        rotc = sb("rotc", [P, P])
        x1t = sb("x1t", [P, DC, S])
        x1r = sb("x1r", [P, DC, S])
        x2 = sb("x2", [P, DC, S])
        x4 = sb("x4", [P, DC, S])
        wid, wsel = (t[:].rearrange("p i (b a) -> p i b a", a=A) for t in (x2, x4))
        bsel = sb("bsel", [P, 2, B])
        xh = sb("xh", [P, 3, QT, D])
        feat = sb("feat", [P, DC, S])
        hh, hl = (sb(n, [P, DC, S], F32R) for n in ("hh", "hl"))
        NGT = 4
        g = sb("g", [P, NGT, S])
        g_w1 = g[:].rearrange("p (c i) s -> p c (i s)", c=DC)
        g_w2 = g[:].rearrange("p i (f n) -> p (i f) n", n=D)
        gh, gl = (sb(n, [P, FC, S], F32R) for n in ("gh", "gl"))
        x24h, x24l = (sb(n, [P, 2, DC, S], F32R) for n in ("x24h", "x24l"))
        wide = sb("wide", [P, 2, S])
        hid, exo = (sb(n, [P, 2, S], F32R) for n in ("hid", "exo"))
        x3 = sb("x3", [P, 2, DC, S])
        res = sb("res", [P, QT, D])
        stats = sb("stats3", [P, 3, QT, 6])
        mv = sb("mv3", [P, 3, QT, 2])
        std = sb("std3", [P, 3, QT])
        rstd = sb("rstd3", [P, 3, QT])
        eps = sb("eps3", [P, 1])
        bank = [ctx.enter_context(nc.psum_tensor(f"bank{i}", [P, 512], F32)) for i in range(8)]

        counts = []
        AHEAD_SAMPLES = 4

        def count(name, per):
            counts.append(Count(sem(name), per, AHEAD_SAMPLES * per))
            return counts[-1]

        x1t_in, x1r_in, stored = count("x1t_in", 16), count("x1r_in", 16), count("stored", 16)
        to_t = [count(f"to_t{i}", 1) for i in range(3)]
        bn_done = [count(f"bn_done{i}", 1) for i in range(3)]
        stat_done = [count(f"stat_done{i}", 1) for i in range(3)]
        std_done = [count(f"std_done{i}", 1) for i in range(3)]
        rstd_done = [count(f"rstd_done{i}", 1) for i in range(3)]
        norm_done = [count(f"norm_done{i}", 1) for i in range(3)]
        to_f = [count(f"to_f{i}", 1) for i in range(2)]
        feat_done = [count(f"feat_done{i}", DC) for i in range(2)]
        hh_done, hl_done = count("hh_done", DC), count("hl_done", DC)
        w1_done = count("w1_done", FC)
        g_done, gh_done, gl_done = count("g_done", FC), count("gh_done", FC), count("gl_done", FC)
        w2_done = count("w2_done", DC)
        x2_done = count("x2_done", DC)
        rotc_done, rotm_done, rotated = count("rotc_done", 1), count("rotm_done", 1), count("rotated", 1)
        x4_done = count("x4_done", DC)
        high_done = [count(f"high_done{i}", DC) for i in range(2)]
        low_done = [count(f"low_done{i}", DC) for i in range(2)]
        down_done = [count(f"down_done{i}", 1) for i in range(2)]
        gelu_done = [count(f"gelu_done{i}", 2) for i in range(2)]
        hid_done = [count(f"hid_done{i}", 1) for i in range(2)]
        ew_done = [count(f"ew_done{i}", 3) for i in range(2)]
        expert_done = [count(f"expert_done{i}", 1) for i in range(2)]
        exw_done = [count(f"exw_done{i}", 2) for i in range(2)]
        exo_done = [count(f"exo_done{i}", 1) for i in range(2)]
        up_done = [count(f"up_done{i}", 1) for i in range(2)]
        x3_done = [count(f"x3_done{i}", DC) for i in range(2)]
        scaled, out_made = count("scaled", 1), count("out_made", 1)
        eps_set = sem("eps_set")
        pool_link, experts_made = sem("pool_link3"), sem("experts_made")
        w1_in, w2_in = sem("w1_in"), sem("w2_in")
        high_w, low_w = sem("high_w"), sem("low_w")
        dve_apart = sem("dve_apart3")
        pool_apart = sem("pool_apart3")
        sp_apart = sem("sp_apart3")
        block = ctx.enter_context(nc.Block())
        NORM_LAG = (-1, 2, 3)

        def on(j, lag):
            return not isinstance(j, int) or 0 <= j - lag < B

        @block.sync
        def _(sp):
            for c in counts:
                sp.sem_inc(c.sem, c.ahead)

            def load(j, buf, arrived, used):
                sp.wait_ge(used.sem, used.at(j - 1, used.per))
                apart(sp, sp_apart)
                sp.dma_start(buf[:], x1_dram[bass.ds(j, 1)].rearrange("o p c t -> (o p) c t")
                             ).then_inc(arrived.sem, 16)

            def iteration(j):
                if on(j, -2):
                    load(j + 2, x1t, x1t_in, to_t[0])
                if on(j, 0):
                    load(j, x1r, x1r_in, x2_done)
                if on(j, 3):
                    sp.wait_ge(out_made.sem, out_made.at(j - 3, 1))
                    apart(sp, sp_apart)
                    sp.dma_start(v["out"][:, bass.ds(j - 3, 1)].rearrange("p o t k -> p (o t) k"), res[:]
                                 ).then_inc(stored.sem, 16)

            sp.dma_start(g_w1, v["W1"]).then_inc(w1_in, 16)
            for j in (-2, -1):
                iteration(j)
                if j == -2:
                    sp.wait_ge(low_w, 3)
                    sp.dma_start(g_w2, v["W2"]).then_inc(w2_in, 16)
            for j in range(0, 3):
                iteration(j)
            with sp.Fori(3, B - 2) as j:
                iteration(j)
            for j in range(B - 2, B + 3):
                iteration(j)
            sp.wait_ge(stored.sem, stored.at(B - 1, 16))

        @block.tensor
        def _(pe):
            ident = k["ident"]
            T_BANK = (6, 2, 4)

            def to_tokens(j, i, src, ready):
                pe.wait_ge(ready.sem, ready.at(j, ready.per))
                if i == 0:
                    pe.wait_ge(x3_done[1].sem, x3_done[1].at(j - 4, DC))
                elif i == 1:
                    pe.wait_ge(feat_done[0].sem, feat_done[0].at(j + 2, DC))
                else:
                    pe.wait_ge(x3_done[0].sem, x3_done[0].at(j + 1, DC))
                for t in range(QT):
                    for c in range(DC):
                        at = (t % 2) * D + c * P
                        last = pe.transpose(bank[T_BANK[i] + t // 2][:, at:at + P], src[:, c, t * P:(t + 1) * P],
                                            ident[:])
                last.then_inc(to_t[i].sem, 1)

            def to_features(j, i):
                pe.wait_ge(norm_done[i].sem, norm_done[i].at(j, 1))
                if i == 0:
                    pe.wait_ge(feat_done[1].sem, feat_done[1].at(j - 3, DC))
                for c in range(DC):
                    for t in range(QT):
                        last = pe.transpose(bank[2 + c][:, t * P:(t + 1) * P], xh[:, i, t, c * P:(c + 1) * P],
                                            ident[:])
                last.then_inc(to_f[i].sem, 1)

            def first_layer(j, f):
                if f == 0:
                    pe.wait_ge(hl_done.sem, hl_done.at(j, DC))
                    pe.wait_ge(hh_done.sem, hh_done.at(j, DC))
                if f < 2:
                    pe.wait_ge(x2_done.sem, x2_done.at(j - 1, f + 1))
                else:
                    pe.wait_ge(g_done.sem, g_done.at(j, f - 1))
                col = slice(f * P, (f + 1) * P)
                parts = [(w, c, h) for c in range(DC) for w, h in ((w1h, hh), (w1h, hl), (w1l, hh))]
                for n, (w, c, h) in enumerate(parts):
                    last = pe.matmul(bank[f % 2][:, :], w[:, c, col], h[:, c, :], start=(n == 0),
                                     stop=(n == len(parts) - 1))
                last.then_inc(w1_done.sem, 1)

            def second_layer(j, n):
                c, q = n // 4, n % 4
                parts = [(w, f, gh) for f in range(FC) for w in (w2h, w2l)] + [(w2h, f, gl) for f in range(FC)]
                if q == 0:
                    pe.wait_ge(g_done.sem, g_done.at(j, FC - 1 + c))
                size = len(parts) // 4
                for m in range(q * size, (q + 1) * size):
                    w, f, gx = parts[m]
                    if c == 0 and w is not w2l:
                        done = gh_done if gx is gh else gl_done
                        pe.wait_ge(done.sem, done.at(j, f + 1))
                    last = pe.matmul(bank[c][:, :], w[:, f, c * P:(c + 1) * P], gx[:, f, :], start=(m == 0),
                                     stop=(m == len(parts) - 1))
                if q == 3:
                    last.then_inc(w2_done.sem, 1)

            def rotate(j):
                pe.wait_ge(feat_done[1].sem, feat_done[1].at(j, DC))
                pe.wait_ge(rotm_done.sem, rotm_done.at(j, 1))
                pe.wait_ge(norm_done[2].sem, norm_done[2].at(j - 1, 1))
                for c in range(DC):
                    last = pe.matmul(bank[4 + c][:, :], rotm[:], feat[:, c, :], start=True, stop=True)
                last.then_inc(rotated.sem, 1)

            def down(j, l):
                pe.wait_ge(low_done[l].sem, low_done[l].at(j, DC))
                pe.wait_ge(high_done[l].sem, high_done[l].at(j, DC))
                pe.wait_ge(norm_done[0].sem, norm_done[0].at(j + (l + 2), 1))
                parts = [(w, c, x) for c in range(DC) for w, x in ((dwh, x24h), (dwh, x24l), (dwl, x24h))]
                for n, (w, c, x) in enumerate(parts):
                    last = pe.matmul(bank[6 + l][:, :], w[:, l, c].rearrange("p r a -> p (r a)"), x[:, l, c, :],
                                     start=(n == 0), stop=(n == len(parts) - 1))
                last.then_inc(down_done[l].sem, 1)

            def expert(j, l):
                pe.wait_ge(hid_done[l].sem, hid_done[l].at(j, 1))
                pe.wait_ge(ew_done[l].sem, ew_done[l].at(j, 3))
                for n, w in enumerate((ewh, ewl)):
                    last = pe.matmul(bank[6 + l][:, :], w[:, l].rearrange("p r a -> p (r a)"), hid[:, l, :],
                                     start=(n == 0), stop=(n == 1))
                last.then_inc(expert_done[l].sem, 1)

            def up(j, l):
                pe.wait_ge(exo_done[l].sem, exo_done[l].at(j, 1))
                if l == 0:
                    pe.wait_ge(x4_done.sem, x4_done.at(j - 1, DC))
                else:
                    pe.wait_ge(exo_done[0].sem, exo_done[0].at(j + 1, 1))
                for c in range(DC):
                    for n, w in enumerate((uwh, uwl)):
                        last = pe.matmul(bank[(4, 6)[l] + c][:, :], w[:, l, c * P:(c + 1) * P], exo[:, l, :],
                                         start=(n == 0), stop=(n == 1))
                last.then_inc(up_done[l].sem, 1)

            def iteration(j):
                if on(j, 2):
                    to_tokens(j - 2, 1, x3[:, 0], x3_done[0])
                for n in range(2 * FC):
                    if on(j, 0):
                        if n < FC:
                            first_layer(j, n)
                        else:
                            second_layer(j, n - FC)
                    if n == 0 and on(j, 3):
                        to_tokens(j - 3, 2, x3[:, 1], x3_done[1])
                    if n == 1 and on(j, -1):
                        to_tokens(j + 1, 0, x1t, x1t_in)
                    if n == 7 and on(j, 2):
                        to_features(j - 2, 1)
                    if n == 9 and on(j, 2):
                        rotate(j - 2)
                    if n == 9 and on(j, -1):
                        to_features(j + 1, 0)
                    for l in range(2):
                        if on(j, 1 + l):
                            if n == 11:
                                down(j - (1 + l), l)
                            if n == 13:
                                expert(j - (1 + l), l)
                            if n == 14 + l:
                                up(j - (1 + l), l)

            iteration(-1)
            pe.wait_ge(high_w, 4)
            pe.wait_ge(low_w, 4)
            for j in range(0, 3):
                iteration(j)
            with pe.Fori(3, B - 1) as j:
                iteration(j)
            for j in range(B - 1, B + 3):
                iteration(j)

        @block.vector
        def _(dve):
            def gelu_high(j, f):
                dve.wait_ge(g_done.sem, g_done.at(j, f + 1))
                if f == 0:
                    dve.wait_ge(w2_done.sem, w2_done.at(j - 1, DC))
                dve.wait_ge(gl_done.sem, gl_done.at(j - 1, f + 1))
                dve.tensor_copy(gh[:, f], g[:, f % NGT]).then_inc(gh_done.sem, 1)

            def low_part(j, l, src, ready):
                dve.wait_ge(ready.sem, ready.at(j, DC))
                for c in range(DC):
                    dve.wait_ge(high_done[l].sem, high_done[l].at(j, c + 1))
                    dve.tensor_tensor(x24l[:, l, c], src[:, c], x24h[:, l, c], ALU.subtract
                                      ).then_inc(low_done[l].sem, 1)

            def take_rotated(j):
                dve.wait_ge(rotated.sem, rotated.at(j, 1))
                for c in range(DC):
                    dve.tensor_copy(x4[:, c], bank[4 + c][:, :]).then_inc(x4_done.sem, 1)

            def hidden_low(j, l):
                dve.wait_ge(gelu_done[l].sem, gelu_done[l].at(j, 2))
                dve.tensor_tensor(hid[A:P, l], wide[A:P, l], hid[A:P, l], ALU.subtract
                                  ).then_inc(hid_done[l].sem, 1)

            def expert_low(j, l):
                dve.wait_ge(exw_done[l].sem, exw_done[l].at(j, 2))
                dve.tensor_tensor(exo[A:P, l], wide[A:P, l], exo[A:P, l], ALU.subtract
                                  ).then_inc(exo_done[l].sem, 1)

            def add(ready, value, pbank, c, bias, resid, dst, done):
                dve.wait_ge(ready.sem, value)
                dve.scalar_tensor_tensor(dst[:, c], bank[pbank][:, :], bias[:, c:c + 1], resid[:, c],
                                         ALU.add, ALU.add).then_inc(done.sem, 1)

            def take_up(j, l):
                for c in range(DC):
                    add(up_done[l], up_done[l].at(j, 1), (4, 6)[l] + c, c, k["up_b"][:, l], (x2, x4)[l], x3[:, l],
                        x3_done[l])

            def take_network(j, c):
                if c == 0:
                    dve.wait_ge(x1r_in.sem, x1r_in.at(j, 16))
                    dve.wait_ge(x3_done[0].sem, x3_done[0].at(j - 1, DC))
                add(w2_done, w2_done.at(j, c + 1), c, c, k["b2"], x1r, x2, x2_done)

            def tile(i, t):
                return bank[(6, 2, 4)[i] + t // 2][:, (t % 2) * D:(t % 2 + 1) * D]

            def statistics(j, i):
                dve.wait_ge(to_t[i].sem, to_t[i].at(j, 1))
                for t in range(QT):
                    last = dve.bn_stats(stats[:, i, t], tile(i, t))
                last.then_inc(bn_done[i].sem, 1)
                dve.wait_ge(bn_done[i].sem, bn_done[i].at(j, 1))
                apart(dve, dve_apart)
                for t in range(QT):
                    last = dve.bn_aggr(mv[:, i, t], stats[:, i, t])
                last.then_inc(stat_done[i].sem, 1)

            def normalise(j, i):
                dve.wait_ge(std_done[i].sem, std_done[i].at(j, 1))
                dve.reciprocal(rstd[:, i], std[:, i]).then_inc(rstd_done[i].sem, 1)
                dve.wait_ge(rstd_done[i].sem, rstd_done[i].at(j, 1))
                if i == 2:
                    dve.wait_ge(scaled.sem, scaled.at(j - 1, 1))
                for t in range(QT):
                    last = dve.tensor_scalar(xh[:, i, t], tile(i, t), mv[:, i, t, 0:1], rstd[:, i, t:t + 1],
                                             ALU.subtract, ALU.mult)
                last.then_inc(norm_done[i].sem, 1)

            def rotation_matrix(j):
                dve.wait_ge(rotated.sem, rotated.at(j - 1, 1))
                dve.tensor_scalar(rotc[:], k["ident"][:], k["rot"][:, 0, bass.ds(j, 1)], None, ALU.mult
                                  ).then_inc(rotc_done.sem, 1)
                dve.wait_ge(rotc_done.sem, rotc_done.at(j, 1))
                dve.scalar_tensor_tensor(rotm[:], k["beside"][:], k["rot"][:, 1, bass.ds(j, 1)], rotc[:],
                                         ALU.mult, ALU.add).then_inc(rotm_done.sem, 1)

            def iteration(j):
                if on(j, 2):
                    statistics(j - 2, 1)
                for n in range(2 * FC):
                    if n < FC and on(j, 0):
                        gelu_high(j, n)
                    if n == 0 and on(j, 3):
                        statistics(j - 3, 2)
                    if n == 1 and on(j, -1):
                        statistics(j + 1, 0)
                    if n == 2 and on(j, 1):
                        low_part(j - 1, 0, x2, x2_done)
                    if n == 2 and on(j, 2):
                        rotation_matrix(j - 2)
                    for m, i in ((3, 1), (4, 2), (6, 0)):
                        if n == m and on(j, NORM_LAG[i]):
                            normalise(j - NORM_LAG[i], i)
                    if n == 9 and on(j, 2):
                        take_rotated(j - 2)
                        low_part(j - 2, 1, x4, x4_done)
                    for l in range(2):
                        if on(j, 1 + l):
                            if n == 11:
                                hidden_low(j - (1 + l), l)
                            if n == 13:
                                expert_low(j - (1 + l), l)
                if on(j, 1):
                    take_up(j - 1, 0)
                if on(j, 0):
                    take_network(j, 0)
                if on(j, 2):
                    take_up(j - 2, 1)
                if on(j, 0):
                    take_network(j, 1)

            dve.memset(eps[:], EPS).then_inc(eps_set, 1)
            dve.wait_ge(k["late_in"], 16 * LATE_LOADS)
            dve.wait_ge(high_w, 2)
            for l in range(2):
                for r in range(2):
                    last = dve.tensor_tensor(dwl[:, l, :, r], k["down_w"][:, l], dwh[:, l, :, r], ALU.subtract)
            last.then_inc(low_w, 1)
            dve.tensor_tensor(uwl[:], k["up_w"][:], uwh[:], ALU.subtract).then_inc(low_w, 1)
            dve.wait_ge(w1_in, 16)
            dve.wait_ge(high_w, 3)
            dve.tensor_tensor(w1l[:], g_w1, w1h[:], ALU.subtract).then_inc(low_w, 1)
            dve.wait_ge(w2_in, 16)
            dve.wait_ge(high_w, 4)
            dve.tensor_tensor(w2l[:], g_w2, w2h[:], ALU.subtract).then_inc(low_w, 1)
            dve.wait_ge(experts_made, 1)
            for j in range(-1, 3):
                iteration(j)
            with dve.Fori(3, B - 1) as j:
                iteration(j)
            for j in range(B - 1, B + 3):
                iteration(j)

        @block.scalar
        def _(act):
            def gelu(j, f):
                act.wait_ge(w1_done.sem, w1_done.at(j, f + 1))
                if f >= NGT:
                    act.wait_ge(gl_done.sem, gl_done.at(j, f - NGT + 1))
                    act.wait_ge(gh_done.sem, gh_done.at(j, f - NGT + 1))
                else:
                    act.wait_ge(gl_done.sem, gl_done.at(j - 1, f + NGT + 1))
                act.activation(g[:, f % NGT], bank[f % 2][:, :], ACT.Gelu_apprx_sigmoid, bias=k["b1"][:, f:f + 1]
                               ).then_inc(g_done.sem, 1)

            def high_part(j, l):
                src, ready = ((x2, x2_done), (x4, x4_done))[l]
                for c in range(DC):
                    act.wait_ge(ready.sem, ready.at(j, c + 1))
                    act.copy(x24h[:, l, c], src[:, c]).then_inc(high_done[l].sem, 1)

            def hidden(j, l):
                act.wait_ge(down_done[l].sem, down_done[l].at(j, 1))
                for dst in (hid, wide):
                    act.activation(dst[:, l], bank[6 + l][:, :], ACT.Gelu, bias=k["down_b"][:, l:l + 1]
                                   ).then_inc(gelu_done[l].sem, 1)

            def expert_high(j, l):
                act.wait_ge(expert_done[l].sem, expert_done[l].at(j, 1))
                act.wait_ge(exo_done[l].sem, exo_done[l].at(j - 1, 1))
                for dst in (exo, wide):
                    act.activation(dst[:, l], bank[6 + l][:, :], ACT.Identity,
                                   bias=k["expert_b"][:, l, bass.ds(j, 1)]).then_inc(exw_done[l].sem, 1)

            def deviation(j, i):
                act.wait_ge(stat_done[i].sem, stat_done[i].at(j, 1))
                act.activation(std[:, i], mv[:, i, :, 1], ACT.Sqrt, bias=eps[:, 0:1]).then_inc(std_done[i].sem, 1)

            def network_input(j):
                act.wait_ge(to_f[0].sem, to_f[0].at(j, 1))
                act.wait_ge(rotated.sem, rotated.at(j - 3, 1))
                for dst, done in ((hh, hh_done), (feat, feat_done[0])):
                    for c in range(DC):
                        act.activation(dst[:, c], bank[2 + c][:, :], ACT.Identity, bias=k["beta2"][:, c:c + 1],
                                       scale=k["g2"][:, c:c + 1]).then_inc(done.sem, 1)

            def rotation_input(j):
                act.wait_ge(to_f[1].sem, to_f[1].at(j, 1))
                act.wait_ge(hl_done.sem, hl_done.at(j + 2, DC))
                for c in range(DC):
                    act.activation(feat[:, c], bank[2 + c][:, :], ACT.Identity, bias=k["beta_f"][:, c:c + 1],
                                   scale=k["gamma_f"][:, c:c + 1]).then_inc(feat_done[1].sem, 1)

            def iteration(j):
                for n in range(2 * FC):
                    if n < FC and on(j, 0):
                        gelu(j, n)
                    if n == 1 and on(j, 1):
                        high_part(j - 1, 0)
                    if n == 3:
                        for i in (1, 2, 0):
                            if on(j, NORM_LAG[i]):
                                deviation(j - NORM_LAG[i], i)
                    if n == 7 and on(j, 2):
                        rotation_input(j - 2)
                    if n == 9 and on(j, 2):
                        high_part(j - 2, 1)
                    if n == 9 and on(j, -1):
                        network_input(j + 1)
                    for l in range(2):
                        if on(j, 1 + l):
                            if n == 11:
                                hidden(j - (1 + l), l)
                            if n == 13:
                                expert_high(j - (1 + l), l)

            act.wait_ge(eps_set, 1)
            act.wait_ge(k["late_in"], 16 * LATE_LOADS)
            for l in range(2):
                for r in range(2):
                    last = act.copy(dwh[:, l, :, r], k["down_w"][:, l])
            last.then_inc(high_w, 1)
            act.copy(uwh[:], k["up_w"][:]).then_inc(high_w, 1)
            act.wait_ge(w1_in, 16)
            act.copy(w1h[:], g_w1).then_inc(high_w, 1)
            act.wait_ge(w2_in, 16)
            act.copy(w2h[:], g_w2).then_inc(high_w, 1)
            act.wait_ge(experts_made, 1)
            for j in range(-1, 3):
                iteration(j)
            with act.Fori(3, B - 1) as j:
                iteration(j)
            for j in range(B - 1, B + 3):
                iteration(j)

        @block.gpsimd
        def _(pool):
            def gelu_low(j, f):
                pool.wait_ge(gh_done.sem, gh_done.at(j, f + 1))
                if f == 0:
                    pool.wait_ge(w2_done.sem, w2_done.at(j - 1, DC))
                pool.tensor_tensor(gl[:, f], g[:, f % NGT], gh[:, f], ALU.subtract).then_inc(gl_done.sem, 1)

            def network_low(j):
                for c in range(DC):
                    pool.wait_ge(feat_done[0].sem, feat_done[0].at(j, c + 1))
                    pool.tensor_tensor(hl[:, c], feat[:, c], hh[:, c], ALU.subtract).then_inc(hl_done.sem, 1)

            def expert_parts(j, l):
                pool.wait_ge(expert_done[l].sem, expert_done[l].at(j - 1, 1))
                apart(pool, pool_apart)
                pool.tensor_copy(ew[:, l], k["expert_w"][:, l, bass.ds(j, 1), :].to_broadcast([P, 2, A])
                                 ).then_inc(ew_done[l].sem, 1)
                pool.wait_ge(ew_done[l].sem, ew_done[l].at(j, 1))
                apart(pool, pool_apart)
                pool.tensor_copy(ewh[:, l], ew[:, l]).then_inc(ew_done[l].sem, 1)
                pool.wait_ge(ew_done[l].sem, ew_done[l].at(j, 2))
                pool.tensor_tensor(ewl[:, l], ew[:, l], ewh[:, l], ALU.subtract).then_inc(ew_done[l].sem, 1)

            def output(j):
                pool.wait_ge(norm_done[2].sem, norm_done[2].at(j, 1))
                pool.wait_ge(stored.sem, stored.at(j - 1, 16))
                pool.tensor_tensor(res[:], xh[:, 2], k["gamma"][:, None, :].to_broadcast([P, QT, D]), ALU.mult
                                   ).then_inc(scaled.sem, 1)
                pool.wait_ge(scaled.sem, scaled.at(j, 1))
                pool.tensor_tensor(res[:], res[:], k["beta"][:, None, :].to_broadcast([P, QT, D]), ALU.add
                                   ).then_inc(out_made.sem, 1)

            def iteration(j):
                for n in range(2 * FC):
                    if n == 0:
                        for l in range(2):
                            if on(j, 1 + l):
                                expert_parts(j - (1 + l), l)
                    if n < FC and on(j, 0):
                        gelu_low(j, n)
                    if n == 9 and on(j, -1):
                        network_low(j + 1)
                    if n == 8 and on(j, 3):
                        output(j - 3)

            pool.wait_ge(k["chosen"], 16 * 12 * B)
            pool.wait_ge(k["late_in"], 16 * LATE_LOADS)
            domf = k["domf"]

            def link(n, ins):
                ins.then_inc(pool_link, 1)
                pool.wait_ge(pool_link, n)

            for n, rows in enumerate(HALVES):
                unit = k["ident"][rows, None, None, rows].to_broadcast([A, 2, B, A])
                link(n + 1, pool.tensor_tensor(wid[rows], unit,
                                               domf[rows, None, 3, :, None].to_broadcast([A, 2, B, A]), ALU.mult))
            link(3, pool.tensor_tensor(wsel[:], k["expert_w"][:], domf[:, None, 2, :, None].to_broadcast([P, 2, B, A]),
                                       ALU.mult))
            link(4, pool.tensor_tensor(k["expert_w"][:], wsel[:], wid[:], ALU.add))
            link(5, pool.tensor_tensor(bsel[:], k["expert_b"][:], domf[:, None, 2].to_broadcast([P, 2, B]), ALU.mult))
            pool.tensor_tensor(k["expert_b"][:], bsel[:], k["domain_emb"][:], ALU.add).then_inc(experts_made, 1)
            for j in range(-1, 3):
                iteration(j)
            with pool.Fori(3, B - 1) as j:
                iteration(j)
            for j in range(B - 1, B + 3):
                iteration(j)


def build(nc, d):
    v = load_layouts(d)
    x1_dram = nc.dram_tensor("x1_dram", [B, P, DC, S], F32, kind="Internal").ap()
    pieces_dram = nc.dram_tensor("pieces_dram", [2, DC, 3, P, S], BF16, kind="Internal").ap()
    pieces_dram = pieces_dram.rearrange("q c i p t -> p q c i t")
    with ExitStack() as ctx:
        def sb(name, shape, dt=F32):
            return ctx.enter_context(nc.sbuf_tensor(name, shape, dt))

        k = dict(
            ident=sb("ident", [P, P]),
            b1=sb("b1", [P, FC]), b2=sb("b2", [P, DC]), g2=sb("g2", [P, DC]), beta2=sb("beta2", [P, DC]),
            down_w=sb("down_w", [P, 2, DC, A]), down_b=sb("down_b", [P, 2]),
            up_w=sb("up_w", [P, 2, D]), up_b=sb("up_b", [P, 2, DC]),
            gamma=sb("gamma", [P, D]), beta=sb("beta", [P, D]), gamma_f=sb("gamma_f", [P, DC]), beta_f=sb("beta_f", [P, DC]),
            beside=sb("beside", [P, P]),
            expert_w=sb("expert_w", [P, 2, B, A]), expert_b=sb("expert_b", [P, 2, B]),
            domain_emb=sb("domain_emb", [P, 2, B]), domf=sb("domf", [P, 4, B]), domi=sb("domi", [P, B], I32),
            late_in=ctx.enter_context(nc.semaphore("late_in")), chosen=ctx.enter_context(nc.semaphore("chosen")),
            ada=sb("ada", [P, 4, B]), trig=sb("trig", [P, 6, B]), rot=sb("rot", [P, 2, B]),
        )
        attention_block(nc, d, v, k, x1_dram, pieces_dram)
        network_block(nc, d, v, k, x1_dram)


def kernel(**inputs):
    import concourse.bacc as bacc
    from concourse.bass_utils import run_bass_kernel_spmd

    nc = bacc.Bacc("TRN2", target_bir_lowering=False, num_devices=1)
    arrays = {}
    for name in INPUTS:
        a = np.asarray(inputs[name])
        if name.endswith("down_W") or name.endswith("up_W"):
            a = a.T
        elif name.endswith("expert_W"):
            a = a.transpose(0, 2, 1)
        elif name.endswith("up_b") or name.startswith("L1_cond_ln") or name in ["L0_cond_" + w for w in BY_FEATURE]:
            a = a.reshape(-1, P).T
        arrays[name] = np.ascontiguousarray(a)
    arrays["ident"] = np.eye(P, dtype=np.float32)
    place = np.arange(P) % 4
    arrays["pairs"] = np.stack([place < 2, place >= 2], 1).astype(np.float32)
    beside = np.zeros((P, P), np.float32)
    beside[np.arange(1, P, 2), np.arange(0, P, 2)] = 1.0
    beside[np.arange(0, P, 2), np.arange(1, P, 2)] = -1.0
    arrays["beside"] = beside
    half = D // 2
    freq = np.exp(np.arange(half, dtype=np.float32) * np.float32(-np.log(10000.0) / (half - 1)))
    arrays["freq"] = freq.astype(np.float32).reshape(P, 1)
    d = {name: nc.dram_tensor("in_" + name, a.shape, mybir.dt.from_np(a.dtype), kind="ExternalInput").ap()
         for name, a in arrays.items()}
    d["out"] = nc.dram_tensor("out", (B, S, D), F32, kind="ExternalOutput").ap()
    build(nc, d)
    r = run_bass_kernel_spmd(nc, [{"in_" + n: a for n, a in arrays.items()}], core_ids=[0])
    return r.results[0]["out"]
```

```python
from contextlib import ExitStack

import numpy as np

import concourse.bass as bass
from concourse import mybir

F32 = mybir.dt.float32
BF16 = mybir.dt.bfloat16
F32R = mybir.dt.float32r
I32 = mybir.dt.int32
U8 = mybir.dt.uint8
ALU = mybir.AluOpType
ACT = mybir.ActivationFunctionType

P = 128
B, S, D, H, HD, F = 8, 512, 256, 16, 16, 1024
A, E = 64, 16
QT = S // P
DC = D // P
FC = F // P
HC = H // DC
G = 4
NG = H // G
VW = 32
STEPS = H * QT
EPS = 1e-5
PE_MASKED = (0, 1, 2, 3, 4, 6, 10, 11)
POOL_MASKED = [h for h in range(H) if h not in PE_MASKED]
NB = 4
MASKED = -1e30
QPIECE = [0, 0, 1, 0, 2, 1, 1, 2]
KPIECE = [0, 1, 0, 2, 0, 1, 2, 1]
NP8 = len(QPIECE)

INPUTS = [
    "x", "itok_B_34_63", "fside_Bx16xSxS_0", "itok_B_0_15", "condB_theta", "condB_phi", "mask_Bx1xSxS_bk0",
    "L0_cond_W_ada", "L0_cond_b_ada", "L0_cond_Wq", "L0_cond_bq", "L0_cond_Wk", "L0_cond_bk", "L0_cond_Wv",
    "L0_cond_bv", "L0_cond_Wo", "L0_cond_bo", "L0_cond_W1", "L0_cond_b1", "L0_cond_W2", "L0_cond_b2",
    "L0_cond_g2", "L0_cond_beta2",
] + [f"L{n}_cond_{w}" for n in (1, 3) for w in (
    "down_W", "down_b", "up_W", "up_b", "expert_W", "expert_b", "domain_emb", "ln_gamma", "ln_beta")]

BY_FEATURE = ("b_ada", "bq", "bk", "bo", "b1", "b2", "g2", "beta2")


LATE_LOADS = 21
HALVES = (slice(0, A), slice(A, P))


def apart(eng, sem):
    eng.sem_inc(sem, 1)


class Count:

    def __init__(self, sem, per, ahead):
        self.sem, self.per, self.ahead = sem, per, ahead

    def at(self, b, k):
        if isinstance(b, int):
            b = min(b, B - 1)
        return b * self.per + (self.ahead + k)


def load_layouts(d):
    v = dict(
        x=d["x"].rearrange("b (t p) d -> p b t d", p=P),
        bias=d["fside_Bx16xSxS_0"].rearrange("b h (t p) k -> p (b h) t k", p=P),
        mask=d["mask_Bx1xSxS_bk0"].rearrange("b o (t p) k -> p (b o) t k", p=P),
        out=d["out"].rearrange("b (t p) d -> p b t d", p=P),
    )
    for w in ("W_ada", "Wq", "Wk", "Wv", "Wo", "W1", "W2"):
        v[w] = d["L0_cond_" + w].rearrange("(c p) n -> p c n", p=P)
    for w in BY_FEATURE:
        v[w] = d["L0_cond_" + w]
    return v


def setup_programs(nc, ctx, d, v, k, bank, w_ada):
    def sb(name, shape, dt=F32):
        return ctx.enter_context(nc.sbuf_tensor(name, shape, dt))

    def sem(name):
        return ctx.enter_context(nc.semaphore(name))

    b_ada = sb("b_ada", [P, 4])
    freq = sb("freq", [P, 1])
    tok = sb("tok", [P, B], I32)
    tokf = sb("tokf", [P, 4, B])
    arg = sb("arg", [P, 6, B])
    turns = sb("turns", [P, 6, B])
    quarter = sb("quarter", [P, 6, B])
    emb = sb("emb", [P, DC, B])
    dom = sb("dom", [P, B], I32)
    pairs = sb("pairs", [P, 2])
    rotp = sb("rotp", [P, 2, B])
    ada_ps = bank[:, 0:4 * B].rearrange("p (c b) -> p c b", b=B)
    cond_in = sem("cond_in")
    dve_step = sem("dve_step")
    sines = sem("sines")
    embedded = sem("embedded")
    ada_done = sem("ada_done")
    conds = [
        (tok[:], d["itok_B_34_63"].partition_broadcast(P)), (dom[:], d["itok_B_0_15"].partition_broadcast(P)),
        (arg[:, 2], d["condB_theta"].partition_broadcast(P)), (arg[:, 3], d["condB_theta"].partition_broadcast(P)),
        (arg[:, 4], d["condB_phi"].partition_broadcast(P)), (arg[:, 5], d["condB_phi"].partition_broadcast(P)),
        (freq[:], d["freq"]), (pairs[:], d["pairs"]), (w_ada, v["W_ada"]), (b_ada[:], v["b_ada"]),
    ]

    def load(sp):
        for dst, src in conds:
            sp.dma_start(dst, src).then_inc(cond_in, 16)

    dve = nc.vector
    n = [0]

    def link(ins):
        n[0] += 1
        ins.then_inc(dve_step, 1)
        dve.wait_ge(dve_step, n[0])

    def angles(dve):
        dve.memset(quarter[:], 0.0).then_inc(dve_step, 1)
        n[0] += 1
        dve.wait_ge(dve_step, n[0])
        for i in (1, 3, 5):
            link(dve.memset(quarter[:, i], 0.25))
        dve.wait_ge(cond_in, 16 * len(conds))
        link(dve.tensor_copy(tokf[:, 0], tok[:]))
        link(dve.tensor_scalar(tokf[:, 1], tokf[:, 0], 0.01, None, ALU.mult))
        link(dve.tensor_copy(tokf[:, 2], tokf[:, 0]))
        for part in (64.0, 32.0, 4.0):
            link(dve.scalar_tensor_tensor(tokf[:, 3], tokf[:, 1], -part, tokf[:, 2], ALU.mult, ALU.add))
            link(dve.tensor_copy(tokf[:, 2], tokf[:, 3]))
        link(dve.scalar_tensor_tensor(tokf[:, 3], tokf[:, 2], 0.01, tokf[:, 1], ALU.mult, ALU.add))
        link(dve.tensor_scalar(tokf[:, 1], tokf[:, 3], 4000.0, None, ALU.mult))
        link(dve.tensor_scalar(arg[:, 0], tokf[:, 1], freq[:, 0:1], None, ALU.mult))
        link(dve.tensor_scalar(arg[:, 1], tokf[:, 1], freq[:, 0:1], None, ALU.mult))
        link(dve.scalar_tensor_tensor(turns[:], arg[:], 1.0 / (2.0 * np.pi), quarter[:], ALU.mult, ALU.add))
        link(dve.tensor_scalar(turns[:], turns[:], 12582912.0, None, ALU.add))
        link(dve.tensor_scalar(turns[:], turns[:], -12582912.0, None, ALU.add))
        for part in TWO_PI_PARTS:
            link(dve.scalar_tensor_tensor(arg[:], turns[:], -part, arg[:], ALU.mult, ALU.add))
        link(dve.scalar_tensor_tensor(arg[:], quarter[:], 2.0 * np.pi, arg[:], ALU.mult, ALU.add))
        dve.tensor_scalar(arg[:], arg[:], 3.1415925, -3.1415925, ALU.min, ALU.max).then_inc(sines, 1)

    def domains(dve):
        link(dve.tensor_copy(k["domf"][:, 0], dom[:]))
        link(dve.tensor_scalar(k["domf"][:, 1], k["domf"][:, 0], 0.0, E - 1.0, ALU.max, ALU.min))
        link(dve.tensor_copy(k["domi"][:], k["domf"][:, 1]))
        link(dve.tensor_tensor(k["domf"][:, 2], k["domf"][:, 0], k["domf"][:, 1], ALU.is_equal))
        link(dve.tensor_scalar(k["domf"][:, 3], k["domf"][:, 2], -1.0, 1.0, ALU.mult, ALU.add))

    def rotations(dve):
        dve.wait_ge(sines, 2)
        for i in range(2):
            link(dve.tensor_scalar(rotp[:, i], k["trig"][:, 5 - i], pairs[:, 1:2], None, ALU.mult))
            link(dve.scalar_tensor_tensor(k["rot"][:, i], k["trig"][:, 3 - i], pairs[:, 0:1], rotp[:, i],
                                          ALU.mult, ALU.add))

    def modulation(dve):
        dve.wait_ge(ada_done, 1)
        for c in range(4):
            link(dve.tensor_scalar(k["ada"][:, c], ada_ps[:, c], b_ada[:, c:c + 1], 1.0 if c < DC else 0.0,
                                   ALU.add, ALU.add))

    def sines_of(act):
        act.wait_ge(sines, 1)
        act.activation(k["trig"][:], arg[:], ACT.Sin).then_inc(sines, 1)
        act.wait_ge(sines, 2)
        act.activation(emb[:], k["trig"][:, 0:2], ACT.Silu).then_inc(embedded, 1)

    def modulate(pe):
        pe.wait_ge(embedded, 1)
        pe.wait_ge(cond_in, 16 * len(conds))
        for c in range(4):
            for i in range(DC):
                last = pe.matmul(ada_ps[:, c], w_ada[:, i, c * P:(c + 1) * P], emb[:, i],
                                 start=(i == 0), stop=(i == DC - 1))
        last.then_inc(ada_done, 1)

    return dict(load=load, angles=angles, domains=domains, rotations=rotations, modulation=modulation,
                sines_of=sines_of, modulate=modulate)


_c1 = 6.28125
_c2 = float(np.float32(np.round((2 * np.pi - _c1) * 2.0 ** 19) / 2.0 ** 19))
TWO_PI_PARTS = (_c1, _c2, 2 * np.pi - _c1 - _c2)

HEADS_OF_LOADS = dict(x1=2, expert=4, store_0=7, store_1=11, stack_0=9)
STATISTICS_AT, DEVIATION_AT, NORMALISE_AT = 11, 12, 14
WEIGH_AFTER = 17
CONTEXT_AFTER = 21
VALUES_AT = (39, 41, 56)
RESIDUAL_AT = 15
MASK_TERM_AT = 56
MASK_LEAD = 9
HIGH_STEP, LOW_STEP = 19, 20
TAIL = [("O", 3, 6, 1), ("C", 0, 8, 1), ("C", 1, 9, 1), ("W", 0, 11, 1), ("W", 1, 12, 1)]
AHEAD = [("XT", 0, 16, 0), ("XT", 1, 17, 0), ("Q", 0, 23, 0), ("K", 0, 24, 0), ("Q", 1, 26, 0), ("K", 1, 29, 0)]
VALUES = [("V", 0, 31, 0), ("V", 1, 35, 0)]
GROUPS = [("O", 0, 32, 0), ("O", 1, 42, 0), ("O", 2, 54, 0)]
SPARE = sorted(TAIL + AHEAD + GROUPS + VALUES, key=lambda use: use[2])
ACT_TAKES = (0, 2, 3, 5, 7)
PROLOGUE = AHEAD + VALUES
CUT_STEPS = [use[2] + 2 for use in AHEAD if use[0] in "QK"]
LAST = TAIL + GROUPS
FINAL = [(what, i, STEPS, 0) for what, i, _, _ in TAIL]


def parts(what):
    return 2 if what in "QKVW" else 1


class SpareBanks:

    def __init__(self, kind):
        self.uses = dict(first=PROLOGUE, middle=SPARE, last=LAST + FINAL)[kind]
        self.kind = kind

    def full(self, n, b):
        k = n // 2 + 1
        return k if self.kind == "first" else b * (len(SPARE) // 2) + (len(PROLOGUE) // 2 + k)


def attention_block(nc, d, v, k, x1_dram, pieces_dram):
    with ExitStack() as ctx:
        def sb(name, shape, dt=F32):
            return ctx.enter_context(nc.sbuf_tensor(name, shape, dt))

        def ps(name):
            return ctx.enter_context(nc.psum_tensor(name, [P, 512], F32))

        def sem(name):
            return ctx.enter_context(nc.semaphore(name))

        NT = 4
        bq_scaled = sb("bq_scaled", [P, DC])
        ident_bf = sb("ident_bf", [P, P], BF16)
        xin = sb("xin", [P, QT, D])
        xhat = sb("xhat", [P, QT, D])
        stats = sb("stats", [P, QT, 6])
        mv = sb("mv", [P, QT, 2])
        std = sb("std", [P, QT])
        rstd = sb("rstd", [P, QT])
        eps = sb("eps", [P, 1])
        xt = sb("xt", [P, DC, S])
        xth, xtl = (sb(n, [P, DC, S], F32R) for n in ("xth", "xtl"))
        xres = sb("xres", [P, DC, S])
        proj = sb("proj", [P, 2, S])
        rest = sb("rest", [P, S])
        pieces = sb("pieces", [P, 2, 3, S], BF16)
        stack_q = sb("stack_q", [P, H, S], BF16)
        stack_k = sb("stack_k", [P, H, S], BF16)
        vst = sb("vst", [P, QT, D])
        val = sb("val", [P, QT, H, VW])
        mraw = sb("mraw", [P, QT, S], U8)
        mterm = sb("mterm", [P, QT, S], BF16)
        bias = k["big"]
        prob = sb("prob", [P, NT, S])
        nmax = sb("nmax", [P, NT])
        pt = sb("pt", [P, G + 1, QT, S])
        osb = sb("osb", [P, S])
        rsum = sb("rsum", [P, QT, G, 1])
        con = sb("con", [P, QT, D])
        cont = sb("cont", [P, DC, S])
        x1 = sb("x1", [P, DC, S])

        s_bank = [ps(f"s_bank{i}") for i in range(3)]
        t_bank = [ps(f"t_bank{i}") for i in range(2)]
        o_bank = ps("o_bank")
        spare = [ps(f"spare{i}") for i in range(2)]

        x_in = Count(sem("x_in"), 16, 16)
        mask_in = Count(sem("mask_in"), 16, 16)
        stat_done = Count(sem("stat_done"), 1, 1)
        std_done = Count(sem("std_done"), 1, 1)
        xhat_done = Count(sem("xhat_done"), 1, 1)
        xt_done = Count(sem("xt_done"), DC, DC)
        proj_done = Count(sem("proj_done"), 4, 4)
        cut_done = Count(sem("cut_done"), 4, 4)
        pieces_out = [[Count(sem(f"pieces_out{c}{qk}"), 16, 16) for qk in range(2)] for c in range(DC)]
        stack_in = [Count(sem(f"stack_in{c}"), 16 * 2 * NP8, 16 * 2 * NP8) for c in range(DC)]
        vst_done = Count(sem("vst_done"), 2, 2)
        val_done = Count(sem("val_done"), NG, NG)
        mask_done = Count(sem("mask_done"), QT, QT)
        res_done = Count(sem("res_done"), 1, 1)
        scored = Count(sem("scored"), STEPS, STEPS)
        biased = Count(sem("biased"), STEPS, STEPS)
        exped = Count(sem("exped"), STEPS, STEPS)
        turned = Count(sem("turned"), STEPS, STEPS)
        per_evac = [STEPS // 8 * len(ACT_TAKES), STEPS // 8 * (8 - len(ACT_TAKES))]
        evac = [Count(sem("evac_act"), per_evac[0], per_evac[0]), Count(sem("evac_dve"), per_evac[1], per_evac[1])]
        weighed = Count(sem("weighed"), NG, NG)
        o_out = Count(sem("o_out"), NG, NG)
        normed = Count(sem("normed"), NG, NG)
        masked = Count(sem("masked"), len(POOL_MASKED), 0)
        cont_done = Count(sem("cont_done"), DC, DC)
        x1_done = Count(sem("x1_done"), DC, DC)
        x1_out = Count(sem("x1_out"), 16, 16)
        credited = [scored, biased, exped, turned, *evac, weighed, o_out, normed, cont_done,
                    x1_done, x1_out]
        bias_in = [sem(f"bias_in{i}") for i in range(NB)]
        spare_full = [sem(f"spare_full{i}") for i in range(2)]
        dve_link = sem("dve_link")
        pool_link = sem("pool_link")
        dve_apart = sem("dve_apart")
        pool_apart = sem("pool_apart")
        sp_apart = sem("sp_apart")
        consts = sem("consts")
        ident_bf_made, bq_made = sem("ident_bf_made"), sem("bq_made")
        early_in, weights_in = sem("early_in"), sem("weights_in")
        w = dict(wq=con[:, 0:2], wk=con[:, 2:4], wv=x1[:, 0].rearrange("p (c n) -> p c n", c=DC),
                 wo=sb("wo", [P, DC, D])[:])
        wh, wl = ({n: sb(n + part, [P, DC, D], F32R) for n in ("wq", "wk", "wv")} for part in "hl")
        w_high, w_low = sem("w_high"), sem("w_low")
        xth_done, xtl_done = Count(sem("xth_done"), DC, DC), Count(sem("xtl_done"), DC, DC)
        vec = {n: sb(n, [P, DC]) for n in ("bq", "bk", "bo")}
        bv = sb("bv", [P, D])
        early = [(k["ident"][:], d["ident"]), (w["wq"], v["Wq"]), (w["wk"], v["Wk"]), (vec["bq"][:], v["bq"]),
                 (vec["bk"][:], v["bk"])]
        later = [(w["wv"], v["Wv"]), (bv[:], d["L0_cond_bv"].partition_broadcast(P)), (w["wo"], v["Wo"]),
                 (vec["bo"][:], v["bo"])]
        late_loads = [(k["b1"][:], v["b1"]), (k["b2"][:], v["b2"]), (k["g2"][:], v["g2"]),
                      (k["beta2"][:], v["beta2"])]
        for l, n in enumerate((1, 3)):
            late_loads += [
                (k["down_w"][:, l], d[f"L{n}_cond_down_W"].rearrange("(c p) a -> p c a", p=P)),
                (k["up_b"][:, l], d[f"L{n}_cond_up_b"]),
            ]
            for rows in HALVES:
                late_loads += [
                    (k["down_b"][rows, l:l + 1], d[f"L{n}_cond_down_b"].rearrange("(a o) -> a o", o=1)),
                    (k["up_w"][rows, l], d[f"L{n}_cond_up_W"]),
                ]
        late_loads += [
            (k["gamma_f"][:], d["L1_cond_ln_gamma"]), (k["beta_f"][:], d["L1_cond_ln_beta"]),
            (k["gamma"][:], d["L3_cond_ln_gamma"].partition_broadcast(P)),
            (k["beta"][:], d["L3_cond_ln_beta"].partition_broadcast(P)),
            (k["beside"][:], d["beside"]),
        ]
        assert len(late_loads) == LATE_LOADS
        first_loads = [(xin[:], v["x"][:, 0], x_in.sem)] + [(dst, src, early_in) for dst, src in early]
        first_loads += [(mraw[:], v["mask"][:, 0], mask_in.sem)] + [(dst, src, weights_in) for dst, src in later]
        first_loads += [(bias[:, h], v["bias"][:, h], bias_in[h]) for h in range(NB)]
        setup = setup_programs(nc, ctx, d, v, k, s_bank[0], cont[:])
        block = ctx.enter_context(nc.Block())

        def pt_slot(h):
            return h % G if h % G else G * (h // G % 2)

        def evac_of(n):
            by_act = n % 8 in ACT_TAKES
            return (0, 1)[not by_act], sum((m % 8 in ACT_TAKES) == by_act for m in range(n + 1))

        def read_of(use, b):
            what, i, _, back = use
            count = dict(XT=xt_done, Q=proj_done, K=proj_done, V=vst_done, O=normed, C=cont_done, W=x1_done)[what]
            if what in "QK":
                i = 2 * i + "QK".index(what)
            return count.sem, count.at(b - back, i + 1)

        @block.sync
        def _(sp):
            setup["load"](sp)
            for dst, src, arrived in first_loads:
                sp.dma_start(dst, src).then_inc(arrived, 16)
            for c in credited:
                sp.sem_inc(c.sem, c.ahead)
            bias_flat = v["bias"]

            def load_bias(b, h):
                sp.dma_start(bias[:, h % NB], bias_flat[:, bass.ds(b * H + h, 1)].rearrange("p o t k -> p (o t) k")
                             ).then_inc(bias_in[h % NB], 16)

            def load_x(b):
                sp.wait_ge(xhat_done.sem, xhat_done.at(b - 1, 1))
                apart(sp, sp_apart)
                sp.dma_start(xin[:], v["x"][:, bass.ds(b + 1, 1)].rearrange("p o t k -> p (o t) k")
                             ).then_inc(x_in.sem, 16)
                sp.wait_ge(mask_done.sem, mask_done.at(b - 1, QT))
                apart(sp, sp_apart)
                sp.dma_start(mraw[:], v["mask"][:, bass.ds(b + 1, 1)].rearrange("p o t k -> p (o t) k")
                             ).then_inc(mask_in.sem, 16)

            def store_pieces(b, c, first=False):
                if not first:
                    sp.wait_ge(stack_in[c].sem, stack_in[c].at(b - 1, stack_in[c].per))
                    apart(sp, sp_apart)
                for qk in range(2):
                    sp.wait_ge(cut_done.sem, cut_done.at(b, 2 * c + qk + 1))
                    apart(sp, sp_apart)
                    sp.dma_start(pieces_dram[:, qk, c], pieces[:, qk, :, :]).then_inc(pieces_out[c][qk].sem, 16)

            def load_stack(b, c, first=False):
                if not first:
                    sp.wait_ge(scored.sem, scored.at(b, STEPS // 2 * (c + 1)))
                    apart(sp, sp_apart)
                for qk, (stack, piece) in enumerate(((stack_q, QPIECE), (stack_k, KPIECE))):
                    sp.wait_ge(pieces_out[c][qk].sem, pieces_out[c][qk].at(b, 16))
                    apart(sp, sp_apart)
                    for i in range(NP8):
                        src = pieces_dram[:, qk, c, piece[i]].rearrange("(h e) t -> e h t", e=HD)
                        sp.dma_start(stack[i * HD:(i + 1) * HD, c * HC:(c + 1) * HC], src
                                     ).then_inc(stack_in[c].sem, 16)

            def store_x1(b):
                sp.wait_ge(x1_done.sem, x1_done.at(b, DC))
                apart(sp, sp_apart)
                sp.dma_start(x1_dram[bass.ds(b, 1)].rearrange("o p c t -> (o p) c t"), x1[:]
                             ).then_inc(x1_out.sem, 16)

            def load_expert(b):
                apart(sp, sp_apart)
                e = sp.value_load(k["domi"][0:1, bass.ds(b, 1)], min_val=0, max_val=E - 1)
                for l, n in enumerate((1, 3)):
                    for name, dst in (("expert_W", k["expert_w"][:, l, bass.ds(b, 1), :]),
                                      ("expert_b", k["expert_b"][:, l, bass.ds(b, 1)]),
                                      ("domain_emb", k["domain_emb"][:, l, bass.ds(b, 1)])):
                        src = d[f"L{n}_cond_{name}"][bass.ds(e, 1)]
                        src = src.rearrange("e i o -> (e i) o") if name == "expert_W" else src.rearrange("e a -> a e")
                        if name == "expert_W":
                            dst = dst.rearrange("p o a -> p (o a)")
                        for rows in HALVES:
                            sp.dma_start(dst[rows], src).then_inc(k["chosen"], 16)

            def iteration(b, first=False, last=False):
                if not last and not first:
                    load_x(b)
                for h in range(H):
                    if not (last and h + NB >= H):
                        sp.wait_ge(biased.sem, biased.at(b, QT * (h + 1)))
                        apart(sp, sp_apart)
                        load_bias(b, h + NB)
                    if h == HEADS_OF_LOADS["x1"] and not first:
                        store_x1(b - 1)
                    if h == HEADS_OF_LOADS["expert"]:
                        load_expert(b)
                    if h == HEADS_OF_LOADS["store_0"] and not last:
                        store_pieces(b, 0)
                    if h == HEADS_OF_LOADS["store_1"] and not last:
                        store_pieces(b, 1)
                    if h == HEADS_OF_LOADS["stack_0"] and not last:
                        load_stack(b, 0)
                if not last:
                    load_stack(b, 1)

            for c in range(DC):
                store_pieces(-1, c, first=True)
                load_stack(-1, c, first=True)
                if c == 0:
                    load_x(0)
            iteration(0, first=True)
            with sp.Fori(1, B - 1) as b:
                iteration(b)
            for dst, src in late_loads:
                sp.dma_start(dst, src).then_inc(k["late_in"], 16)
            iteration(B - 1, last=True)
            sp.wait_ge(biased.sem, biased.at(B - 1, QT * (H - 1)))
            w1_raw, w2_raw, x1t = raw_views(k["big"])
            sp.dma_start(x1t, x1_dram[0]).then_inc(k["x1t_in"], 16)
            sp.dma_start(w1_raw, v["W1"]).then_inc(k["w1_in"], 16)
            sp.dma_start(w2_raw, v["W2"]).then_inc(k["w2_in"], 16)
            store_x1(B - 1)
            sp.wait_ge(x1_out.sem, x1_out.at(B - 1, 16))

        @block.tensor
        def _(pe):
            ident = k["ident"]

            def spare_take(banks, n, b):
                if n >= 2:
                    pe.wait_ge(*read_of(banks.uses[n - 2], b))
                elif banks.kind != "first":
                    pe.wait_ge(*read_of(SPARE[n - 2], b - 1))
                return spare[n % 2]

            def scores(b, n):
                h, t = n // QT, n % QT
                if n % (STEPS // 2) == 0:
                    c = n // (STEPS // 2)
                    pe.wait_ge(stack_in[c].sem, stack_in[c].at(b - 1, stack_in[c].per))
                if n < QT:
                    pe.wait_ge(mask_done.sem, mask_done.at(b - 1, n + 1))
                before = n - 3 if n >= 3 else (63, 61, 62)[n] - STEPS
                pe.wait_ge(biased.sem, biased.at(b, before + 1))
                bank = s_bank[n % 3][:, :]
                last = pe.matmul(bank, stack_q[:, h, t * P:(t + 1) * P], stack_k[:, h, :], start=True,
                                 stop=(h not in PE_MASKED))
                if h in PE_MASKED:
                    last = pe.matmul(bank, ident_bf[:], mterm[:, t, :], start=False, stop=True)
                last.then_inc(scored.sem, 1)

            def turn(b, n):
                h, t = n // QT, n % QT
                pe.wait_ge(exped.sem, exped.at(b, n + 1))
                who, taken = evac_of((n - 2) % STEPS)
                pe.wait_ge(evac[who].sem, evac[who].at(b, taken - (per_evac[who] if n < 2 else 0)))
                for c in range(QT):
                    last = pe.transpose(t_bank[n % 2][:, c * P:(c + 1) * P], prob[:, n % NT, c * P:(c + 1) * P],
                                        ident[:])
                last.then_inc(turned.sem, 1)

            def weigh(b, g, c):
                if c == 0:
                    for who, e in enumerate(evac):
                        pe.wait_ge(e.sem, e.at(b, per_evac[who] // NG * (g + 1)))
                    pe.wait_ge(val_done.sem, val_done.at(b - 1, g + 1))
                    pe.wait_ge(o_out.sem, o_out.at(b, g))
                for j in range(G):
                    last = pe.matmul(o_bank[VW * j:VW * (j + 1), :], val[:, c, G * g + j, :],
                                     pt[:, pt_slot(G * g + j), c, :],
                                     start=(c == 0), stop=(c == QT - 1), tile_position=(0, VW * j))
                if c == QT - 1:
                    last.then_inc(weighed.sem, 1)

            def spare_use(banks, n, b, part):
                what, i, _, back = banks.uses[n]
                if what == "XT":
                    if i == 0:
                        pe.wait_ge(xhat_done.sem, xhat_done.at(b, 1))
                    bank = spare_take(banks, n, b)
                    for t in range(QT):
                        last = pe.transpose(bank[:, t * P:(t + 1) * P], xhat[:, t, i * P:(i + 1) * P], ident[:])
                elif what in "QK":
                    if part == 0:
                        pe.wait_ge(xth_done.sem, xth_done.at(b, DC))
                        pe.wait_ge(xtl_done.sem, xtl_done.at(b, DC))
                        spare_take(banks, n, b)
                    name = "wq" if what == "Q" else "wk"
                    for m, (wx, x) in enumerate(((wh, xth), (wh, xtl), (wl, xth))):
                        last = pe.matmul(spare[n % 2][:, :], wx[name][:, part, i * P:(i + 1) * P], x[:, part, :],
                                         start=(part == m == 0), stop=(part == 1 and m == 2))
                elif what == "V":
                    if part == 0:
                        spare_take(banks, n, b)
                    tok = (2 * i + part) * P
                    products = [(x, wx, c) for c in range(DC) for x, wx in ((xth, wh), (xth, wl), (xtl, wh))]
                    for m, (x, wx, c) in enumerate(products):
                        last = pe.matmul(spare[n % 2][:, part * D:(part + 1) * D], x[:, c, tok:tok + P],
                                         wx["wv"][:, c, :], start=(m == 0), stop=(m == len(products) - 1))
                elif what == "O":
                    pe.wait_ge(o_out.sem, o_out.at(b - back, i + 1))
                    bank = spare_take(banks, n, b)
                    for t in range(QT):
                        last = pe.transpose(bank[:, t * P:(t + 1) * P], osb[:, t * P:(t + 1) * P], ident[:])
                elif what == "C":
                    if i == 0:
                        pe.wait_ge(normed.sem, normed.at(b - back, NG))
                    bank = spare_take(banks, n, b)
                    for t in range(QT):
                        last = pe.transpose(bank[:, t * P:(t + 1) * P], con[:, t, i * P:(i + 1) * P], ident[:])
                elif what == "W":
                    if part == 0:
                        pe.wait_ge(cont_done.sem, cont_done.at(b - back, DC))
                        spare_take(banks, n, b)
                    last = pe.matmul(spare[n % 2][:, :], w["wo"][:, part, i * P:(i + 1) * P], cont[:, part, :],
                                     start=(part == 0), stop=(part == 1))
                if part == parts(what) - 1:
                    last.then_inc(spare_full[n % 2], 1)

            def iteration(b, first=False, last=False):
                banks = SpareBanks("last" if last else "middle")
                for n in range(STEPS):
                    if n + 3 < STEPS:
                        scores(b, n + 3)
                    elif not last:
                        scores(b + 1, n + 3 - STEPS)
                    g, c = (n - WEIGH_AFTER) // 16, (n - WEIGH_AFTER) % 16
                    if c < QT and g >= 0:
                        weigh(b, g, c)
                    elif c < QT and g == -1 and not first:
                        weigh(b - 1, NG - 1, c)
                    turn(b, n)
                    for m, use in enumerate(banks.uses):
                        if use[2] <= n < use[2] + parts(use[0]) and not (first and use in TAIL):
                            spare_use(banks, m, b, n - use[2])
                if last:
                    for c in range(QT):
                        weigh(b, NG - 1, c)
                    for m in range(len(LAST), len(banks.uses)):
                        for part in range(parts(banks.uses[m][0])):
                            spare_use(banks, m, b, part)

            setup["modulate"](pe)
            banks = SpareBanks("first")
            pe.wait_ge(early_in, 16 * len(early))
            for m, use in enumerate(banks.uses):
                if use[0] in "QV":
                    ready = 2 if use[0] == "Q" else 3
                    pe.wait_ge(w_high, ready)
                    pe.wait_ge(w_low, ready)
                for part in range(parts(use[0])):
                    spare_use(banks, m, -1, part)
            pe.wait_ge(weights_in, 16 * len(later))
            pe.wait_ge(ident_bf_made, 1)
            pe.wait_ge(vst_done.sem, vst_done.at(-1, 2))
            for m in range(len(TAIL)):
                pe.sem_inc(spare_full[m % 2], 1)
            for n in range(3):
                scores(0, n)
            iteration(0, first=True)
            with pe.Fori(1, B - 1) as b:
                iteration(b)
            iteration(B - 1, last=True)

        @block.vector
        def _(dve):
            links = [0]
            per_link = 2 + NG

            def link(b, ins):
                links[0] += 1
                ins.then_inc(dve_link, 1)
                dve.wait_ge(dve_link, links[0] if isinstance(b, int) else (b - 1) * per_link + links[0])

            def add_bias(b, n):
                h, t = n // QT, n % QT
                if t == 0 and h in PE_MASKED:
                    dve.wait_ge(bias_in[h % NB], b * (16 * H // NB) + 16 * (h // NB + 1))
                elif t == 0:
                    dve.wait_ge(masked.sem, masked.at(b, POOL_MASKED.index(h) + 1))
                dve.wait_ge(scored.sem, scored.at(b, n + 1))
                dve.wait_ge(turned.sem, turned.at(b, n + 1 - NT))
                apart(dve, dve_apart)
                dve.tensor_tensor_reduce(out=prob[:, n % NT, :], in0=s_bank[n % 3][:, :],
                                         in1=bias[:, h % NB, t, :], scale=-1.0, scalar=3e38,
                                         op0=ALU.add, op1=ALU.min, accum_out=nmax[:, n % NT:n % NT + 1]
                                         ).then_inc(biased.sem, 1)

            def take_turned(b, n):
                h, t = n // QT, n % QT
                dve.wait_ge(turned.sem, turned.at(b, n + 1))
                dve.wait_ge(weighed.sem, weighed.at(b, h // G - (h % G == 0)))
                dve.tensor_copy(pt[:, pt_slot(h), :, t * P:(t + 1) * P],
                                t_bank[n % 2][:, :].rearrange("p (c q) -> p c q", c=QT)).then_inc(evac[1].sem, 1)

            def statistics(b):
                dve.wait_ge(x_in.sem, x_in.at(b, 16))
                for t in range(QT):
                    last = dve.bn_stats(stats[:, t], xin[:, t])
                link(b, last)
                apart(dve, dve_apart)
                for t in range(QT):
                    last = dve.bn_aggr(mv[:, t], stats[:, t])
                last.then_inc(stat_done.sem, 1)

            def normalise(b):
                dve.wait_ge(std_done.sem, std_done.at(b, 1))
                link(b, dve.reciprocal(rstd[:], std[:]))
                for t in range(QT):
                    last = dve.tensor_scalar(xhat[:, t], xin[:, t], mv[:, t, 0:1], rstd[:, t:t + 1],
                                             ALU.subtract, ALU.mult)
                last.then_inc(xhat_done.sem, 1)

            def low_parts(b):
                for c in range(DC):
                    dve.wait_ge(xth_done.sem, xth_done.at(b, c + 1))
                    dve.wait_ge(xt_done.sem, xt_done.at(b, c + 1))
                    dve.tensor_tensor(xtl[:, c], xt[:, c], xth[:, c], ALU.subtract).then_inc(xtl_done.sem, 1)

            def spare_use(banks, m, b, first=False):
                what, i, _, back = banks.uses[m]
                if what in ("Q", "K", "C"):
                    return
                s = spare[m % 2]
                dve.wait_ge(spare_full[m % 2], banks.full(m, b))
                if what == "XT":
                    if i == 0 and not first:
                        dve.wait_ge(res_done.sem, res_done.at(b - 1, 1))
                    dve.tensor_scalar(xt[:, i], s[:, :], k["ada"][:, i, bass.ds(b + 1, 1)],
                                      k["ada"][:, DC + i, bass.ds(b + 1, 1)], ALU.mult, ALU.add
                                      ).then_inc(xt_done.sem, 1)
                elif what == "V":
                    if i == 0 and not first:
                        dve.wait_ge(val_done.sem, val_done.at(b - 1, NG))
                    for t in range(2):
                        last = dve.tensor_tensor(vst[:, 2 * i + t], s[:, t * D:(t + 1) * D], bv[:], ALU.add)
                    last.then_inc(vst_done.sem, 1)
                elif what == "O":
                    o = s[:, :].rearrange("p (t j e) -> p t j e", t=QT, j=G)
                    link(b, dve.reciprocal(rsum[:], o[:, :, :, HD:HD + 1]))
                    dve.tensor_tensor(con[:, :, i * G * HD:(i + 1) * G * HD].rearrange("p t (j e) -> p t j e", j=G),
                                      o[:, :, :, 0:HD], rsum[:].to_broadcast([P, QT, G, HD]), ALU.mult
                                      ).then_inc(normed.sem, 1)
                elif what == "W":
                    dve.wait_ge(res_done.sem, res_done.at(b - back - 1, 1))
                    dve.wait_ge(x1_out.sem, x1_out.at(b - back, 0))
                    dve.scalar_tensor_tensor(x1[:, i], s[:, :], vec["bo"][:, i:i + 1], xres[:, i],
                                             ALU.add, ALU.add).then_inc(x1_done.sem, 1)

            def iteration(b, first=False, last=False):
                banks = SpareBanks("last" if last else "middle")
                for n in range(STEPS + 1):
                    if n + 2 < STEPS:
                        add_bias(b, n + 2)
                    elif n < STEPS and not last:
                        add_bias(b + 1, n + 2 - STEPS)
                    if n > 0 and (n - 1) % 8 not in ACT_TAKES:
                        take_turned(b, n - 1)
                    if not last and n == STATISTICS_AT:
                        statistics(b)
                    if not last and n == NORMALISE_AT:
                        normalise(b)
                    for m, use in enumerate(banks.uses):
                        if use[2] + parts(use[0]) == n and not (first and use in TAIL):
                            spare_use(banks, m, b)
                    if not last and n == LOW_STEP:
                        low_parts(b)
                if last:
                    for m in range(len(LAST), len(banks.uses)):
                        spare_use(banks, m, b)

            def cut(u):
                dve.wait_ge(proj_done.sem, proj_done.at(-1, u + 1))
                if u >= 2:
                    dve.wait_ge(pieces_out[0][u % 2].sem, pieces_out[0][u % 2].at(-1, 16))
                high, mid, low = (pieces[:, u % 2, i, :] for i in range(3))
                link(-1, dve.tensor_copy(high, proj[:, u % 2]))
                link(-1, dve.tensor_tensor(rest[:], proj[:, u % 2], high, ALU.subtract))
                link(-1, dve.tensor_copy(mid, rest[:]))
                dve.tensor_tensor(low, rest[:], mid, ALU.subtract).then_inc(cut_done.sem, 1)
                dve.wait_ge(cut_done.sem, cut_done.at(-1, u + 1))

            dve.memset(eps[:], EPS).then_inc(consts, 1)
            dve.memset(val[:], 0.0).then_inc(consts, 1)
            dve.wait_ge(consts, 2)
            dve.memset(val[:, :, :, HD:HD + 1], 1.0).then_inc(consts, 1)
            setup["angles"](dve)
            statistics(-1)
            setup["domains"](dve)
            setup["rotations"](dve)
            normalise(-1)
            setup["modulation"](dve)
            banks = SpareBanks("first")
            dve.wait_ge(early_in, 16 * len(early))
            for m, name in enumerate(("wq", "wk")):
                dve.wait_ge(w_high, m + 1)
                dve.tensor_tensor(wl[name][:], w[name], wh[name][:], ALU.subtract).then_inc(w_low, 1)
            dve.tensor_scalar(bq_scaled[:], vec["bq"][:], HD ** -0.5, None, ALU.mult).then_inc(bq_made, 1)
            dve.tensor_copy(ident_bf[:], k["ident"][:]).then_inc(ident_bf_made, 1)
            for m, use in enumerate(banks.uses):
                if use in VALUES:
                    dve.wait_ge(weights_in, 16 * len(later))
                    if use[1] == 0:
                        dve.wait_ge(w_high, 3)
                        dve.tensor_tensor(wl["wv"][:], w["wv"], wh["wv"][:], ALU.subtract).then_inc(w_low, 1)
                spare_use(banks, m, -1, first=True)
                if use[:2] == ("XT", 1):
                    low_parts(-1)
                if use[0] in "QK":
                    cut(2 * use[1] + "QK".index(use[0]))
            for n in range(2):
                add_bias(0, n)
            iteration(0, first=True)
            before = links[0]
            with dve.Fori(1, B - 1) as b:
                iteration(b)
            assert links[0] - before == per_link
            links[0] = before + (B - 2) * per_link
            iteration(B - 1, last=True)

        @block.scalar
        def _(act):
            def exponent(b, n):
                act.wait_ge(biased.sem, biased.at(b, n + 1))
                tile = prob[:, n % NT, :]
                act.activation(tile, tile, ACT.Exp, bias=nmax[:, n % NT:n % NT + 1], scale=-1.0
                               ).then_inc(exped.sem, 1)

            def take_turned(b, n):
                h, t = n // QT, n % QT
                act.wait_ge(turned.sem, turned.at(b, n + 1))
                act.wait_ge(weighed.sem, weighed.at(b, h // G - (h % G == 0)))
                act.copy(pt[:, pt_slot(h), :, t * P:(t + 1) * P],
                         t_bank[n % 2][:, :].rearrange("p (c q) -> p c q", c=QT)).then_inc(evac[0].sem, 1)

            def deviation(b):
                act.wait_ge(stat_done.sem, stat_done.at(b, 1))
                act.activation(std[:], mv[:, :, 1], ACT.Sqrt, bias=eps[:, 0:1]).then_inc(std_done.sem, 1)

            def high_parts(b):
                act.wait_ge(vst_done.sem, vst_done.at(b - 1, 2))
                for c in range(DC):
                    act.wait_ge(xt_done.sem, xt_done.at(b, c + 1))
                    act.copy(xth[:, c], xt[:, c]).then_inc(xth_done.sem, 1)

            def take_context(b, g):
                act.wait_ge(weighed.sem, weighed.at(b, g + 1))
                act.wait_ge(normed.sem, normed.at(b, g))
                act.copy(osb[:], o_bank[:, :]).then_inc(o_out.sem, 1)

            def spare_use(banks, m, b, first=False):
                what, i, _, back = banks.uses[m]
                if what not in ("Q", "K", "C"):
                    return
                s = spare[m % 2]
                act.wait_ge(spare_full[m % 2], banks.full(m, b))
                if what == "C":
                    act.copy(cont[:, i], s[:, :]).then_inc(cont_done.sem, 1)
                else:
                    u = 2 * i + "QK".index(what)
                    if not (first and u < 2):
                        act.wait_ge(cut_done.sem, cut_done.at(b, u - 1))
                    act.activation(proj[:, u % 2], s[:, :], ACT.Identity,
                                   bias=(bq_scaled if what == "Q" else vec["bk"])[:, i:i + 1],
                                   scale=HD ** -0.5 if what == "Q" else 1.0).then_inc(proj_done.sem, 1)

            def iteration(b, first=False, last=False):
                banks = SpareBanks("last" if last else "middle")
                for n in range(STEPS + 1):
                    if n + 1 < STEPS:
                        exponent(b, n + 1)
                    elif n < STEPS and not last:
                        exponent(b + 1, 0)
                    if n > 0 and (n - 1) % 8 in ACT_TAKES:
                        take_turned(b, n - 1)
                    if not last and n == DEVIATION_AT:
                        deviation(b)
                    if n == CONTEXT_AFTER - 16 and not first:
                        take_context(b - 1, NG - 1)
                    if not last and n == HIGH_STEP:
                        high_parts(b)
                    if n > 16 and n % 16 == CONTEXT_AFTER % 16:
                        take_context(b, n // 16 - 1)
                    for m, use in enumerate(banks.uses):
                        if use[2] + parts(use[0]) == n and not (first and use in TAIL):
                            spare_use(banks, m, b)
                if last:
                    take_context(b, NG - 1)
                    for m in range(len(LAST), len(banks.uses)):
                        spare_use(banks, m, b)

            setup["sines_of"](act)
            act.wait_ge(consts, 1)
            deviation(-1)
            banks = SpareBanks("first")
            act.wait_ge(early_in, 16 * len(early))
            for name in ("wq", "wk"):
                act.copy(wh[name][:], w[name]).then_inc(w_high, 1)
            act.wait_ge(weights_in, 16 * len(later))
            act.copy(wh["wv"][:], w["wv"]).then_inc(w_high, 1)
            high_parts(-1)
            act.wait_ge(bq_made, 1)
            for m in range(len(banks.uses)):
                spare_use(banks, m, -1, first=True)
            exponent(0, 0)
            iteration(0, first=True)
            with act.Fori(1, B - 1) as b:
                iteration(b)
            iteration(B - 1, last=True)

        @block.gpsimd
        def _(pool):
            links = [0]
            per_link = 3 * 4

            def link(b, ins):
                links[0] += 1
                ins.then_inc(pool_link, 1)
                pool.wait_ge(pool_link, links[0] if isinstance(b, int) else (b - 1) * per_link + links[0])

            def cut(b, u):
                c, qk = u // 2, u % 2
                pool.wait_ge(proj_done.sem, proj_done.at(b, u + 1))
                before = pieces_out[c - 1][qk]
                pool.wait_ge(before.sem, before.at(b - 1 if c == 0 else b, 16))
                high, mid, low = (pieces[:, qk, i, :] for i in range(3))
                apart(pool, pool_apart)
                link(b, pool.tensor_scalar(high, proj[:, u % 2], 1.0, 0.0, ALU.mult, ALU.add))
                link(b, pool.tensor_tensor(rest[:], proj[:, u % 2], high, ALU.subtract))
                apart(pool, pool_apart)
                link(b, pool.tensor_scalar(mid, rest[:], 1.0, 0.0, ALU.mult, ALU.add))
                pool.tensor_tensor(low, rest[:], mid, ALU.subtract).then_inc(cut_done.sem, 1)
                pool.wait_ge(cut_done.sem, cut_done.at(b, u + 1))

            def copy_values(b, g, first=False):
                if g == 0:
                    pool.wait_ge(vst_done.sem, vst_done.at(b, 2))
                if not first:
                    pool.wait_ge(weighed.sem, weighed.at(b, g + 1))
                apart(pool, pool_apart)
                for t in range(QT):
                    last = pool.tensor_scalar(val[:, t, G * g:G * (g + 1), 0:HD],
                                              vst[:, t, G * HD * g:G * HD * (g + 1)].rearrange("p (j e) -> p j e", j=G),
                                              1.0, 0.0, ALU.mult, ALU.add)
                last.then_inc(val_done.sem, 1)

            def mask_term(b, t, first=False):
                if t == 0:
                    pool.wait_ge(mask_in.sem, mask_in.at(b, 16))
                if not first:
                    pool.wait_ge(scored.sem, scored.at(b, QT * max(PE_MASKED) + t + 1))
                    if t == 0:
                        pool.wait_ge(masked.sem, masked.at(b, len(POOL_MASKED)))
                apart(pool, pool_apart)
                pool.tensor_scalar(
                    mterm[:, t, :], mraw[:, t, :], MASKED, 0.0, ALU.mult, ALU.add
                ).then_inc(mask_done.sem, 1)

            def keep_residual(b, first=False):
                pool.wait_ge(xt_done.sem, xt_done.at(b, DC))
                if not first:
                    pool.wait_ge(x1_done.sem, x1_done.at(b, DC))
                apart(pool, pool_apart)
                pool.tensor_scalar(xres[:], xt[:], 1.0, 0.0, ALU.mult, ALU.add).then_inc(res_done.sem, 1)

            def mask_bias(b, h):
                pool.wait_ge(bias_in[h % NB], b * (16 * H // NB) + 16 * (h // NB + 1))
                if h == POOL_MASKED[0]:
                    pool.wait_ge(mask_done.sem, mask_done.at(b - 1, QT))
                apart(pool, pool_apart)
                pool.tensor_tensor(bias[:, h % NB], bias[:, h % NB], mterm[:], ALU.add).then_inc(masked.sem, 1)

            def iteration(b, first=False, last=False):
                for n in range(STEPS):
                    if n == CONTEXT_AFTER - 16 and not first:
                        copy_values(b - 1, NG - 1)
                    if n == RESIDUAL_AT and not first:
                        keep_residual(b - 1)
                    if (n + MASK_LEAD) % QT == 0 and (n + MASK_LEAD) // QT in POOL_MASKED:
                        mask_bias(b, (n + MASK_LEAD) // QT)
                    if n == 0:
                        for h in POOL_MASKED:
                            if QT * h < MASK_LEAD:
                                mask_bias(b, h)
                    if not last and n in CUT_STEPS:
                        cut(b, CUT_STEPS.index(n))
                    if not last and n in VALUES_AT:
                        copy_values(b, VALUES_AT.index(n))
                    if not last and n == MASK_TERM_AT:
                        for t in range(QT):
                            mask_term(b, t)

            for t in range(QT):
                mask_term(-1, t, first=True)
            pool.wait_ge(consts, 3)
            for g in range(NG):
                copy_values(-1, g, first=True)
            keep_residual(-1, first=True)
            iteration(0, first=True)
            before = links[0]
            with pool.Fori(1, B - 1) as b:
                iteration(b)
            assert links[0] - before == per_link
            iteration(B - 1, last=True)


def raw_views(big):
    assert NB >= 3 and QT * S == DC * F == FC * D == 2 * DC * S
    w1 = big[:, 0].rearrange("p (c i) s -> p c (i s)", c=DC)
    w2 = big[:, 1].rearrange("p i (f n) -> p (i f) n", n=D)
    return w1, w2, big[:, 2, 0:DC]


def network_block(nc, d, v, k, x1_dram):
    with ExitStack() as ctx:
        def sb(name, shape, dt=F32):
            return ctx.enter_context(nc.sbuf_tensor(name, shape, dt))

        def sem(name):
            return ctx.enter_context(nc.semaphore(name))

        w1h, w1l = (sb(n, [P, DC, F], F32R) for n in ("w1h", "w1l"))
        w2h, w2l = (sb(n, [P, FC, D], F32R) for n in ("w2h", "w2l"))
        dwh, dwl = (sb(n, [P, 2, DC, 2, A], F32R) for n in ("dwh", "dwl"))
        uwh, uwl = (sb(n, [P, 2, D], F32R) for n in ("uwh", "uwl"))
        ew = sb("ew", [P, 2, 2, A])
        ewh, ewl = (sb(n, [P, 2, 2, A], F32R) for n in ("ewh", "ewl"))
        rotm = sb("rotm", [P, P])
        rotc = sb("rotc", [P, P])
        g_w1, g_w2, x1t = raw_views(k["big"])
        x1r = sb("x1r", [P, DC, S])
        x2 = sb("x2", [P, DC, S])
        x4 = sb("x4", [P, DC, S])
        wid, wsel = (t[:].rearrange("p i (b a) -> p i b a", a=A) for t in (x2, x4))
        bsel = sb("bsel", [P, 2, B])
        xh = sb("xh", [P, 3, QT, D])
        feat = sb("feat", [P, DC, S])
        hh, hl = (sb(n, [P, DC, S], F32R) for n in ("hh", "hl"))
        NGT = 4
        g = k["big"][:, 0]
        gh, gl = (sb(n, [P, FC, S], F32R) for n in ("gh", "gl"))
        x24h, x24l = (sb(n, [P, 2, DC, S], F32R) for n in ("x24h", "x24l"))
        wide = sb("wide", [P, 2, S])
        hid, exo = (sb(n, [P, 2, S], F32R) for n in ("hid", "exo"))
        x3 = k["big"][:, 1].rearrange("p (l c) s -> p l c s", l=2)
        res = sb("res", [P, QT, D])
        stats = sb("stats3", [P, 3, QT, 6])
        mv = sb("mv3", [P, 3, QT, 2])
        std = sb("std3", [P, 3, QT])
        rstd = sb("rstd3", [P, 3, QT])
        eps = sb("eps3", [P, 1])
        bank = [ctx.enter_context(nc.psum_tensor(f"bank{i}", [P, 512], F32)) for i in range(8)]

        counts = []
        AHEAD_SAMPLES = 4

        def count(name, per):
            counts.append(Count(sem(name), per, AHEAD_SAMPLES * per))
            return counts[-1]

        x1t_in = Count(k["x1t_in"], 16, AHEAD_SAMPLES * 16)
        counts.append(x1t_in)
        x1r_in, stored = count("x1r_in", 16), count("stored", 16)
        to_t = [count(f"to_t{i}", 1) for i in range(3)]
        bn_done = [count(f"bn_done{i}", 1) for i in range(3)]
        stat_done = [count(f"stat_done{i}", 1) for i in range(3)]
        std_done = [count(f"std_done{i}", 1) for i in range(3)]
        rstd_done = [count(f"rstd_done{i}", 1) for i in range(3)]
        norm_done = [count(f"norm_done{i}", 1) for i in range(3)]
        to_f = [count(f"to_f{i}", 1) for i in range(2)]
        feat_done = [count(f"feat_done{i}", DC) for i in range(2)]
        hh_done, hl_done = count("hh_done", DC), count("hl_done", DC)
        w1_done = count("w1_done", FC)
        g_done, gh_done, gl_done = count("g_done", FC), count("gh_done", FC), count("gl_done", FC)
        w2_done = count("w2_done", DC)
        x2_done = count("x2_done", DC)
        rotc_done, rotm_done, rotated = count("rotc_done", 1), count("rotm_done", 1), count("rotated", 1)
        x4_done = count("x4_done", DC)
        high_done = [count(f"high_done{i}", DC) for i in range(2)]
        low_done = [count(f"low_done{i}", DC) for i in range(2)]
        down_done = [count(f"down_done{i}", 1) for i in range(2)]
        gelu_done = [count(f"gelu_done{i}", 2) for i in range(2)]
        hid_done = [count(f"hid_done{i}", 1) for i in range(2)]
        ew_done = [count(f"ew_done{i}", 3) for i in range(2)]
        expert_done = [count(f"expert_done{i}", 1) for i in range(2)]
        exw_done = [count(f"exw_done{i}", 2) for i in range(2)]
        exo_done = [count(f"exo_done{i}", 1) for i in range(2)]
        up_done = [count(f"up_done{i}", 1) for i in range(2)]
        x3_done = [count(f"x3_done{i}", DC) for i in range(2)]
        scaled, out_made = count("scaled", 1), count("out_made", 1)
        eps_set = sem("eps_set")
        pool_link, experts_made = sem("pool_link3"), sem("experts_made")
        w1_in, w2_in = k["w1_in"], k["w2_in"]
        high_w, low_w = sem("high_w"), sem("low_w")
        dve_apart = sem("dve_apart3")
        pool_apart = sem("pool_apart3")
        sp_apart = sem("sp_apart3")
        block = ctx.enter_context(nc.Block())
        TOKENS_AT, STATISTICS3_AT, NORMALISE3_AT, DEVIATION3_AT, INPUT_AT = 3, 5, 7, 8, 10
        TO_ROTATE_AT, ROTATE_AT, DOWN_AT, EXPERT_AT, UP_AT = 7, 9, 11, 13, 14
        NORM_LAG = (-1, 2, 3)

        def on(j, lag):
            return not isinstance(j, int) or 0 <= j - lag < B

        @block.sync
        def _(sp):
            first = [x1t_in, x3_done[1], norm_done[1], scaled, feat_done[1], rotated, hl_done, w1_done]
            for c in first + [c for c in counts if c not in first]:
                sp.sem_inc(c.sem, c.ahead)

            def load(j, buf, arrived, used):
                sp.wait_ge(used.sem, used.at(j - 1, used.per))
                apart(sp, sp_apart)
                sp.dma_start(buf, x1_dram[bass.ds(j, 1)].rearrange("o p c t -> (o p) c t")
                             ).then_inc(arrived.sem, 16)

            def iteration(j):
                if on(j, -2):
                    load(j + 2, x1t, x1t_in, to_t[0])
                if on(j, 0):
                    load(j, x1r[:], x1r_in, x2_done)
                if on(j, 3):
                    sp.wait_ge(out_made.sem, out_made.at(j - 3, 1))
                    apart(sp, sp_apart)
                    sp.dma_start(v["out"][:, bass.ds(j - 3, 1)].rearrange("p o t k -> p (o t) k"), res[:]
                                 ).then_inc(stored.sem, 16)

            iteration(-1)
            for j in range(0, 3):
                iteration(j)
            with sp.Fori(3, B - 2) as j:
                iteration(j)
            for j in range(B - 2, B + 3):
                iteration(j)
            sp.wait_ge(stored.sem, stored.at(B - 1, 16))

        @block.tensor
        def _(pe):
            ident = k["ident"]
            T_BANK = (6, 2, 4)

            def to_tokens(j, i, src, ready):
                pe.wait_ge(ready.sem, ready.at(j, ready.per))
                if i == 0:
                    pe.wait_ge(x3_done[1].sem, x3_done[1].at(j - 4, DC))
                elif i == 1:
                    pe.wait_ge(feat_done[0].sem, feat_done[0].at(j + 2, DC))
                else:
                    pe.wait_ge(x3_done[0].sem, x3_done[0].at(j + 1, DC))
                for t in range(QT):
                    for c in range(DC):
                        at = (t % 2) * D + c * P
                        last = pe.transpose(bank[T_BANK[i] + t // 2][:, at:at + P], src[:, c, t * P:(t + 1) * P],
                                            ident[:])
                last.then_inc(to_t[i].sem, 1)

            def to_features(j, i):
                pe.wait_ge(norm_done[i].sem, norm_done[i].at(j, 1))
                if i == 0:
                    pe.wait_ge(feat_done[1].sem, feat_done[1].at(j - 3, DC))
                for c in range(DC):
                    for t in range(QT):
                        last = pe.transpose(bank[2 + c][:, t * P:(t + 1) * P], xh[:, i, t, c * P:(c + 1) * P],
                                            ident[:])
                last.then_inc(to_f[i].sem, 1)

            def first_layer(j, f):
                if f == 0:
                    pe.wait_ge(hl_done.sem, hl_done.at(j, DC))
                    pe.wait_ge(hh_done.sem, hh_done.at(j, DC))
                if f < 2:
                    pe.wait_ge(x2_done.sem, x2_done.at(j - 1, f + 1))
                else:
                    pe.wait_ge(g_done.sem, g_done.at(j, f - 1))
                col = slice(f * P, (f + 1) * P)
                parts = [(w, c, h) for c in range(DC) for w, h in ((w1h, hh), (w1h, hl), (w1l, hh))]
                for n, (w, c, h) in enumerate(parts):
                    last = pe.matmul(bank[f % 2][:, :], w[:, c, col], h[:, c, :], start=(n == 0),
                                     stop=(n == len(parts) - 1))
                last.then_inc(w1_done.sem, 1)

            def second_layer(j, n):
                c, q = n // 4, n % 4
                parts = [(w, f, gh) for f in range(FC) for w in (w2h, w2l)] + [(w2h, f, gl) for f in range(FC)]
                if c == q == 0 and isinstance(j, int) and j == 0:
                    pe.wait_ge(high_w, 4)
                    pe.wait_ge(low_w, 4)
                if q == 0:
                    pe.wait_ge(g_done.sem, g_done.at(j, FC - 1 + c))
                size = len(parts) // 4
                for m in range(q * size, (q + 1) * size):
                    w, f, gx = parts[m]
                    if c == 0 and w is not w2l:
                        done = gh_done if gx is gh else gl_done
                        pe.wait_ge(done.sem, done.at(j, f + 1))
                    last = pe.matmul(bank[c][:, :], w[:, f, c * P:(c + 1) * P], gx[:, f, :], start=(m == 0),
                                     stop=(m == len(parts) - 1))
                if q == 3:
                    last.then_inc(w2_done.sem, 1)

            def rotate(j, at=4):
                pe.wait_ge(feat_done[1].sem, feat_done[1].at(j, DC))
                pe.wait_ge(rotm_done.sem, rotm_done.at(j, 1))
                if at == 4:
                    pe.wait_ge(norm_done[2].sem, norm_done[2].at(j - 1, 1))
                else:
                    pe.wait_ge(x3_done[0].sem, x3_done[0].at(j, DC))
                for c in range(DC):
                    last = pe.matmul(bank[at + c][:, :], rotm[:], feat[:, c, :], start=True, stop=True)
                last.then_inc(rotated.sem, 1)

            def down(j, l):
                pe.wait_ge(low_done[l].sem, low_done[l].at(j, DC))
                pe.wait_ge(high_done[l].sem, high_done[l].at(j, DC))
                if isinstance(j, int) and j == B - 1 and l == 1:
                    pe.wait_ge(x3_done[1].sem, x3_done[1].at(j - 1, DC))
                pe.wait_ge(norm_done[0].sem, norm_done[0].at(j + (l + 2), 1))
                parts = [(w, c, x) for c in range(DC) for w, x in ((dwh, x24h), (dwh, x24l), (dwl, x24h))]
                for n, (w, c, x) in enumerate(parts):
                    last = pe.matmul(bank[6 + l][:, :], w[:, l, c].rearrange("p r a -> p (r a)"), x[:, l, c, :],
                                     start=(n == 0), stop=(n == len(parts) - 1))
                last.then_inc(down_done[l].sem, 1)

            def expert(j, l):
                pe.wait_ge(hid_done[l].sem, hid_done[l].at(j, 1))
                pe.wait_ge(ew_done[l].sem, ew_done[l].at(j, 3))
                for n, w in enumerate((ewh, ewl)):
                    last = pe.matmul(bank[6 + l][:, :], w[:, l].rearrange("p r a -> p (r a)"), hid[:, l, :],
                                     start=(n == 0), stop=(n == 1))
                last.then_inc(expert_done[l].sem, 1)

            def up(j, l, at=None):
                at = (4, 6)[l] if at is None else at
                pe.wait_ge(exo_done[l].sem, exo_done[l].at(j, 1))
                if at == 0:
                    pe.wait_ge(x2_done.sem, x2_done.at(j, DC))
                elif l == 0:
                    pe.wait_ge(x4_done.sem, x4_done.at(j - 1, DC))
                else:
                    pe.wait_ge(exo_done[0].sem, exo_done[0].at(j + 1, 1))
                for c in range(DC):
                    for n, w in enumerate((uwh, uwl)):
                        last = pe.matmul(bank[at + c][:, :], w[:, l, c * P:(c + 1) * P], exo[:, l, :],
                                         start=(n == 0), stop=(n == 1))
                last.then_inc(up_done[l].sem, 1)

            def iteration(j):
                if on(j, 2):
                    to_tokens(j - 2, 1, x3[:, 0], x3_done[0])
                for n in range(2 * FC):
                    if on(j, 0):
                        if n < FC:
                            first_layer(j, n)
                        else:
                            second_layer(j, n - FC)
                    if n == 0 and on(j, 3):
                        to_tokens(j - 3, 2, x3[:, 1], x3_done[1])
                    if n == TOKENS_AT and on(j, -1):
                        to_tokens(j + 1, 0, x1t, x1t_in)
                    if n == TO_ROTATE_AT and on(j, 2):
                        to_features(j - 2, 1)
                    if n == ROTATE_AT and on(j, 2):
                        rotate(j - 2)
                    if n == INPUT_AT and on(j, -1):
                        to_features(j + 1, 0)
                    for l in range(2):
                        if on(j, 1 + l):
                            if n == DOWN_AT:
                                down(j - (1 + l), l)
                            if n == EXPERT_AT:
                                expert(j - (1 + l), l)
                            if n == UP_AT + l:
                                up(j - (1 + l), l)

            iteration(-1)
            pe.wait_ge(high_w, 3)
            pe.wait_ge(low_w, 3)
            for j in range(0, 3):
                iteration(j)
            with pe.Fori(3, B - 1) as j:
                iteration(j)
            iteration(B - 1)
            y, z = B - 2, B - 1
            to_tokens(y, 1, x3[:, 0], x3_done[0])
            to_tokens(y - 1, 2, x3[:, 1], x3_done[1])
            down(z, 0)
            to_features(y, 1)
            expert(z, 0)
            rotate(y)
            up(z, 0, at=0)
            down(y, 1)
            expert(y, 1)
            to_tokens(z, 1, x3[:, 0], x3_done[0])
            up(y, 1)
            to_features(z, 1)
            to_tokens(y, 2, x3[:, 1], x3_done[1])
            rotate(z, at=0)
            down(z, 1)
            expert(z, 1)
            up(z, 1)
            pe.wait_ge(norm_done[2].sem, norm_done[2].at(y, 1))
            to_tokens(z, 2, x3[:, 1], x3_done[1])

        @block.vector
        def _(dve):
            def gelu_high(j, f):
                dve.wait_ge(g_done.sem, g_done.at(j, f + 1))
                if f == 0:
                    dve.wait_ge(w2_done.sem, w2_done.at(j - 1, DC))
                dve.wait_ge(gl_done.sem, gl_done.at(j - 1, f + 1))
                dve.tensor_copy(gh[:, f], g[:, f % NGT]).then_inc(gh_done.sem, 1)

            def low_part(j, l, src, ready):
                dve.wait_ge(ready.sem, ready.at(j, DC))
                for c in range(DC):
                    dve.wait_ge(high_done[l].sem, high_done[l].at(j, c + 1))
                    dve.tensor_tensor(x24l[:, l, c], src[:, c], x24h[:, l, c], ALU.subtract
                                      ).then_inc(low_done[l].sem, 1)

            def take_rotated(j, at=4):
                dve.wait_ge(rotated.sem, rotated.at(j, 1))
                for c in range(DC):
                    dve.tensor_copy(x4[:, c], bank[at + c][:, :]).then_inc(x4_done.sem, 1)

            def hidden_low(j, l):
                dve.wait_ge(gelu_done[l].sem, gelu_done[l].at(j, 2))
                dve.tensor_tensor(hid[A:P, l], wide[A:P, l], hid[A:P, l], ALU.subtract
                                  ).then_inc(hid_done[l].sem, 1)

            def expert_low(j, l):
                dve.wait_ge(exw_done[l].sem, exw_done[l].at(j, 2))
                dve.tensor_tensor(exo[A:P, l], wide[A:P, l], exo[A:P, l], ALU.subtract
                                  ).then_inc(exo_done[l].sem, 1)

            def add(ready, value, pbank, c, bias, resid, dst, done):
                dve.wait_ge(ready.sem, value)
                dve.scalar_tensor_tensor(dst[:, c], bank[pbank][:, :], bias[:, c:c + 1], resid[:, c],
                                         ALU.add, ALU.add).then_inc(done.sem, 1)

            def take_up(j, l, at=None):
                at = (4, 6)[l] if at is None else at
                for c in range(DC):
                    add(up_done[l], up_done[l].at(j, 1), at + c, c, k["up_b"][:, l], (x2, x4)[l], x3[:, l],
                        x3_done[l])

            def take_network(j, c):
                if c == 0:
                    dve.wait_ge(x1r_in.sem, x1r_in.at(j, 16))
                    dve.wait_ge(x3_done[0].sem, x3_done[0].at(j - 1, DC))
                add(w2_done, w2_done.at(j, c + 1), c, c, k["b2"], x1r, x2, x2_done)

            def tile(i, t):
                return bank[(6, 2, 4)[i] + t // 2][:, (t % 2) * D:(t % 2 + 1) * D]

            def statistics(j, i):
                dve.wait_ge(to_t[i].sem, to_t[i].at(j, 1))
                for t in range(QT):
                    last = dve.bn_stats(stats[:, i, t], tile(i, t))
                last.then_inc(bn_done[i].sem, 1)
                dve.wait_ge(bn_done[i].sem, bn_done[i].at(j, 1))
                apart(dve, dve_apart)
                for t in range(QT):
                    last = dve.bn_aggr(mv[:, i, t], stats[:, i, t])
                last.then_inc(stat_done[i].sem, 1)

            def normalise(j, i):
                dve.wait_ge(std_done[i].sem, std_done[i].at(j, 1))
                dve.reciprocal(rstd[:, i], std[:, i]).then_inc(rstd_done[i].sem, 1)
                dve.wait_ge(rstd_done[i].sem, rstd_done[i].at(j, 1))
                if i == 2:
                    dve.wait_ge(scaled.sem, scaled.at(j - 1, 1))
                for t in range(QT):
                    last = dve.tensor_scalar(xh[:, i, t], tile(i, t), mv[:, i, t, 0:1], rstd[:, i, t:t + 1],
                                             ALU.subtract, ALU.mult)
                last.then_inc(norm_done[i].sem, 1)

            def rotation_matrix(j):
                dve.wait_ge(rotated.sem, rotated.at(j - 1, 1))
                dve.tensor_scalar(rotc[:], k["ident"][:], k["rot"][:, 0, bass.ds(j, 1)], None, ALU.mult
                                  ).then_inc(rotc_done.sem, 1)
                dve.wait_ge(rotc_done.sem, rotc_done.at(j, 1))
                dve.scalar_tensor_tensor(rotm[:], k["beside"][:], k["rot"][:, 1, bass.ds(j, 1)], rotc[:],
                                         ALU.mult, ALU.add).then_inc(rotm_done.sem, 1)

            def iteration(j):
                if on(j, 2):
                    statistics(j - 2, 1)
                for n in range(2 * FC):
                    if n < FC and on(j, 0):
                        gelu_high(j, n)
                    if n == 0 and on(j, 3):
                        statistics(j - 3, 2)
                    if n == STATISTICS3_AT and on(j, -1):
                        statistics(j + 1, 0)
                    if n == 2 and on(j, 1):
                        low_part(j - 1, 0, x2, x2_done)
                    if n == 2 and on(j, 2):
                        rotation_matrix(j - 2)
                    for m, i in ((3, 1), (4, 2), (NORMALISE3_AT, 0)):
                        if n == m and on(j, NORM_LAG[i]):
                            normalise(j - NORM_LAG[i], i)
                    if n == ROTATE_AT and on(j, 2):
                        take_rotated(j - 2)
                        low_part(j - 2, 1, x4, x4_done)
                    for l in range(2):
                        if on(j, 1 + l):
                            if n == DOWN_AT:
                                hidden_low(j - (1 + l), l)
                            if n == EXPERT_AT:
                                expert_low(j - (1 + l), l)
                if on(j, 1):
                    take_up(j - 1, 0)
                if on(j, 0):
                    take_network(j, 0)
                if on(j, 2):
                    take_up(j - 2, 1)
                if on(j, 0):
                    take_network(j, 1)

            dve.memset(eps[:], EPS).then_inc(eps_set, 1)
            dve.wait_ge(k["late_in"], 16 * LATE_LOADS)
            dve.wait_ge(high_w, 2)
            for l in range(2):
                for r in range(2):
                    last = dve.tensor_tensor(dwl[:, l, :, r], k["down_w"][:, l], dwh[:, l, :, r], ALU.subtract)
            last.then_inc(low_w, 1)
            dve.tensor_tensor(uwl[:], k["up_w"][:], uwh[:], ALU.subtract).then_inc(low_w, 1)
            statistics(0, 0)
            normalise(0, 0)
            dve.wait_ge(w1_in, 16)
            dve.wait_ge(high_w, 3)
            dve.tensor_tensor(w1l[:], g_w1, w1h[:], ALU.subtract).then_inc(low_w, 1)
            dve.wait_ge(w2_in, 16)
            dve.wait_ge(high_w, 4)
            dve.tensor_tensor(w2l[:], g_w2, w2h[:], ALU.subtract).then_inc(low_w, 1)
            dve.wait_ge(experts_made, 1)
            for j in range(0, 3):
                iteration(j)
            with dve.Fori(3, B - 1) as j:
                iteration(j)
            iteration(B - 1)
            y, z = B - 2, B - 1
            statistics(y, 1)
            statistics(y - 1, 2)
            low_part(z, 0, x2, x2_done)
            normalise(y, 1)
            rotation_matrix(y)
            normalise(y - 1, 2)
            hidden_low(z, 0)
            take_rotated(y)
            expert_low(z, 0)
            low_part(y, 1, x4, x4_done)
            take_up(z, 0, at=0)
            hidden_low(y, 1)
            expert_low(y, 1)
            statistics(z, 1)
            normalise(z, 1)
            rotation_matrix(z)
            take_up(y, 1)
            statistics(y, 2)
            take_rotated(z, at=0)
            low_part(z, 1, x4, x4_done)
            normalise(y, 2)
            hidden_low(z, 1)
            expert_low(z, 1)
            take_up(z, 1)
            statistics(z, 2)
            normalise(z, 2)
            dve.wait_ge(norm_done[2].sem, norm_done[2].at(z, 1))
            dve.wait_ge(stored.sem, stored.at(y, 16))
            dve.tensor_tensor(res[:], xh[:, 2], k["gamma"][:, None, :].to_broadcast([P, QT, D]), ALU.mult
                              ).then_inc(scaled.sem, 1)
            dve.wait_ge(scaled.sem, scaled.at(z, 1))
            dve.tensor_tensor(res[:], res[:], k["beta"][:, None, :].to_broadcast([P, QT, D]), ALU.add
                              ).then_inc(out_made.sem, 1)

        @block.scalar
        def _(act):
            def gelu(j, f):
                act.wait_ge(w1_done.sem, w1_done.at(j, f + 1))
                if f >= NGT:
                    act.wait_ge(gl_done.sem, gl_done.at(j, f - NGT + 1))
                    act.wait_ge(gh_done.sem, gh_done.at(j, f - NGT + 1))
                else:
                    act.wait_ge(gl_done.sem, gl_done.at(j - 1, f + NGT + 1))
                act.activation(g[:, f % NGT], bank[f % 2][:, :], ACT.Gelu_apprx_sigmoid, bias=k["b1"][:, f:f + 1]
                               ).then_inc(g_done.sem, 1)

            def high_part(j, l):
                src, ready = ((x2, x2_done), (x4, x4_done))[l]
                for c in range(DC):
                    act.wait_ge(ready.sem, ready.at(j, c + 1))
                    act.copy(x24h[:, l, c], src[:, c]).then_inc(high_done[l].sem, 1)

            def hidden(j, l):
                act.wait_ge(down_done[l].sem, down_done[l].at(j, 1))
                for dst in (hid, wide):
                    act.activation(dst[:, l], bank[6 + l][:, :], ACT.Gelu, bias=k["down_b"][:, l:l + 1]
                                   ).then_inc(gelu_done[l].sem, 1)

            def expert_high(j, l):
                act.wait_ge(expert_done[l].sem, expert_done[l].at(j, 1))
                act.wait_ge(exo_done[l].sem, exo_done[l].at(j - 1, 1))
                for dst in (exo, wide):
                    act.activation(dst[:, l], bank[6 + l][:, :], ACT.Identity,
                                   bias=k["expert_b"][:, l, bass.ds(j, 1)]).then_inc(exw_done[l].sem, 1)

            def deviation(j, i):
                act.wait_ge(stat_done[i].sem, stat_done[i].at(j, 1))
                act.activation(std[:, i], mv[:, i, :, 1], ACT.Sqrt, bias=eps[:, 0:1]).then_inc(std_done[i].sem, 1)

            def network_input(j):
                act.wait_ge(to_f[0].sem, to_f[0].at(j, 1))
                act.wait_ge(rotated.sem, rotated.at(j - 3, 1))
                for dst, done in ((hh, hh_done), (feat, feat_done[0])):
                    for c in range(DC):
                        act.activation(dst[:, c], bank[2 + c][:, :], ACT.Identity, bias=k["beta2"][:, c:c + 1],
                                       scale=k["g2"][:, c:c + 1]).then_inc(done.sem, 1)

            def rotation_input(j):
                act.wait_ge(to_f[1].sem, to_f[1].at(j, 1))
                act.wait_ge(hl_done.sem, hl_done.at(j + 2, DC))
                for c in range(DC):
                    act.activation(feat[:, c], bank[2 + c][:, :], ACT.Identity, bias=k["beta_f"][:, c:c + 1],
                                   scale=k["gamma_f"][:, c:c + 1]).then_inc(feat_done[1].sem, 1)

            def iteration(j):
                for n in range(2 * FC):
                    if n < FC and on(j, 0):
                        gelu(j, n)
                    if n == 1 and on(j, 1):
                        high_part(j - 1, 0)
                    if n == 3:
                        for i in (1, 2):
                            if on(j, NORM_LAG[i]):
                                deviation(j - NORM_LAG[i], i)
                    if n == DEVIATION3_AT and on(j, -1):
                        deviation(j + 1, 0)
                    if n == TO_ROTATE_AT and on(j, 2):
                        rotation_input(j - 2)
                    if n == ROTATE_AT and on(j, 2):
                        high_part(j - 2, 1)
                    if n == INPUT_AT and on(j, -1):
                        network_input(j + 1)
                    for l in range(2):
                        if on(j, 1 + l):
                            if n == DOWN_AT:
                                hidden(j - (1 + l), l)
                            if n == EXPERT_AT:
                                expert_high(j - (1 + l), l)

            act.wait_ge(eps_set, 1)
            act.wait_ge(k["late_in"], 16 * LATE_LOADS)
            for l in range(2):
                for r in range(2):
                    last = act.copy(dwh[:, l, :, r], k["down_w"][:, l])
            last.then_inc(high_w, 1)
            act.copy(uwh[:], k["up_w"][:]).then_inc(high_w, 1)
            act.wait_ge(w1_in, 16)
            act.copy(w1h[:], g_w1).then_inc(high_w, 1)
            deviation(0, 0)
            network_input(0)
            act.wait_ge(w2_in, 16)
            act.copy(w2h[:], g_w2).then_inc(high_w, 1)
            act.wait_ge(low_w, 3)
            act.wait_ge(experts_made, 1)
            for j in range(0, 3):
                iteration(j)
            with act.Fori(3, B - 1) as j:
                iteration(j)
            iteration(B - 1)
            y, z = B - 2, B - 1
            high_part(z, 0)
            deviation(y, 1)
            deviation(y - 1, 2)
            hidden(z, 0)
            rotation_input(y)
            expert_high(z, 0)
            high_part(y, 1)
            hidden(y, 1)
            expert_high(y, 1)
            deviation(z, 1)
            rotation_input(z)
            deviation(y, 2)
            high_part(z, 1)
            hidden(z, 1)
            expert_high(z, 1)
            deviation(z, 2)

        @block.gpsimd
        def _(pool):
            def gelu_low(j, f):
                pool.wait_ge(gh_done.sem, gh_done.at(j, f + 1))
                if f == 0:
                    pool.wait_ge(w2_done.sem, w2_done.at(j - 1, DC))
                pool.tensor_tensor(gl[:, f], g[:, f % NGT], gh[:, f], ALU.subtract).then_inc(gl_done.sem, 1)

            def network_low(j):
                for c in range(DC):
                    pool.wait_ge(feat_done[0].sem, feat_done[0].at(j, c + 1))
                    pool.tensor_tensor(hl[:, c], feat[:, c], hh[:, c], ALU.subtract).then_inc(hl_done.sem, 1)

            def expert_parts(j, l):
                pool.wait_ge(expert_done[l].sem, expert_done[l].at(j - 1, 1))
                apart(pool, pool_apart)
                pool.tensor_copy(ew[:, l], k["expert_w"][:, l, bass.ds(j, 1), :].to_broadcast([P, 2, A])
                                 ).then_inc(ew_done[l].sem, 1)
                pool.wait_ge(ew_done[l].sem, ew_done[l].at(j, 1))
                apart(pool, pool_apart)
                pool.tensor_copy(ewh[:, l], ew[:, l]).then_inc(ew_done[l].sem, 1)
                pool.wait_ge(ew_done[l].sem, ew_done[l].at(j, 2))
                pool.tensor_tensor(ewl[:, l], ew[:, l], ewh[:, l], ALU.subtract).then_inc(ew_done[l].sem, 1)

            def output(j):
                pool.wait_ge(norm_done[2].sem, norm_done[2].at(j, 1))
                pool.wait_ge(stored.sem, stored.at(j - 1, 16))
                pool.tensor_tensor(res[:], xh[:, 2], k["gamma"][:, None, :].to_broadcast([P, QT, D]), ALU.mult
                                   ).then_inc(scaled.sem, 1)
                pool.wait_ge(scaled.sem, scaled.at(j, 1))
                pool.tensor_tensor(res[:], res[:], k["beta"][:, None, :].to_broadcast([P, QT, D]), ALU.add
                                   ).then_inc(out_made.sem, 1)

            def iteration(j):
                for n in range(2 * FC):
                    if n == 0:
                        for l in range(2):
                            if on(j, 1 + l):
                                expert_parts(j - (1 + l), l)
                    if n < FC and on(j, 0):
                        gelu_low(j, n)
                    if n == INPUT_AT and on(j, -1):
                        network_low(j + 1)
                    if n == 8 and on(j, 3):
                        output(j - 3)

            pool.wait_ge(k["chosen"], 16 * 12 * B)
            pool.wait_ge(k["late_in"], 16 * LATE_LOADS)
            domf = k["domf"]

            def link(n, ins):
                ins.then_inc(pool_link, 1)
                pool.wait_ge(pool_link, n)

            for n, rows in enumerate(HALVES):
                unit = k["ident"][rows, None, None, rows].to_broadcast([A, 2, B, A])
                link(n + 1, pool.tensor_tensor(wid[rows], unit,
                                               domf[rows, None, 3, :, None].to_broadcast([A, 2, B, A]), ALU.mult))
            link(3, pool.tensor_tensor(wsel[:], k["expert_w"][:], domf[:, None, 2, :, None].to_broadcast([P, 2, B, A]),
                                       ALU.mult))
            link(4, pool.tensor_tensor(k["expert_w"][:], wsel[:], wid[:], ALU.add))
            link(5, pool.tensor_tensor(bsel[:], k["expert_b"][:], domf[:, None, 2].to_broadcast([P, 2, B]), ALU.mult))
            pool.tensor_tensor(k["expert_b"][:], bsel[:], k["domain_emb"][:], ALU.add).then_inc(experts_made, 1)
            for j in range(-1, 3):
                iteration(j)
            with pool.Fori(3, B - 1) as j:
                iteration(j)
            iteration(B - 1)
            y, z = B - 2, B - 1
            expert_parts(z, 0)
            expert_parts(y, 1)
            output(y - 1)
            expert_parts(z, 1)
            output(y)


def build(nc, d):
    v = load_layouts(d)
    x1_dram = nc.dram_tensor("x1_dram", [B, P, DC, S], F32, kind="Internal").ap()
    pieces_dram = nc.dram_tensor("pieces_dram", [2, DC, 3, P, S], BF16, kind="Internal").ap()
    pieces_dram = pieces_dram.rearrange("q c i p t -> p q c i t")
    with ExitStack() as ctx:
        def sb(name, shape, dt=F32):
            return ctx.enter_context(nc.sbuf_tensor(name, shape, dt))

        k = dict(
            ident=sb("ident", [P, P]),
            big=sb("big", [P, NB, QT, S]),
            b1=sb("b1", [P, FC]), b2=sb("b2", [P, DC]), g2=sb("g2", [P, DC]), beta2=sb("beta2", [P, DC]),
            down_w=sb("down_w", [P, 2, DC, A]), down_b=sb("down_b", [P, 2]),
            up_w=sb("up_w", [P, 2, D]), up_b=sb("up_b", [P, 2, DC]),
            gamma=sb("gamma", [P, D]), beta=sb("beta", [P, D]),
            gamma_f=sb("gamma_f", [P, DC]), beta_f=sb("beta_f", [P, DC]),
            beside=sb("beside", [P, P]),
            expert_w=sb("expert_w", [P, 2, B, A]), expert_b=sb("expert_b", [P, 2, B]),
            domain_emb=sb("domain_emb", [P, 2, B]), domf=sb("domf", [P, 4, B]), domi=sb("domi", [P, B], I32),
            late_in=ctx.enter_context(nc.semaphore("late_in")), w1_in=ctx.enter_context(nc.semaphore("w1_in")),
            w2_in=ctx.enter_context(nc.semaphore("w2_in")), x1t_in=ctx.enter_context(nc.semaphore("x1t_in")),
            chosen=ctx.enter_context(nc.semaphore("chosen")),
            ada=sb("ada", [P, 4, B]), trig=sb("trig", [P, 6, B]), rot=sb("rot", [P, 2, B]),
        )
        attention_block(nc, d, v, k, x1_dram, pieces_dram)
        network_block(nc, d, v, k, x1_dram)


def kernel(**inputs):
    import concourse.bacc as bacc
    from concourse.bass_utils import run_bass_kernel_spmd

    nc = bacc.Bacc("TRN2", target_bir_lowering=False, num_devices=1)
    arrays = {}
    for name in INPUTS:
        a = np.asarray(inputs[name])
        if name.endswith("down_W") or name.endswith("up_W"):
            a = a.T
        elif name.endswith("expert_W"):
            a = a.transpose(0, 2, 1)
        elif name.endswith("up_b") or name.startswith("L1_cond_ln") or name in ["L0_cond_" + w for w in BY_FEATURE]:
            a = a.reshape(-1, P).T
        arrays[name] = np.ascontiguousarray(a)
    arrays["ident"] = np.eye(P, dtype=np.float32)
    place = np.arange(P) % 4
    arrays["pairs"] = np.stack([place < 2, place >= 2], 1).astype(np.float32)
    beside = np.zeros((P, P), np.float32)
    beside[np.arange(1, P, 2), np.arange(0, P, 2)] = 1.0
    beside[np.arange(0, P, 2), np.arange(1, P, 2)] = -1.0
    arrays["beside"] = beside
    half = D // 2
    freq = np.exp(np.arange(half, dtype=np.float32) * np.float32(-np.log(10000.0) / (half - 1)))
    arrays["freq"] = freq.astype(np.float32).reshape(P, 1)
    d = {name: nc.dram_tensor("in_" + name, a.shape, mybir.dt.from_np(a.dtype), kind="ExternalInput").ap()
         for name, a in arrays.items()}
    d["out"] = nc.dram_tensor("out", (B, S, D), F32, kind="ExternalOutput").ap()
    build(nc, d)
    r = run_bass_kernel_spmd(nc, [{"in_" + n: a for n, a in arrays.items()}], core_ids=[0])
    return r.results[0]["out"]
```
